# Optimizing a Trainium2 kernel written in Bass

```python
import numpy as np
import jax
import jax.numpy as jnp

def _softmax(x, axis=-1):
    return jax.nn.softmax(x, axis=axis)

def _gelu(x):
    return jax.nn.gelu(x, approximate=True)

def _silu(x):
    return jax.nn.silu(x)

def _sigmoid(x):
    return jax.nn.sigmoid(x)

def _layernorm(x, axis=-1, eps=1e-05):
    m = jnp.mean(x, axis=axis, keepdims=True)
    v = jnp.var(x, axis=axis, keepdims=True)
    return (x - m) / jnp.sqrt(v + eps)

def _scatter_add(tgt, idx, src, axis=0):
    return tgt.at[idx].add(src)

def _segment_sum(src, seg, n):
    return jax.ops.segment_sum(src, seg, n)
kernel_name = 'mk_adaln_d1_jaxref_r4_c7d84d'

def setup_inputs(seed: int=0):
    np.random.seed(seed)
    _w = jnp.asarray

    def _L0_attn_setup():
        import jax, jax.numpy as jnp
        import numpy as np
        B, N, DIM, H = (8, 1024, 256, 16)
        D = DIM // H
        EPS_NORM = 1e-12
        EPS_PI = 1e-08
        key = jax.random.key(seed)
        k1, k2, k3 = jax.random.split(key, 3)
        x = jax.random.normal(k1, (B, N, DIM), dtype=jnp.float32)
        Wqkv = jax.random.normal(k2, (DIM, DIM), dtype=jnp.float32) * (1.0 / np.sqrt(DIM))
        temp = jnp.ones((H, 1), dtype=jnp.float32)
        Wout = jax.random.normal(k3, (DIM, DIM), dtype=jnp.float32) * (1.0 / np.sqrt(DIM))
        bout = jnp.zeros((DIM,), dtype=jnp.float32)
        return {'x': x, 'Wqkv': Wqkv, 'temp': temp, 'Wout': Wout, 'bout': bout}
    _L0_attn_in = _L0_attn_setup()

    def _L0_ffn_setup():
        import jax, jax.numpy as jnp
        import numpy as np
        D_MODEL = 256
        NUM_HEADS = 4
        NUM_EXPERTS = 8
        TOP_K = 2
        D_FF = 256
        EPS = 1e-06

        def _rmsnorm(x, g):
            return x * jax.lax.rsqrt(jnp.mean(x * x, axis=-1, keepdims=True) + EPS) * g

        def _swiglu(x, w1, w2, w3):
            return jax.nn.silu(x @ w1.T) * (x @ w3.T) @ w2.T
        key = jax.random.key(seed)
        ks = jax.random.split(key, 16)
        d, e, f = (D_MODEL, NUM_EXPERTS, D_FF)
        dc = d // 4
        s = 0.02
        return {'X': jax.random.normal(ks[0], (2, 256, d), dtype=jnp.float32), 'g1': jnp.ones((d,), jnp.float32), 'g2': jnp.ones((d,), jnp.float32), 'Wq': jax.random.normal(ks[1], (d, d), jnp.float32) * s, 'Wkc': jax.random.normal(ks[2], (dc, d), jnp.float32) * s, 'Wvc': jax.random.normal(ks[3], (dc, d), jnp.float32) * s, 'Wo': jax.random.normal(ks[4], (d, d), jnp.float32) * s, 'Wr': jax.random.normal(ks[5], (e, d), jnp.float32) * s, 'expert_bias': jnp.zeros((e,), jnp.float32), 'sW1': jax.random.normal(ks[6], (f, d), jnp.float32) * s, 'sW2': jax.random.normal(ks[7], (d, f), jnp.float32) * s, 'sW3': jax.random.normal(ks[8], (f, d), jnp.float32) * s, 'eW1': jax.random.normal(ks[9], (e, f, d), jnp.float32) * s, 'eW2': jax.random.normal(ks[10], (e, d, f), jnp.float32) * s, 'eW3': jax.random.normal(ks[11], (e, f, d), jnp.float32) * s}
    _L0_ffn_in = _L0_ffn_setup()
    _L0_c = _w((lambda *s: np.random.randn(*s).astype(np.float32) * 0.05)(2, 256))
    _L0_wmod = _w((lambda *s: np.random.randn(*s).astype(np.float32) * 0.05)(256, 6 * 256) * 256 ** (-0.5))
    _d = {'L0_attn_x': _L0_attn_in['x'], 'L0_attn_Wqkv': _L0_attn_in['Wqkv'], 'L0_attn_temp': _L0_attn_in['temp'], 'L0_attn_Wout': _L0_attn_in['Wout'], 'L0_attn_bout': _L0_attn_in['bout'], 'L0_ffn_g1': _L0_ffn_in['g1'], 'L0_ffn_g2': _L0_ffn_in['g2'], 'L0_ffn_Wq': _L0_ffn_in['Wq'], 'L0_ffn_Wkc': _L0_ffn_in['Wkc'], 'L0_ffn_Wvc': _L0_ffn_in['Wvc'], 'L0_ffn_Wo': _L0_ffn_in['Wo'], 'L0_ffn_Wr': _L0_ffn_in['Wr'], 'L0_ffn_expert_bias': _L0_ffn_in['expert_bias'], 'L0_ffn_sW1': _L0_ffn_in['sW1'], 'L0_ffn_sW2': _L0_ffn_in['sW2'], 'L0_ffn_sW3': _L0_ffn_in['sW3'], 'L0_ffn_eW1': _L0_ffn_in['eW1'], 'L0_ffn_eW2': _L0_ffn_in['eW2'], 'L0_ffn_eW3': _L0_ffn_in['eW3'], 'L0_c': _L0_c, 'L0_wmod': _L0_wmod}
    _x0 = _d['L0_attn_x']
    _d['L0_attn_x'] = jax.random.normal(jax.random.fold_in(jax.random.key(seed), 1), (2, 2048, 256), dtype=_x0.dtype)
    del _x0
    return _d

def reference(L0_attn_x, L0_attn_Wqkv, L0_attn_temp, L0_attn_Wout, L0_attn_bout, L0_ffn_g1, L0_ffn_g2, L0_ffn_Wq, L0_ffn_Wkc, L0_ffn_Wvc, L0_ffn_Wo, L0_ffn_Wr, L0_ffn_expert_bias, L0_ffn_sW1, L0_ffn_sW2, L0_ffn_sW3, L0_ffn_eW1, L0_ffn_eW2, L0_ffn_eW3, L0_c, L0_wmod):

    def _L0_attn_ref(x, Wqkv, temp, Wout, bout):
        import jax, jax.numpy as jnp
        import numpy as np
        B, N, DIM, H = (8, 1024, 256, 16)
        D = DIM // H
        EPS_NORM = 1e-12
        EPS_PI = 1e-08
        b, n, dim = x.shape
        h, d = (H, dim // H)
        w = (x @ Wqkv.T).reshape(b, n, h, d).transpose(0, 2, 1, 3)
        norm = jnp.sqrt(jnp.sum(w * w, axis=-2, keepdims=True))
        w_normed = w / jnp.maximum(norm, EPS_NORM)
        logits = jnp.sum(w_normed * w_normed, axis=-1) * temp[None, :, :]
        Pi = jax.nn.softmax(logits, axis=1)
        Pi_norm = Pi / (jnp.sum(Pi, axis=-1, keepdims=True) + EPS_PI)
        dots = jnp.einsum('bhn,bhnd->bhd', Pi_norm, w * w)
        attn = 1.0 / (1.0 + dots)
        out = -(w * Pi[..., None]) * attn[:, :, None, :]
        out = out.transpose(0, 2, 1, 3).reshape(b, n, dim)
        return out @ Wout.T + bout

    def _L0_ffn_ref(X, g1, g2, Wq, Wkc, Wvc, Wo, Wr, expert_bias, sW1, sW2, sW3, eW1, eW2, eW3):
        import jax, jax.numpy as jnp
        import numpy as np
        D_MODEL = 256
        NUM_HEADS = 4
        NUM_EXPERTS = 8
        TOP_K = 2
        D_FF = 256
        EPS = 1e-06

        def _rmsnorm(x, g):
            return x * jax.lax.rsqrt(jnp.mean(x * x, axis=-1, keepdims=True) + EPS) * g

        def _swiglu(x, w1, w2, w3):
            return jax.nn.silu(x @ w1.T) * (x @ w3.T) @ w2.T
        B, S, d = X.shape
        H = NUM_HEADS
        dk = d // H
        scale = 1.0 / jnp.sqrt(jnp.float32(dk))
        nx = _rmsnorm(X, g1)
        Q = (nx @ Wq.T).reshape(B, S, H, dk).transpose(0, 2, 1, 3)
        Kc = nx @ Wkc.T
        Vc = nx @ Wvc.T
        scores = jnp.einsum('bhsd,btd->bhst', Q, Kc) * scale
        attn = jax.nn.softmax(scores, axis=-1)
        out = jnp.einsum('bhst,btd->bhsd', attn, Vc)
        out = out.transpose(0, 2, 1, 3).reshape(B, S, d) @ Wo.T
        X = X + out
        nx = _rmsnorm(X, g2)
        xf = nx.reshape(-1, d)
        logits = xf @ Wr.T + expert_bias
        rw = jax.nn.softmax(logits, axis=-1)
        topw, topi = jax.lax.top_k(rw, TOP_K)
        topw = jax.nn.softmax(topw, axis=-1)
        combine = jnp.sum(jax.nn.one_hot(topi, NUM_EXPERTS, dtype=xf.dtype) * topw[..., None], axis=1)
        shared = _swiglu(xf, sW1, sW2, sW3)
        h = jax.nn.silu(jnp.einsum('td,efd->etf', xf, eW1)) * jnp.einsum('td,efd->etf', xf, eW3)
        eo = jnp.einsum('etf,edf->etd', h, eW2)
        specialist = jnp.einsum('te,etd->td', combine, eo)
        moe_out = (shared + specialist).reshape(B, S, d)
        return X + moe_out
    x = L0_attn_x
    mod = (_silu(L0_c) @ L0_wmod).reshape(L0_c.shape[0], 6, 1, -1)
    sa, ca, ga, sb, cb, gb = (mod[:, 0], mod[:, 1], mod[:, 2], mod[:, 3], mod[:, 4], mod[:, 5])
    ga = (2 * (ga >= 0) - 1) * jnp.maximum(jnp.abs(ga), 0.25)
    gb = (2 * (gb >= 0) - 1) * jnp.maximum(jnp.abs(gb), 0.25)
    h = _layernorm(x, axis=-1) * (1 + ca) + sa
    x = x + ga * _L0_attn_ref(h, L0_attn_Wqkv, L0_attn_temp, L0_attn_Wout, L0_attn_bout)
    h = _layernorm(x, axis=-1) * (1 + cb) + sb
    x = x + gb * _L0_ffn_ref(h, L0_ffn_g1, L0_ffn_g2, L0_ffn_Wq, L0_ffn_Wkc, L0_ffn_Wvc, L0_ffn_Wo, L0_ffn_Wr, L0_ffn_expert_bias, L0_ffn_sW1, L0_ffn_sW2, L0_ffn_sW3, L0_ffn_eW1, L0_ffn_eW2, L0_ffn_eW3)
    return x

_drawn_inputs = setup_inputs


def setup_inputs(seed=0):
    import zlib

    import numpy as np

    out = dict(_drawn_inputs(seed))
    spreads = {'L0_attn_temp': (1.0, 0.6),
     'L0_attn_bout': (0.0, 0.336),
     'L0_ffn_g1': (1.0, 0.6),
     'L0_ffn_g2': (1.0, 0.6),
     'L0_ffn_expert_bias': (0.0, 0.8)}
    factors = {'L0_attn_Wqkv': 7.294,
     'L0_attn_Wout': 7.201,
     'L0_ffn_Wq': 8.0,
     'L0_ffn_Wkc': 8.0,
     'L0_ffn_Wvc': 8.0,
     'L0_ffn_Wo': 8.0,
     'L0_ffn_Wr': 8.0,
     'L0_ffn_sW1': 8.0,
     'L0_ffn_sW2': 8.0,
     'L0_ffn_sW3': 8.0,
     'L0_ffn_eW1': 8.0,
     'L0_ffn_eW2': 8.0,
     'L0_ffn_eW3': 8.0}
    for name, (base, spread) in spreads.items():
        noise = np.random.default_rng([zlib.crc32(name.encode()), seed]).standard_normal(out[name].shape)
        drawn = base * np.exp(spread * noise) if base else spread * noise
        out[name] = jnp.asarray(drawn.astype(out[name].dtype))
    for name, factor in factors.items():
        out[name] = (out[name] * factor).astype(out[name].dtype)
    return out
```

```python
from contextlib import ExitStack

import concourse.bass as bass
from concourse import mybir

ALU = mybir.AluOpType
ACT = mybir.ActivationFunctionType
F32 = mybir.dt.float32
F32R = mybir.dt.float32r
AX = mybir.AxisListType.X

P = 128
D = 256
NB = 2
NT = 16
S = 2048
NE = 8
EPS_LN = 1e-5
EPS_RMS = 1e-6


class Prog:

    def __init__(self, nc, ctx):
        self.nc, self.ctx = nc, ctx
        self.q = {k: [] for k in ("pe", "act", "dve", "pool", "sp")}
        self.sem = {k: ctx.enter_context(nc.semaphore("s_" + k)) for k in ("pe", "act", "dve", "pool")}
        self.n = {k: 0 for k in self.sem}
        self.dsem = 0

    def put(self, k, fn, waits):
        self.n[k] += 1
        self.q[k].append((flat(waits), fn, self.sem[k], 1))
        return (self.sem[k], self.n[k])

    def T(self, fn, *w):
        return self.put("pe", fn, w)

    def A(self, fn, *w):
        return self.put("act", fn, w)

    def V(self, fn, *w):
        return self.put("dve", fn, w)

    def G(self, fn, *w):
        return self.put("pool", fn, w)

    def dma(self, k, out, in_, *w):
        self.dsem += 1
        sem = self.ctx.enter_context(self.nc.semaphore(f"d{self.dsem}"))
        self.q[k].append((flat(w), lambda e: e.dma_start(out, in_), sem, 16))
        return (sem, 16)

    def wait(self, k, *w):
        self.q[k].append((flat(w), None, None, 0))

    def play(self, k, eng):
        seen = {}
        for waits, fn, sem, inc in self.q[k]:
            for s, v in waits:
                if seen.get(s.num, 0) < v:
                    eng.wait_ge(s, v)
                    seen[s.num] = v
            if fn is not None:
                fn(eng).then_inc(sem, inc)


def flat(x):
    out = []
    for y in x:
        if y is None:
            continue
        if isinstance(y, list):
            out += flat(y)
        else:
            out.append(y)
    return out


def bc(ap, n, axis):
    return ap.unsqueeze(axis).to_broadcast(list(ap.shape[:axis]) + [n] + list(ap.shape[axis:]))


def build(nc, I, out):
    with ExitStack() as ctx:
        _build(nc, ctx, I, out)


def _build(nc, ctx, I, out):
    pr = Prog(nc, ctx)
    T, A, V, G, dma = pr.T, pr.A, pr.V, pr.G, pr.dma

    def sb(name, shape, dt=F32, c=None):
        return (c or ctx).enter_context(nc.sbuf_tensor(name, shape, dt))

    PS = ctx.enter_context(nc.psum_tensor("PS", [P, 8, 512], F32))
    rel = {i: [] for i in range(8)}

    class Ring:
        def __init__(self, banks):
            self.banks, self.i = banks, 0

        def take(self):
            b = self.banks[self.i % len(self.banks)]
            self.i += 1
            return b

    ident = sb("ident", [P, P])
    X2 = sb("X2", [P, NB * NT, D])
    gb = sb("gb", [P, NB, D])
    g1c = sb("g1c", [P, 2])
    g2c = sb("g2c", [P, 2])
    eps = sb("eps", [P, 2])
    ssq2 = sb("ssq2", [P, NB * NT])
    rs2 = sb("rs2", [P, NB * NT])
    x1d = nc.dram_tensor("x1_scratch", [NB, S, D], F32, kind="Internal").ap()

    t_id = dma("sp", ident[:, :], I["ident"])
    t_g1 = dma("act", g1c[:, :], I["g1"])
    t_g2 = dma("act", g2c[:, :], I["g2"])
    t_e0 = V(lambda e: e.memset(eps[:, 0:1], EPS_LN))
    t_eps = V(lambda e: e.memset(eps[:, 1:2], EPS_RMS))

    def tokens(ap, b):
        return ap[b].rearrange("(p t) d -> p t d", t=NT)

    c1 = ExitStack()
    cX = ExitStack()
    x = sb("x", [P, NB * NT, D], c=cX)
    rows = sb("rows", [P, NB, 4, D], c=cX)
    st = sb("st", [P, 4, 6], c=cX)
    mv = sb("mv", [P, NB * NT, 2], c=cX)
    sd = sb("sd", [P, NB * NT], c=cX)
    rs = sb("rs", [P, NB * NT], c=cX)
    xn = sb("xn", [P, 2, 4, D], c=cX)

    cT = sb("cT", [P, 2, NB], c=c1)
    sil = sb("sil", [P, 2, NB], c=c1)
    silB = sb("silB", [P, 2, NB, P], c=c1)
    sc = sb("sc", [P, 2, NB], c=c1)
    modc = sb("modc", [P, 2, 2, NB], c=c1)
    gab = sb("gab", [P, NB, D], c=c1)
    boutB = sb("boutB", [P, D], c=c1)
    gtmp = sb("gtmp", [P, 2, D], c=c1)
    wqkv = sb("wqkv", [P, 2, D], c=c1)
    wout = sb("wout", [P, 2, D], c=c1)
    wouts = sb("wouts", [P, 2, NB, D], c=c1)
    mask = sb("mask", [P, 2, 16], c=c1)
    tempB = sb("tempB", [P, 16], c=c1)
    LB = sb("LB", [P, 2, NB, 16], c=c1)
    ssq = sb("ssq", [P, 2, NB, 4], c=c1)
    n2 = sb("n2", [P, 2, NB], c=c1)
    piS = sb("piS", [P, 2, NB, 4], c=c1)
    dS = sb("dS", [P, 2, NB, 4], c=c1)
    cf = sb("cf", [P, 2, NB, 3], c=c1)
    lg = sb("lg", [P, NT, 16], c=c1)
    le = sb("le", [P, NT, 16], c=c1)
    lm = sb("lm", [P, NB, NT, 3], c=c1)
    piE = sb("piE", [P, 4, D], c=c1)
    hT = sb("hT", [P, 2, 512], c=c1)
    wT = sb("wT", [P, 2, NB * S], c=c1)
    w2T = sb("w2T", [P, 2, NB * S], c=c1)
    piT = sb("piT", [P, 2, 512], c=c1)
    junk = sb("junk", [P, 512], c=c1)

    cm = ExitStack()
    wmod = sb("wmod", [P, 2, 6 * D], c=cm)

    t_c = dma("sp", cT[:, :, :], I["cT"].rearrange("(c p) b -> p c b", p=P))
    t_wm = dma("sp", wmod[:, :, :], I["wmod"].rearrange("(c p) n -> p c n", p=P))
    t_x = []
    for b in range(NB):
        for g in range(4):
            t_x.append(dma("sp", x[:, b * NT + 4 * g:b * NT + 4 * g + 4, :], tokens(I["x"], b)[:, 4 * g:4 * g + 4, :]))
    t_wq = dma("act", wqkv[:, :, :], I["wqkvT"].rearrange("(c p) n -> p c n", p=P))
    t_mk = dma("act", mask[:, :, :], I["mask"].rearrange("(c p) n -> p c n", p=P))
    t_tp = dma("act", tempB[:, :], I["temp"].rearrange("h o -> o h").to_broadcast([P, 16]))
    t_wo = dma("act", wout[:, :, :], I["woutT"].rearrange("(c p) n -> p c n", p=P))
    t_bo = dma("act", boutB[:, :], I["bout"].unsqueeze(0).to_broadcast([P, D]))

    t = A(lambda e: e.activation(sc[:, :, :], cT[:, :, :], ACT.Exp, scale=-1.0), t_c)
    t = V(lambda e: e.tensor_scalar_add(sc[:, :, :], sc[:, :, :], 1.0), t)
    t = V(lambda e: e.reciprocal(sc[:, :, :], sc[:, :, :]), t)
    t_sil = V(lambda e: e.tensor_tensor(sil[:, :, :], sc[:, :, :], cT[:, :, :], ALU.mult), t)
    t_silB = V(lambda e: e.tensor_copy(silB[:, :, :, :], bc(sil[:, :, :], P, 3)), t_sil)

    def mod_cols(e):
        for i in range(2):
            for j in range(2):
                for k in range(2):
                    mm = e.matmul(PS[:, 0, (i * 2 + j) * 2:(i * 2 + j) * 2 + 2],
                                  wmod[:, k, i * D + j * P:i * D + j * P + P], sil[:, k, :],
                                  start=(k == 0), stop=(k == 1))
        return mm
    t = T(mod_cols, t_wm, t_sil)
    pm = PS[:, 0, 0:8].rearrange("p (i j b) -> p i j b", i=2, j=2)
    V(lambda e: e.tensor_copy(modc[:, 0, :, :], pm[:, 0, :, :]), t)
    t_modc = V(lambda e: e.tensor_scalar_add(modc[:, 1, :, :], pm[:, 1, :, :], 1.0), t)
    rel[0] = [t_modc]

    t_rows = []
    for b in range(NB):
        def mod_rows(e, b=b):
            for n in range(2):
                for k in range(2):
                    mm = e.matmul(PS[:, 2 + 2 * b + n, :], silB[:, k, b, :],
                                  wmod[:, k, 2 * D + n * 512:2 * D + n * 512 + 512], start=(k == 0), stop=(k == 1))
            return mm
        t_mr = T(mod_rows, t_wm, t_silB)
        pg = PS[:, 2 + 2 * b:4 + 2 * b, :].rearrange("p a (c d) -> p (a c) d", c=2)
        for i, dst in ((0, rows[:, b, 0, :]), (3, gb[:, b, :])):
            t1 = V(lambda e, i=i, pg=pg: e.tensor_scalar(gtmp[:, 0, :], pg[:, i, :], 0.0, 2.0, ALU.is_ge, ALU.mult), t_mr,
                   t_rows[-1:])
            t2 = V(lambda e, i=i, pg=pg: e.tensor_scalar(gtmp[:, 1, :], pg[:, i, :], -1.0, None, ALU.mult), t_mr, t_rows[-1:])
            t2 = V(lambda e, i=i, pg=pg: e.scalar_tensor_tensor(gtmp[:, 1, :], pg[:, i, :], 0.25, gtmp[:, 1, :],
                                                                ALU.max, ALU.max), t2)
            t_rows.append(V(lambda e, dst=dst: e.scalar_tensor_tensor(dst, gtmp[:, 0, :], -1.0, gtmp[:, 1, :],
                                                                      ALU.add, ALU.mult), t1, t2))
        V(lambda e, b=b, pg=pg: e.tensor_copy(rows[:, b, 1, :], pg[:, 1, :]), t_mr)
        t_r = V(lambda e, b=b, pg=pg: e.tensor_scalar_add(rows[:, b, 2, :], pg[:, 2, :], 1.0), t_mr)
        t_rows.append(t_r)
        rel[2 + 2 * b] = [t_r]
        rel[3 + 2 * b] = [t_r]
        t_gab = V(lambda e, b=b: e.tensor_tensor(gab[:, b, :], rows[:, b, 0, :], boutB[:, :], ALU.mult), t_rows, t_bo)
    cm.close()

    ring = Ring([0, 1, 2, 3, 4, 5, 6, 7])

    def layernorm(g, src, tsrc, twrite):
        ts = slice(4 * g, 4 * g + 4)
        for i in range(4):
            ta = V(lambda e, i=i: e.bn_stats(st[:, i, :], src[:, 4 * g + i, :]), tsrc, ln_done[-1:])
        for i in range(4):
            tb = V(lambda e, i=i: e.bn_aggr(mv[:, 4 * g + i, :], st[:, i, :]), ta)
        ln_done.append(tb)
        tc = A(lambda e: e.activation(sd[:, ts], mv[:, ts, 1], ACT.Sqrt, bias=eps[:, 0:1]), tb, t_eps)
        td = V(lambda e: e.reciprocal(rs[:, ts], sd[:, ts]), tc)
        for i in range(4):
            n = 4 * g + i
            t = V(lambda e, i=i, n=n: e.tensor_scalar(xn[:, g % 2, i, :], src[:, n, :], mv[:, n, 0:1], rs[:, n:n + 1],
                                                      ALU.subtract, ALU.mult), td, twrite)
        return t

    ln_done = []
    xn_free = [None, None]
    hT_free = [None, None]
    t_w = {}
    for g in range(8):
        b = g // 4
        t_xn = layernorm(g, x, t_x[g], xn_free[g % 2])
        t_h = []
        for dc in range(2):
            k = ring.take()

            def tr(e, dc=dc, k=k, g=g):
                for i in range(4):
                    mm = e.transpose(PS[:, k, i * P:i * P + P], xn[:, g % 2, i, dc * P:dc * P + P], ident[:, :])
                return mm
            t = T(tr, t_xn, t_id, rel[k])
            t = A(lambda e, dc=dc, k=k, b=b: e.activation(hT[:, dc, :], PS[:, k, :], ACT.Identity,
                                                          bias=modc[:, 0, dc, b:b + 1], scale=modc[:, 1, dc, b:b + 1]),
                  t, t_modc, hT_free[dc])
            rel[k] = [t]
            t_h.append(t)
        xn_free[g % 2] = t_h[1]
        cols = slice(g * 512, g * 512 + 512)
        for oc in range(2):
            k = ring.take()

            def proj(e, oc=oc, k=k):
                for dc in range(2):
                    mm = e.matmul(PS[:, k, :], wqkv[:, dc, oc * P:oc * P + P], hT[:, dc, :], start=(dc == 0), stop=(dc == 1))
                return mm
            tm = T(proj, t_h, t_wq, rel[k])
            ta = A(lambda e, oc=oc, k=k, b=b, g=g, cols=cols: e.activation(
                w2T[:, oc, cols], PS[:, k, :], ACT.Square, accum_out=ssq[:, oc, b, g % 4:g % 4 + 1]), tm)
            tv = V(lambda e, oc=oc, k=k, cols=cols: e.tensor_copy(wT[:, oc, cols], PS[:, k, :]), ta)
            rel[k] = [tv]
        hT_free = [tm, tm]
        t_w[b] = tv

    t_xp = {}
    for b in range(NB):
        t_xp[b] = G(lambda e, b=b: e.tensor_tensor(x[:, b * NT:b * NT + NT, :], x[:, b * NT:b * NT + NT, :],
                                                   bc(gab[:, b, :], NT, 1), ALU.add), t_gab, t_w[b], t_x, t_xp.get(b - 1))

    t_mt = V(lambda e: e.tensor_tensor(mask[:, :, :], mask[:, :, :], bc(tempB[:, :], 2, 1), ALU.mult), t_mk, t_tp)
    t_piT = [None, None]
    t_piE = t_junk = None
    lg_free = le_free = None
    t_x1 = []
    for b in range(NB):
        t = V(lambda e, b=b: e.tensor_reduce(n2[:, :, b], ssq[:, :, b, :], AX, ALU.add), t_w[b])
        t = V(lambda e, b=b: e.tensor_scalar(n2[:, :, b], n2[:, :, b], 1e-24, None, ALU.max), t)
        t = V(lambda e, b=b: e.reciprocal(n2[:, :, b], n2[:, :, b]), t)
        for oc in range(2):
            t_lb = V(lambda e, b=b, oc=oc: e.tensor_scalar(LB[:, oc, b, :], mask[:, oc, :], n2[:, oc, b:b + 1], None,
                                                           ALU.mult), t, t_mt)
        k = ring.take()
        pl = PS[:, k, 0:256].rearrange("p (t h) -> p t h", h=16)

        def logits(e, b=b, pl=pl):
            for i in range(NT):
                for oc in range(2):
                    mm = e.matmul(pl[:, i, :], w2T[:, oc, b * S + i * P:b * S + i * P + P], LB[:, oc, b, :],
                                  start=(oc == 0), stop=(oc == 1))
            return mm
        tl = T(logits, t_lb, rel[k])
        t = V(lambda e, b=b, pl=pl: e.tensor_reduce(lm[:, b, :, 0], pl, AX, ALU.max), tl)
        t = V(lambda e, b=b, pl=pl: e.tensor_tensor(lg[:, :, :], pl, bc(lm[:, b, :, 0], 16, 2), ALU.subtract), t, lg_free)
        rel[k] = [t]
        t = A(lambda e: e.activation(le[:, :, :], lg[:, :, :], ACT.Exp), t, le_free)
        lg_free = t
        ts = V(lambda e, b=b: e.tensor_reduce(lm[:, b, :, 1], le[:, :, :], AX, ALU.add), t)
        ts = V(lambda e, b=b: e.reciprocal(lm[:, b, :, 2], lm[:, b, :, 1]), ts)
        t_pi = V(lambda e, b=b: e.tensor_tensor(le[:, :, :], le[:, :, :], bc(lm[:, b, :, 2], 16, 2), ALU.mult), ts)
        t_d = []
        for g in range(4):
            cols = slice(b * S + g * 512, b * S + g * 512 + 512)
            t_pe = A(lambda e, g=g: e.activation(
                piE[:, :, :].rearrange("p t (h d) -> p (t h) d", d=16),
                bc(le[:, 4 * g:4 * g + 4, :].rearrange("p t h -> p (t h)"), 16, 2), ACT.Copy), t_pi, t_piE)
            for oc in range(2):
                k = ring.take()

                def tr(e, oc=oc, k=k):
                    for i in range(4):
                        mm = e.transpose(PS[:, k, i * P:i * P + P], piE[:, i, oc * P:oc * P + P], ident[:, :])
                    return mm
                t = T(tr, t_pe, rel[k])
                t_piE = t
                t = A(lambda e, oc=oc, k=k, b=b, g=g: e.activation(piT[:, oc, :], PS[:, k, :], ACT.Copy,
                                                                   accum_out=piS[:, oc, b, g:g + 1]), t, t_piT[oc])
                rel[k] = [t]
                t1 = V(lambda e, oc=oc, b=b, g=g, cols=cols: e.tensor_tensor_reduce(
                    out=junk[:, :], in0=piT[:, oc, :], in1=w2T[:, oc, cols], scale=1.0, scalar=0.0,
                    op0=ALU.mult, op1=ALU.add, accum_out=dS[:, oc, b, g:g + 1]), t, t_junk)
                t_junk = t1
                t_piT[oc] = V(lambda e, oc=oc, cols=cols: e.tensor_tensor(wT[:, oc, cols], wT[:, oc, cols], piT[:, oc, :],
                                                                          ALU.mult), t, t_w[b])
                t_d += [t, t1, t_piT[oc]]
        le_free = t_pe
        t1 = V(lambda e, b=b: e.tensor_reduce(cf[:, :, b, 0], piS[:, :, b, :], AX, ALU.add), t_d)
        t2 = V(lambda e, b=b: e.tensor_reduce(cf[:, :, b, 1], dS[:, :, b, :], AX, ALU.add), t_d)
        t = V(lambda e, b=b: e.tensor_scalar_add(cf[:, :, b, 0], cf[:, :, b, 0], 1e-8), t1)
        t = V(lambda e, b=b: e.reciprocal(cf[:, :, b, 0], cf[:, :, b, 0]), t)
        t = V(lambda e, b=b: e.tensor_tensor(cf[:, :, b, 1], cf[:, :, b, 1], cf[:, :, b, 0], ALU.mult), t, t2)
        t = V(lambda e, b=b: e.tensor_scalar_add(cf[:, :, b, 1], cf[:, :, b, 1], 1.0), t)
        t = V(lambda e, b=b: e.reciprocal(cf[:, :, b, 2], cf[:, :, b, 1]), t)
        for oc in range(2):
            t_ws = V(lambda e, b=b, oc=oc: e.tensor_scalar(wouts[:, oc, b, :], wout[:, oc, :], cf[:, oc, b, 2:3], -1.0,
                                                           ALU.mult, ALU.mult), t, t_wo)
        for oc in range(2):
            t_wg = V(lambda e, b=b, oc=oc: e.tensor_tensor(wouts[:, oc, b, :], wouts[:, oc, b, :], rows[:, b, 0, :],
                                                           ALU.mult), t_ws, t_rows)
        for i in range(NT // 2):
            k = ring.take()

            def oproj(e, b=b, i=i, k=k):
                for j in range(2):
                    n = b * S + (2 * i + j) * P
                    for oc in range(2):
                        mm = e.matmul(PS[:, k, j * D:j * D + D], wT[:, oc, n:n + P], wouts[:, oc, b, :],
                                      start=(oc == 0), stop=(oc == 1))
                return mm
            t = T(oproj, t_wg, t_d, rel[k])
            n = b * NT + 2 * i
            t = V(lambda e, n=n, k=k: e.tensor_tensor(x[:, n:n + 2, :], PS[:, k, :].rearrange("p (t d) -> p t d", d=D),
                                                      x[:, n:n + 2, :], ALU.add), t, t_xp[b])
            rel[k] = [t]
            t_x1.append(t)
    t_p1 = [t_x1[-1], t_piT[1], t_pe, t]
    c1.close()

    t_sp = [dma("sp", tokens(x1d, b), x[:, b * NT:b * NT + NT, :], t_x1[8 * b + 7]) for b in range(NB)]
    t_h2 = []
    sq_prev = None
    for g in range(8):
        b = g // 4
        ts = slice(4 * g, 4 * g + 4)
        t_xn = layernorm(g, x, t_x1[2 * g + 1], xn_free[g % 2])
        t = V(lambda e, g=g, b=b: e.tensor_tensor(xn[:, g % 2, :, :], xn[:, g % 2, :, :], bc(rows[:, b, 2, :], 4, 1),
                                                  ALU.mult), t_xn)
        t = V(lambda e, g=g, b=b, ts=ts: e.tensor_tensor(X2[:, ts, :], xn[:, g % 2, :, :], bc(rows[:, b, 1, :], 4, 1),
                                                         ALU.add), t)
        for i in range(4):
            n = 4 * g + i
            sq = A(lambda e, g=g, i=i, n=n: e.activation(xn[:, g % 2, i, :], X2[:, n, :], ACT.Square,
                                                         accum_out=ssq2[:, n:n + 1]), t)
        xn_free[g % 2] = sq
        t = A(lambda e, ts=ts: e.activation(rs2[:, ts], ssq2[:, ts], ACT.Sqrt, bias=eps[:, 1:2], scale=1.0 / D), sq)
        t_h2.append(V(lambda e, ts=ts: e.reciprocal(rs2[:, ts], rs2[:, ts]), t))
    t_p2 = [t_h2[-1], sq, t_sp]
    cX.close()

    c3 = ExitStack()
    nx = sb("nx", [P, 2, D], c=c3)
    nxT = sb("nxT", [P, 2, S], c=c3)
    QA = sb("QA", [P, 4, S], F32R, c=c3)
    QB = sb("QB", [P, 4, S], F32R, c=c3)
    KA = sb("KA", [P, NB, S], F32R, c=c3)
    KB = sb("KB", [P, NB, S], F32R, c=c3)
    ktm = sb("ktm", [P, 512], c=c3)
    VA = sb("VA", [P, NB * NT, 65], c=c3)
    PT = sb("PT", [P, 4, 1024], c=c3)
    O = sb("O", [65, S], c=c3)
    mx = sb("mx", [P, 2, NT, 4], c=c3)
    m16 = sb("m16", [P, 2, NT], c=c3)
    mT = sb("mT", [NT, 2, P], F32R, c=c3)
    rz = sb("rz", [P, 2, 1], c=c3)
    wk = sb("wk", [P, 2, P], c=c3)
    wv = sb("wv", [P, 2, 64], c=c3)
    wqp = sb("wqp", [P, 2, D], c=c3)
    woa = sb("woa", [65, 4, 257], c=c3)
    ktf, qaf = ktm, QA[:, :, :].bitcast(F32)
    kaf = KA[:, :, :].bitcast(F32)

    t_wk = dma("sp", wk[:, :, :], I["wkcT2"].rearrange("(c p) n -> p c n", p=P), t_p1, t_p2)
    t_wv = dma("sp", wv[:, :, :], I["wvcT"].rearrange("(c p) n -> p c n", p=P), t_p1, t_p2)
    t_wqp = dma("sp", wqp[:, :, :], I["wqT"].rearrange("(c p) n -> p c n", p=P), t_p1, t_p2)
    t_woa = dma("sp", woa[:, :, :], I["woA"], t_p1, t_p2)
    t = G(lambda e: e.memset(KB[64:65, :, :].bitcast(F32), -1.0), t_p1, t_p2)
    t_one = G(lambda e: e.memset(VA[:, :, 64:65], 1.0), t)

    st_nx = [None, None]
    t_nxT = {}
    nxT_free = {0: [t_p1, t_p2], 1: []}
    t_k, t_v, t_q = {}, {}, {}
    q_free = {0: [], 1: []}
    ktm_free = [None]
    cnt = [0]

    def nx_jobs(b):
        def job(i):
            n = b * NT + i
            s = cnt[0] % 2
            cnt[0] += 1
            k = ring.take()
            t = V(lambda e: e.tensor_scalar(nx[:, s, :], X2[:, n, :], rs2[:, n:n + 1], None, ALU.mult),
                  t_h2[n // 4], st_nx[s], t_p1, t_p2)

            def tr(e):
                for dc in range(2):
                    mm = e.transpose(PS[:, k, dc * P:dc * P + P], nx[:, s, dc * P:dc * P + P], ident[:, :])
                return mm
            t = T(tr, t, rel[k])
            st_nx[s] = t
            for dc in range(2):
                t2 = A(lambda e, dc=dc: e.activation(nxT[:, dc, i * P:i * P + P], PS[:, k, dc * P:dc * P + P], ACT.Copy,
                                                     scale=g1c[:, dc:dc + 1]), t, t_g1, nxT_free[b])
            rel[k] = [t2]
            t_nxT[b, i] = t2
        return [lambda i=i: job(i) for i in range(NT)]

    def k_jobs(b):
        def job(c):
            k = ring.take()

            def mmk(e):
                for dc in range(2):
                    mm = e.matmul(PS[:, k, :], wk[:, dc, :], nxT[:, dc, c * 512:c * 512 + 512], start=(dc == 0), stop=(dc == 1))
                return mm
            t = T(mmk, t_wk, t_nxT[b, 4 * c + 3], rel[k])
            cols = slice(c * 512, c * 512 + 512)
            ta = A(lambda e: e.activation(KA[0:64, b, cols], PS[0:64, k, :], ACT.Copy), t, t_p1, t_p2)
            ta = A(lambda e: e.activation(KB[0:64, b, cols], PS[0:64, k, :], ACT.Copy), t)
            th = V(lambda e: e.tensor_copy(ktm[64:128, :].bitcast(F32R), PS[64:128, k, :]), ta, ktm_free[0], t_p1, t_p2)
            tv = V(lambda e: e.tensor_tensor(KA[64:128, b, cols], PS[64:128, k, :], ktm[64:128, :], ALU.subtract), th)
            ktm_free[0] = tv
            rel[k] = [tv]
            t_k[b, c] = tv
        return [lambda c=c: job(c) for c in range(4)]

    def v_jobs(b):
        def job(c):
            k = ring.take()

            def mmv(e):
                for i in range(4):
                    for dc in range(2):
                        mm = e.matmul(PS[:, k, i * 64:i * 64 + 64], nxT[:, dc, (4 * c + i) * P:(4 * c + i + 1) * P],
                                      wv[:, dc, :], start=(dc == 0), stop=(dc == 1))
                return mm
            t = T(mmv, t_wv, t_nxT[b, 4 * c + 3], rel[k])
            n = b * NT + 4 * c
            t = A(lambda e: e.activation(VA[:, n:n + 4, 0:64], PS[:, k, 0:256].rearrange("p (t d) -> p t d", d=64),
                                         ACT.Copy), t, t_one)
            rel[k] = [t]
            t_v[b, c] = t
        return [lambda c=c: job(c) for c in range(4)]

    def q_jobs(b, pair):
        def job(c):
            k = ring.take()

            def mmq(e):
                for dc in range(2):
                    mm = e.matmul(PS[:, k, :], wqp[:, dc, pair * P:pair * P + P], nxT[:, dc, c * 512:c * 512 + 512],
                                  start=(dc == 0), stop=(dc == 1))
                return mm
            t = T(mmq, t_wqp, t_nxT[b, 4 * c + 3], rel[k])
            t_last_q[b] = t
            cols = slice(c * 512, c * 512 + 512)
            for j in range(2):
                s, r = 2 * pair + j, slice(64 * j, 64 * j + 64)
                ta = A(lambda e, s=s, r=r: e.activation(QA[0:64, s, cols], PS[r, k, :], ACT.Copy), t, q_free[pair], t_p1, t_p2)
                ta = A(lambda e, s=s, r=r: e.activation(QA[64:128, s, cols], PS[r, k, :], ACT.Copy), t)
                tv = V(lambda e, s=s, r=r: e.tensor_tensor(QB[0:64, s, cols], PS[r, k, :], qaf[r, s, cols], ALU.subtract),
                       ta, q_free[pair])
                t_q[b, 2 * pair + j, c] = tv
                t = tv if j == 0 else t
            rel[k] = [tv]
        return [lambda c=c: job(c) for c in range(4)]

    t_last_q = {}
    mx_free = [None, None]
    m_free = [None, None]
    t_m = {}

    def max_jobs(bh):
        b, h = bh // 4, bh % 4
        s = bh % 2

        def job(i, c):
            k = ring.take()
            t = T(lambda e: e.matmul(PS[:, k, :], QA[:, h, i * P:i * P + P], KA[:, b, c * 512:c * 512 + 512],
                                     start=True, stop=True), t_q[b, h, i // 4], t_k[b, c], rel[k])
            t = V(lambda e: e.tensor_reduce(mx[:, s, i, c:c + 1], PS[:, k, :], AX, ALU.max), t, mx_free[s], t_p1, t_p2)
            rel[k] = [t]

        def close():
            k = ring.take()
            t = V(lambda e: e.tensor_reduce(m16[:, s, :], mx[:, s, :, :], AX, ALU.max), rel[ring.banks[0]],
                  rel[ring.banks[1 % len(ring.banks)]], [rel[x] for x in ring.banks], m_free[s])
            mx_free[s] = t
            t = T(lambda e: e.transpose(PS[0:NT, k, 0:P], m16[:, s, :], ident[:, :]), t, rel[k])
            t = V(lambda e: e.tensor_copy(mT[:, s, :], PS[0:NT, k, 0:P]), t, m_free[s], t_p1, t_p2)
            rel[k] = [t]
            t_m[bh] = dma("sp", QB[64:65, h, :].bitcast(F32), mT[:, s, :].bitcast(F32), t, q_free[h // 2])
            m_free[s] = t_m[bh]
        return [lambda i=i, c=c: job(i, c) for i in range(NT) for c in range(4)] + [close]

    O_free = [t_p1 + t_p2, []]
    t_O = {}
    rz_free = [None, None]
    t_X2 = {}

    def proj_jobs(bh):
        b, h = bh // 4, bh % 4

        def job(i):
            k = ring.take()
            s = i % 2
            n = b * NT + i
            t = T(lambda e: e.matmul(PS[:, k, 0:257], O[0:65, i * P:i * P + P], woa[0:65, h, :], start=True, stop=True),
                  t_O[bh, i // 8], t_woa, rel[k])
            O_free[i // 8] = [t]
            t = V(lambda e: e.reciprocal(rz[:, s, :], PS[:, k, 256:257]), t, rz_free[s], t_p1, t_p2)
            t = V(lambda e: e.scalar_tensor_tensor(X2[:, n, :], PS[:, k, 0:256], rz[:, s, :], X2[:, n, :],
                                                   ALU.mult, ALU.add), t, t_X2.get(n), st_nx)
            rz_free[s] = t
            t_X2[n] = t
            rel[k] = [t]
        return [lambda i=i: job(i) for i in range(NT)]

    SB = [(0, 1), (2, 3)]
    pt_free = [None] * 4
    step = [0]

    def main(bh, jobs):
        b, h = bh // 4, bh % 4
        nstep = 32
        state = {}

        def qk(i):
            qc, kc = divmod(i, 16)
            gs = step[0] + i
            bk = SB[gs % 2]

            def f(e):
                for n in range(2):
                    q0 = qc * 1024 + n * 512
                    e.matmul(PS[:, bk[n], :], KA[:, b, kc * P:kc * P + P], QA[:, h, q0:q0 + 512], start=True, stop=False)
                for n in range(2):
                    q0 = qc * 1024 + n * 512
                    mm = e.matmul(PS[:, bk[n], :], KB[0:65, b, kc * P:kc * P + P], QB[0:65, h, q0:q0 + 512],
                                  start=False, stop=True)
                return mm
            t = T(f, t_m[bh], [t_q[b, h, c] for c in range(4)], t_k[b, kc // 4], t_one, rel[bk[0]], rel[bk[1]])
            ps = gs % 4
            t = A(lambda e: e.activation(PT[:, ps, :], PS[:, bk[0]:bk[0] + 2, :].rearrange("p a n -> p (a n)"), ACT.Exp,
                                         scale=0.125), t, pt_free[ps], t_p1, t_p2)
            rel[bk[0]], rel[bk[1]] = [t], [t]
            state[i] = (t, ps)

        def av(i):
            qc, kc = divmod(i, 16)
            t, ps = state[i]

            def f(e):
                for n in range(2):
                    mm = e.matmul(PS[0:65, 4 + n, :], VA[:, b * NT + kc, :], PT[:, ps, n * 512:n * 512 + 512],
                                  start=(kc == 0), stop=(kc == 15))
                return mm
            t = T(f, t, t_v[b, kc // 4], rel[4] if kc == 0 else None, rel[5] if kc == 0 else None)
            pt_free[ps] = t
            if kc == 15:
                t = A(lambda e: e.activation(O[:, qc * 1024:qc * 1024 + 1024],
                                             PS[0:65, 4:6, :].rearrange("p a n -> p (a n)"), ACT.Copy), t, O_free[qc])
                t_O[bh, qc] = t
                rel[4], rel[5] = [t], [t]
            return t

        per = -(-len(jobs) // (nstep - 3)) if jobs else 0
        qk(0)
        for i in range(nstep):
            if i + 1 < nstep:
                qk(i + 1)
            for j in jobs[i * per:(i + 1) * per]:
                j()
            tl = av(i)
        q_done = pr.n["pe"]
        step[0] += nstep
        return (pr.sem["pe"], q_done)

    for j in nx_jobs(0) + k_jobs(0) + v_jobs(0) + q_jobs(0, 0) + max_jobs(0):
        j()
    ring = Ring([6, 7])
    rel_pre = [rel[i] for i in range(6)]
    for bh in range(8):
        b, h = bh // 4, bh % 4
        jobs = proj_jobs(bh - 1) if bh else []
        if h == 0:
            jobs = q_jobs(b, 1) + jobs
        if b == 0 and h == 1:
            nxT_free[1] = [t_last_q[0]]
            jobs = jobs + nx_jobs(1)
        if b == 0 and h == 2:
            jobs = jobs + k_jobs(1) + v_jobs(1) + q_jobs(1, 0)
        if bh < 7:
            jobs = jobs + max_jobs(bh + 1)
        t_main = main(bh, jobs)
        if h % 2:
            q_free[h // 2] = [t_main]
    ring = Ring([6, 7, 0, 1, 2, 3])
    for j in proj_jobs(7):
        j()
    t_p3 = [t_main, t_X2[31], (pr.sem["pe"], pr.n["pe"]), (pr.sem["act"], pr.n["act"]), (pr.sem["dve"], pr.n["dve"])]
    c3.close()

    c4 = ExitStack()
    xh = sb("xh", [P, 2, NB * S], F32R, c=c4)
    xl = sb("xl", [P, 2, NB * S], F32R, c=c4)
    xhf = xh[:, :, :].bitcast(F32)
    nx2 = sb("nx2", [P, 2, D], c=c4)
    sq2 = sb("sq2", [P, D], c=c4)
    wr = sb("wr", [P, 2, NE], c=c4)
    wrh = sb("wrh", [P, 2, NE], F32R, c=c4)
    wrl = sb("wrl", [P, 2, NE], F32R, c=c4)
    ebB = sb("ebB", [P, NE], c=c4)
    pri = sb("pri", [P, NE], c=c4)
    rl = sb("rl", [P, 32, NE], c=c4)
    rq = sb("rq", [P, 32, NE], c=c4)
    oh1 = sb("oh1", [P, 32, NE], c=c4)
    oh2 = sb("oh2", [P, 32, NE], c=c4)
    comb = sb("comb", [P, 32, NE], c=c4)
    rm = sb("rm", [P, 8, 32], c=c4)
    wst = sb("wst", [P, 2, 2, 768], c=c4)
    wh = sb("wh", [P, 2, 2, 768], F32R, c=c4)
    wl = sb("wl", [P, 2, 2, 768], F32R, c=c4)
    whf = wh[:, :, :, :].bitcast(F32)
    sg = sb("sg", [P, 2, 512], c=c4)
    hg = sb("hg", [P, 2, 512], c=c4)
    hh = sb("hh", [P, 2, 2, 512], F32R, c=c4)
    hl = sb("hl", [P, 2, 2, 512], F32R, c=c4)
    hhf = hh[:, :, :, :].bitcast(F32)

    t_wr = dma("sp", wr[:, :, :], I["wrT"].rearrange("(c p) n -> p c n", p=P), t_p3)
    t_eb = dma("sp", ebB[:, :], I["ebias"].unsqueeze(0).to_broadcast([P, NE]), t_p3)
    t_pri = dma("sp", pri[:, :], I["pri"].unsqueeze(0).to_broadcast([P, NE]), t_p3)
    order = [NE] + list(range(NE))
    t_wst = {}
    w_free = [t_p3, t_p3]
    t_wsp = {}
    wd = I["wexp"].rearrange("e (c p) n -> e p c n", p=P)

    def load_w(j):
        s = j % 2
        t_wst[j] = dma("sp", wst[:, s, :, :], wd[order[j]], t_p3, t_wsp[j - 2] if j >= 2 else None)

    def split_w(j):
        s = j % 2
        t1 = G(lambda e: e.tensor_copy(wh[:, s, :, :], wst[:, s, :, :]), t_wst[j], w_free[s], t_wsp.get(j - 1))
        t_wsp[j] = G(lambda e: e.tensor_tensor(wl[:, s, :, :], wst[:, s, :, :], whf[:, s, :, :], ALU.subtract), t1)

    load_w(0)
    load_w(1)
    split_w(0)
    split_w(1)
    t1 = V(lambda e: e.tensor_copy(wrh[:, :, :], wr[:, :, :]), t_wr, t_p3)
    t_wrl = V(lambda e: e.tensor_tensor(wrl[:, :, :], wr[:, :, :], wrh[:, :, :].bitcast(F32), ALU.subtract), t1)

    t_sq = None
    for n in range(32):
        t = A(lambda e, n=n: e.activation(sq2[:, :], X2[:, n, :], ACT.Square, accum_out=ssq2[:, n:n + 1]), t_X2[n], t_p3, t_sq)
        t_sq = t
    t = A(lambda e: e.activation(rs2[:, :], ssq2[:, :], ACT.Sqrt, bias=eps[:, 1:2], scale=1.0 / D), t)
    t_rs = V(lambda e: e.reciprocal(rs2[:, :], rs2[:, :]), t)
    ring = Ring([0, 1, 2, 3, 4, 5])
    for i in range(8):
        rel[i] = rel[i] + t_p3
    nxf = [None, None]
    t_xT = {}
    for n in range(32):
        s = n % 2
        t = V(lambda e, n=n, s=s: e.tensor_scalar(nx2[:, s, :], X2[:, n, :], rs2[:, n:n + 1], None, ALU.mult), t_rs, nxf[s])
        k = ring.take()

        def tr(e, s=s, k=k):
            for dc in range(2):
                mm = e.transpose(PS[:, k, dc * P:dc * P + P], nx2[:, s, dc * P:dc * P + P], ident[:, :])
            return mm
        t = T(tr, t, rel[k])
        nxf[s] = t
        cols = slice(n * P, n * P + P)
        for dc in range(2):
            ta = A(lambda e, dc=dc, k=k, cols=cols: e.activation(xh[:, dc, cols], PS[:, k, dc * P:dc * P + P], ACT.Copy,
                                                                 scale=g2c[:, dc:dc + 1]), t, t_g2)
        for dc in range(2):
            tv = V(lambda e, dc=dc, k=k, cols=cols: e.scalar_tensor_tensor(
                xl[:, dc, cols], PS[:, k, dc * P:dc * P + P], g2c[:, dc:dc + 1], xhf[:, dc, cols], ALU.mult, ALU.subtract), ta)
        rel[k] = [tv]
        t_xT[n] = tv

    pl = PS[:, 6, 0:256].rearrange("p (t e) -> p t e", e=NE)

    def router(e):
        for n in range(32):
            i = 0
            for dc in range(2):
                for a, w in ((xl, wrh), (xh, wrl), (xh, wrh)):
                    mm = e.matmul(pl[:, n, :], a[:, dc, n * P:n * P + P], w[:, dc, :], start=(i == 0), stop=(i == 5))
                    i += 1
        return mm
    tr_ = T(router, t_xT[31], t_wrl, rel[6])
    t = V(lambda e: e.tensor_tensor(rl[:, :, :], pl, bc(ebB[:, :], 32, 1), ALU.add), tr_, t_eb)
    rel[6] = [t]

    def b8(ap):
        return bc(ap, NE, 2)
    t = V(lambda e: e.tensor_reduce(rm[:, 0, :], rl[:, :, :], AX, ALU.max), t)
    t = V(lambda e: e.tensor_tensor(rl[:, :, :], rl[:, :, :], b8(rm[:, 0, :]), ALU.subtract), t)
    t = A(lambda e: e.activation(rq[:, :, :], rl[:, :, :], ACT.Exp), t)
    t = V(lambda e: e.tensor_reduce(rm[:, 1, :], rq[:, :, :], AX, ALU.add), t)
    t = V(lambda e: e.reciprocal(rm[:, 1, :], rm[:, 1, :]), t)
    t = V(lambda e: e.tensor_tensor(rq[:, :, :], rq[:, :, :], b8(rm[:, 1, :]), ALU.mult), t)
    for r, (oh, col) in enumerate(((oh1, 2), (oh2, 3))):
        t = V(lambda e, col=col: e.tensor_reduce(rm[:, col, :], rq[:, :, :], AX, ALU.max), t)
        t = V(lambda e, oh=oh, col=col: e.tensor_tensor(oh[:, :, :], rq[:, :, :], b8(rm[:, col, :]), ALU.is_equal), t)
        t = V(lambda e, oh=oh: e.tensor_tensor(oh[:, :, :], oh[:, :, :], bc(pri[:, :], 32, 1), ALU.mult), t, t_pri)
        t = V(lambda e, oh=oh: e.tensor_reduce(rm[:, 4, :], oh[:, :, :], AX, ALU.max), t)
        t = V(lambda e, oh=oh: e.tensor_tensor(oh[:, :, :], oh[:, :, :], b8(rm[:, 4, :]), ALU.is_equal), t)
        if r == 0:
            t = V(lambda e: e.scalar_tensor_tensor(rq[:, :, :], oh1[:, :, :], -4.0, rq[:, :, :], ALU.mult, ALU.add), t)
    t = V(lambda e: e.tensor_tensor(rm[:, 5, :], rm[:, 3, :], rm[:, 2, :], ALU.subtract), t)
    t = A(lambda e: e.activation(rm[:, 5, :], rm[:, 5, :], ACT.Exp), t)
    t = V(lambda e: e.tensor_scalar_add(rm[:, 6, :], rm[:, 5, :], 1.0), t)
    t = V(lambda e: e.reciprocal(rm[:, 6, :], rm[:, 6, :]), t)
    t = V(lambda e: e.tensor_tensor(rm[:, 7, :], rm[:, 5, :], rm[:, 6, :], ALU.mult), t)
    t1 = V(lambda e: e.tensor_tensor(oh1[:, :, :], oh1[:, :, :], b8(rm[:, 6, :]), ALU.mult), t)
    t2 = V(lambda e: e.tensor_tensor(oh2[:, :, :], oh2[:, :, :], b8(rm[:, 7, :]), ALU.mult), t)
    t_cb = V(lambda e: e.tensor_tensor(comb[:, :, :], oh1[:, :, :], oh2[:, :, :], ALU.add), t1, t2)

    gu = Ring([0, 1, 2, 3])
    yr = Ring([4, 5, 6, 7])
    sgf = [None, None]
    hgf = [None, None]
    hf = [None, None]
    it = 0
    t_acc = dict(t_X2)

    def up(j, c):
        s, hs = j % 2, (j * 8 + c) % 2
        res = []
        for fc in range(2):
            ps = []
            for m in range(2):
                k = gu.take()

                def f(e, k=k, m=m, fc=fc):
                    i = 0
                    f0 = m * 256 + fc * P
                    for dc in range(2):
                        for w, a in ((wh, xh), (wh, xl), (wl, xh)):
                            mm = e.matmul(PS[:, k, :], w[:, s, dc, f0:f0 + P], a[:, dc, c * 512:c * 512 + 512],
                                          start=(i == 0), stop=(i == 5))
                            i += 1
                    return mm
                ps.append((k, T(f, t_wsp[j], t_xT[31], rel[k])))
            (k0, t0), (k1, t1) = ps
            ta = A(lambda e, k0=k0, fc=fc: e.activation(sg[:, fc, :], PS[:, k0, :], ACT.Silu), t0, sgf[fc], t_p3)
            rel[k0] = [ta]
            tv = V(lambda e, k1=k1, fc=fc: e.tensor_tensor(hg[:, fc, :], PS[:, k1, :], sg[:, fc, :], ALU.mult), t1, ta,
                   hgf[fc], t_p3)
            rel[k1] = [tv]
            sgf[fc] = tv
            ta = A(lambda e, fc=fc: e.activation(hh[:, hs, fc, :], hg[:, fc, :], ACT.Copy), tv, hf[hs], t_p3)
            tv = V(lambda e, fc=fc: e.tensor_tensor(hl[:, hs, fc, :], hg[:, fc, :], hhf[:, hs, fc, :], ALU.subtract), ta, tv,
                   hf[hs], t_p3)
            hgf[fc] = tv
            res.append(tv)
        return res

    def down(j, c, th):
        s, hs = j % 2, (j * 8 + c) % 2
        for i in range(4):
            n = 4 * c + i
            k = yr.take()

            def f(e, k=k, i=i):
                q = 0
                for fc in range(2):
                    for a, w in ((hh, wh), (hh, wl), (hl, wh)):
                        mm = e.matmul(PS[:, k, 0:256], a[:, hs, fc, i * P:i * P + P], w[:, s, fc, 512:768],
                                      start=(q == 0), stop=(q == 5))
                        q += 1
                return mm
            t = T(f, th, rel[k])
            ex = order[j]
            if ex == NE:
                tv = V(lambda e, n=n, k=k: e.tensor_tensor(X2[:, n, :], PS[:, k, 0:256], X2[:, n, :], ALU.add), t, t_acc[n],
                       t_rs, nxf)
            else:
                tv = V(lambda e, n=n, k=k, ex=ex: e.scalar_tensor_tensor(
                    X2[:, n, :], PS[:, k, 0:256], comb[:, n, ex:ex + 1], X2[:, n, :], ALU.mult, ALU.add), t, t_cb, t_acc[n])
            rel[k] = [tv]
            t_acc[n] = tv
        hf[hs] = t
        return t

    seq = [(j, c) for j in range(9) for c in range(8)]
    th = up(*seq[0])
    for i, (j, c) in enumerate(seq):
        nth = up(*seq[i + 1]) if i + 1 < len(seq) else None
        t_dn = down(j, c, th)
        th = nth
        if c == 7:
            w_free[j % 2] = [t_dn]
            if j + 2 < 9:
                load_w(j + 2)
                split_w(j + 2)

    xo = wst[:, :, :, :].rearrange("p a b n -> p (a b n)")[:, 0:2048].rearrange("p (s t d) -> p s t d", s=2, d=D)
    t_o = [[t_wsp[8], t_wsp[7]], [t_wsp[8], t_wsp[7]]]
    t_fin = []
    for g in range(8):
        b, s = g // 4, g % 2
        ts = slice(4 * g, 4 * g + 4)
        tl = dma("sp", xo[:, s, :, :], tokens(x1d, b)[:, 4 * (g % 4):4 * (g % 4) + 4, :], t_o[s], t_sp)
        t = V(lambda e, ts=ts, b=b: e.tensor_tensor(X2[:, ts, :], X2[:, ts, :], bc(gb[:, b, :], 4, 1), ALU.mult),
              [t_acc[n] for n in range(4 * g, 4 * g + 4)])
        t = V(lambda e, ts=ts, s=s: e.tensor_tensor(X2[:, ts, :], X2[:, ts, :], xo[:, s, :, :], ALU.add), t, tl)
        t_o[s] = [t]
        t_fin.append(dma("act", tokens(out, b)[:, 4 * (g % 4):4 * (g % 4) + 4, :], X2[:, ts, :], t))
    pr.wait("sp", t_fin)
    c4.close()

    block = ctx.enter_context(nc.Block())

    @block.sync
    def _(eng):
        pr.play("sp", eng)

    @block.scalar
    def _(eng):
        pr.play("act", eng)

    @block.vector
    def _(eng):
        pr.play("dve", eng)

    @block.gpsimd
    def _(eng):
        pr.play("pool", eng)

    @block.tensor
    def _(eng):
        pr.play("pe", eng)


def kernel(**inputs):
    import numpy as np
    import concourse.bacc as bacc
    from concourse.bass_utils import run_bass_kernel_spmd

    a = {k: np.asarray(v) for k, v in inputs.items()}

    def tr(w):
        return np.ascontiguousarray(np.swapaxes(w, -1, -2))

    mask = np.zeros((D, 16), np.float32)
    mask[np.arange(D), np.arange(D) // 16] = 1.0
    woa = np.zeros((65, 4, 257), np.float32)
    woa[0:64, :, 0:256] = tr(a["L0_ffn_Wo"]).reshape(4, 64, D).transpose(1, 0, 2)
    woa[64, :, 256] = 1.0
    wexp = np.zeros((NE + 1, D, 768), np.float32)
    for i, (e, s) in enumerate((("eW1", "sW1"), ("eW3", "sW3"), ("eW2", "sW2"))):
        wexp[:NE, :, i * D:i * D + D] = tr(a["L0_ffn_" + e])
        wexp[NE, :, i * D:i * D + D] = tr(a["L0_ffn_" + s])
    wk = tr(a["L0_ffn_Wkc"])
    arrays = {
        "x": a["L0_attn_x"], "cT": tr(a["L0_c"]), "wmod": a["L0_wmod"],
        "wqkvT": tr(a["L0_attn_Wqkv"]), "woutT": tr(a["L0_attn_Wout"]), "bout": a["L0_attn_bout"],
        "temp": a["L0_attn_temp"], "g1": tr(a["L0_ffn_g1"].reshape(2, P)), "g2": tr(a["L0_ffn_g2"].reshape(2, P)),
        "wqT": tr(a["L0_ffn_Wq"]), "wkcT2": np.concatenate([wk, wk], axis=1), "wvcT": tr(a["L0_ffn_Wvc"]),
        "woA": woa, "wrT": tr(a["L0_ffn_Wr"]), "ebias": a["L0_ffn_expert_bias"], "wexp": wexp,
        "ident": np.eye(P, dtype=np.float32), "mask": mask,
        "pri": np.arange(NE, 0, -1).astype(np.float32),
    }
    nc = bacc.Bacc("TRN2", target_bir_lowering=False, num_devices=1)
    I, feeds = {}, {}
    for n, v in arrays.items():
        v = np.ascontiguousarray(v)
        feeds["in_" + n] = v
        I[n] = nc.dram_tensor("in_" + n, v.shape, mybir.dt.from_np(v.dtype), kind="ExternalInput").ap()
    out = nc.dram_tensor("out_0", (NB, S, D), F32, kind="ExternalOutput").ap()
    build(nc, I, out)
    r = run_bass_kernel_spmd(nc, [feeds], core_ids=[0])
    return r.results[0]["out_0"]
```

```python
from contextlib import ExitStack

import concourse.bass as bass
from concourse import mybir

ALU = mybir.AluOpType
ACT = mybir.ActivationFunctionType
F32 = mybir.dt.float32
F32R = mybir.dt.float32r
AX = mybir.AxisListType.X

P = 128
D = 256
NB = 2
NT = 16
S = 2048
NE = 8
EPS_LN = 1e-5
EPS_RMS = 1e-6
POOL_EVERY = 4
NTI = 39


class Prog:

    def __init__(self, nc, ctx):
        self.nc, self.ctx = nc, ctx
        self.q = {k: [] for k in ("pe", "act", "dve", "pool", "sp")}
        self.sem = {k: ctx.enter_context(nc.semaphore("s_" + k)) for k in ("pe", "act", "dve", "pool")}
        self.n = {k: 0 for k in self.sem}
        self.dsem = 0

    def put(self, k, fn, waits):
        self.n[k] += 1
        self.q[k].append((flat(waits), fn, self.sem[k], 1))
        return (self.sem[k], self.n[k])

    def T(self, fn, *w):
        return self.put("pe", fn, w)

    def A(self, fn, *w):
        return self.put("act", fn, w)

    def V(self, fn, *w):
        return self.put("dve", fn, w)

    def G(self, fn, *w):
        return self.put("pool", fn, w)

    def counter(self):
        self.dsem += 1
        return [self.ctx.enter_context(self.nc.semaphore(f"d{self.dsem}")), 0]

    def dma(self, k, out, in_, *w, on=None):
        return self.start(k, lambda e: e.dma_start(out, in_), w, on)

    def start(self, k, fn, w, on=None):
        on = on or self.counter()
        on[1] += 1
        self.q[k].append((flat(w), fn, on[0], 16))
        return (on[0], 16 * on[1])

    def do(self, k, fn, *w):
        self.q[k].append((flat(w), fn, None, 0))

    def wait(self, k, *w):
        self.q[k].append((flat(w), None, None, 0))

    def play(self, k, eng):
        seen = {}
        for waits, fn, sem, inc in self.q[k]:
            for s, v in waits:
                if seen.get(s.num, 0) < v:
                    eng.wait_ge(s, v)
                    seen[s.num] = v
            if fn is not None:
                ins = fn(eng)
                if sem is not None:
                    ins.then_inc(sem, inc)


def flat(x):
    out = []
    for y in x:
        if y is None:
            continue
        if isinstance(y, list):
            out += flat(y)
        else:
            out.append(y)
    return out


def bc(ap, n, axis):
    return ap.unsqueeze(axis).to_broadcast(list(ap.shape[:axis]) + [n] + list(ap.shape[axis:]))


def build(nc, I, out):
    with ExitStack() as ctx:
        _build(nc, ctx, I, out)


def _build(nc, ctx, I, out):
    pr = Prog(nc, ctx)
    T, A, V, G, dma = pr.T, pr.A, pr.V, pr.G, pr.dma

    def sb(name, shape, dt=F32, c=None):
        return (c or ctx).enter_context(nc.sbuf_tensor(name, shape, dt))

    PS = ctx.enter_context(nc.psum_tensor("PS", [P, 8, 512], F32))
    rel = {i: [] for i in range(8)}

    class Ring:
        def __init__(self, banks):
            self.banks, self.i = banks, 0

        def take(self):
            b = self.banks[self.i % len(self.banks)]
            self.i += 1
            return b

    ident = sb("ident", [P, P])
    X2 = sb("X2", [P, NB * NT, D])
    gb = sb("gb", [P, NB, D])
    g1c = sb("g1c", [P, 2])
    g2c = sb("g2c", [P, 2])
    eps = sb("eps", [P, 2])
    ssq2 = sb("ssq2", [P, NB * NT])
    rs2 = sb("rs2", [P, NB * NT])
    x1d = nc.dram_tensor("x1_scratch", [NB, S, D], F32, kind="Internal").ap()

    tri = sb("tri", [P, 2, P])
    ebB = sb("ebB", [P, NE])
    pri = sb("pri", [P, NE])
    thr = sb("thr", [1, NTI])
    wr = sb("wr", [P, 2, NE])
    r_l = sb("r_l", [P, NT, NE])
    r_q = sb("r_q", [P, NT, NE])
    r_M = sb("r_M", [P, NE, NT])
    r_s = r_l[:, :, :].rearrange("p t e -> p (t e)").rearrange("p (e t) -> p e t", e=NE)
    r_c = r_q[:, :, :].rearrange("p t e -> p (t e)").rearrange("p (e t) -> p e t", e=NE)
    r_e = sb("r_e", [P, 6, NE])
    r_i = sb("r_i", [P, NE], mybir.dt.int32)
    r_t = sb("r_t", [1, NTI, NE])
    r_v = sb("r_v", [1, NTI])
    rm = sb("rm", [P, 8, NT])
    oh1 = sb("oh1", [P, NT, NE])
    oh2 = sb("oh2", [P, NT, NE])
    gate = sb("gate", [P, NB, 2, NT])
    slot = sb("slot", [P, NB, 2, NT], mybir.dt.int32)
    texp = sb("texp", [1, NB, NTI], mybir.dt.int32)
    nx = sb("nx", [P, 2, D])
    xT = sb("xT", [P, 2, 2, P])
    zero = sb("zero", [P, D])
    xbuf = [nc.dram_tensor(f"xbuf{b}", [NTI * P, D], F32, kind="Internal").ap() for b in range(NB)]
    ybuf = [nc.dram_tensor(f"ybuf{b}", [NTI * P, D], F32, kind="Internal").ap() for b in range(NB)]

    t_id = dma("sp", ident[:, :], I["ident"])
    t_tri = dma("act", tri[:, :, :], I["tri"])
    t_thr = dma("act", thr[:, :], I["thr"])
    t_wr0 = dma("act", wr[:, :, :], I["wrT"].rearrange("(c p) n -> p c n", p=P))
    t_eb = dma("act", ebB[:, :], I["ebias"].unsqueeze(0).to_broadcast([P, NE]))
    t_pri = dma("act", pri[:, :], I["pri"].unsqueeze(0).to_broadcast([P, NE]))
    t_g1 = dma("act", g1c[:, :], I["g1"])
    t_g2 = dma("act", g2c[:, :], I["g2"])
    t_e0 = V(lambda e: e.memset(eps[:, 0:1], EPS_LN))
    t_eps = V(lambda e: e.memset(eps[:, 1:2], EPS_RMS))
    for dc in range(2):
        t_wr = V(lambda e, dc=dc: e.tensor_scalar(wr[:, dc, :], wr[:, dc, :], g2c[:, dc:dc + 1], None, ALU.mult), t_wr0, t_g2)
    t_z = G(lambda e: e.memset(zero[:, :], 0.0))

    def tokens(ap, b):
        return ap[b].rearrange("(p t) d -> p t d", t=NT)

    c1 = ExitStack()
    cX = ExitStack()
    x = sb("x", [P, NB * NT, D], c=cX)
    rows = sb("rows", [P, NB, 4, D], c=cX)
    st = sb("st", [P, 4, 6], c=cX)
    mv = sb("mv", [P, NB * NT, 2], c=cX)
    sd = sb("sd", [P, NB * NT], c=cX)
    rs = sb("rs", [P, NB * NT], c=cX)
    xn = sb("xn", [P, 2, 4, D], c=cX)

    cT = sb("cT", [P, 2, NB], c=c1)
    sil = sb("sil", [P, 2, NB], c=c1)
    silB = sb("silB", [P, 2, NB, P], c=c1)
    sc = sb("sc", [P, 2, NB], c=c1)
    modc = sb("modc", [P, 2, 2, NB], c=c1)
    gab = sb("gab", [P, NB, D], c=c1)
    boutB = sb("boutB", [P, D], c=c1)
    gtmp = sb("gtmp", [P, 2, D], c=c1)
    wqkv = sb("wqkv", [P, 2, D], c=c1)
    wout = sb("wout", [P, 2, D], c=c1)
    wouts = sb("wouts", [P, 2, NB, D], c=c1)
    mask = sb("mask", [P, 2, 16], c=c1)
    tempB = sb("tempB", [P, 16], c=c1)
    LB = sb("LB", [P, 2, NB, 16], c=c1)
    ssq = sb("ssq", [P, 2, NB, 4], c=c1)
    n2 = sb("n2", [P, 2, NB], c=c1)
    piS = sb("piS", [P, 2, NB, 4], c=c1)
    dS = sb("dS", [P, 2, NB, 4], c=c1)
    cf = sb("cf", [P, 2, NB, 3], c=c1)
    lg = sb("lg", [P, NT, 16], c=c1)
    le = sb("le", [P, NT, 16], c=c1)
    lm = sb("lm", [P, NB, NT, 3], c=c1)
    piE = sb("piE", [P, 4, D], c=c1)
    hT = sb("hT", [P, 2, 512], c=c1)
    wT = sb("wT", [P, 2, NB * S], c=c1)
    w2T = sb("w2T", [P, 2, NB * S], c=c1)
    piT = sb("piT", [P, 2, 512], c=c1)
    junk = sb("junk", [P, 512], c=c1)

    cm = ExitStack()
    wmod = sb("wmod", [P, 2, 6 * D], c=cm)

    t_c = dma("sp", cT[:, :, :], I["cT"].rearrange("(c p) b -> p c b", p=P))
    t_wm = dma("sp", wmod[:, :, :], I["wmod"].rearrange("(c p) n -> p c n", p=P))
    t_x = []
    for b in range(NB):
        for g in range(4):
            t_x.append(dma("sp", x[:, b * NT + 4 * g:b * NT + 4 * g + 4, :], tokens(I["x"], b)[:, 4 * g:4 * g + 4, :]))
    t_wq = dma("act", wqkv[:, :, :], I["wqkvT"].rearrange("(c p) n -> p c n", p=P))
    t_mk = dma("act", mask[:, :, :], I["mask"].rearrange("(c p) n -> p c n", p=P))
    t_tp = dma("act", tempB[:, :], I["temp"].rearrange("h o -> o h").to_broadcast([P, 16]))
    t_wo = dma("act", wout[:, :, :], I["woutT"].rearrange("(c p) n -> p c n", p=P))
    t_bo = dma("act", boutB[:, :], I["bout"].unsqueeze(0).to_broadcast([P, D]))

    t = A(lambda e: e.activation(sc[:, :, :], cT[:, :, :], ACT.Exp, scale=-1.0), t_c)
    t = V(lambda e: e.tensor_scalar_add(sc[:, :, :], sc[:, :, :], 1.0), t)
    t = V(lambda e: e.reciprocal(sc[:, :, :], sc[:, :, :]), t)
    t_sil = V(lambda e: e.tensor_tensor(sil[:, :, :], sc[:, :, :], cT[:, :, :], ALU.mult), t)
    t_silB = V(lambda e: e.tensor_copy(silB[:, :, :, :], bc(sil[:, :, :], P, 3)), t_sil)

    def mod_cols(e):
        for i in range(2):
            for j in range(2):
                for k in range(2):
                    mm = e.matmul(PS[:, 0, (i * 2 + j) * 2:(i * 2 + j) * 2 + 2],
                                  wmod[:, k, i * D + j * P:i * D + j * P + P], sil[:, k, :],
                                  start=(k == 0), stop=(k == 1))
        return mm
    t = T(mod_cols, t_wm, t_sil)
    pm = PS[:, 0, 0:8].rearrange("p (i j b) -> p i j b", i=2, j=2)
    V(lambda e: e.tensor_copy(modc[:, 0, :, :], pm[:, 0, :, :]), t)
    t_modc = V(lambda e: e.tensor_scalar_add(modc[:, 1, :, :], pm[:, 1, :, :], 1.0), t)
    rel[0] = [t_modc]

    t_rows = []
    for b in range(NB):
        def mod_rows(e, b=b):
            for n in range(2):
                for k in range(2):
                    mm = e.matmul(PS[:, 2 + 2 * b + n, :], silB[:, k, b, :],
                                  wmod[:, k, 2 * D + n * 512:2 * D + n * 512 + 512], start=(k == 0), stop=(k == 1))
            return mm
        t_mr = T(mod_rows, t_wm, t_silB)
        pg = PS[:, 2 + 2 * b:4 + 2 * b, :].rearrange("p a (c d) -> p (a c) d", c=2)
        for i, dst in ((0, rows[:, b, 0, :]), (3, gb[:, b, :])):
            t1 = V(lambda e, i=i, pg=pg: e.tensor_scalar(gtmp[:, 0, :], pg[:, i, :], 0.0, 2.0, ALU.is_ge, ALU.mult), t_mr,
                   t_rows[-1:])
            t2 = V(lambda e, i=i, pg=pg: e.tensor_scalar(gtmp[:, 1, :], pg[:, i, :], -1.0, None, ALU.mult), t_mr, t_rows[-1:])
            t2 = V(lambda e, i=i, pg=pg: e.scalar_tensor_tensor(gtmp[:, 1, :], pg[:, i, :], 0.25, gtmp[:, 1, :],
                                                                ALU.max, ALU.max), t2)
            t_rows.append(V(lambda e, dst=dst: e.scalar_tensor_tensor(dst, gtmp[:, 0, :], -1.0, gtmp[:, 1, :],
                                                                      ALU.add, ALU.mult), t1, t2))
        V(lambda e, b=b, pg=pg: e.tensor_copy(rows[:, b, 1, :], pg[:, 1, :]), t_mr)
        t_r = V(lambda e, b=b, pg=pg: e.tensor_scalar_add(rows[:, b, 2, :], pg[:, 2, :], 1.0), t_mr)
        t_rows.append(t_r)
        rel[2 + 2 * b] = [t_r]
        rel[3 + 2 * b] = [t_r]
        t_gab = V(lambda e, b=b: e.tensor_tensor(gab[:, b, :], rows[:, b, 0, :], boutB[:, :], ALU.mult), t_rows, t_bo)
    cm.close()

    ring = Ring([0, 1, 2, 3, 4, 5, 6, 7])

    def layernorm(g, src, tsrc, twrite):
        ts = slice(4 * g, 4 * g + 4)
        for i in range(4):
            ta = V(lambda e, i=i: e.bn_stats(st[:, i, :], src[:, 4 * g + i, :]), tsrc, ln_done[-1:])
        for i in range(4):
            tb = V(lambda e, i=i: e.bn_aggr(mv[:, 4 * g + i, :], st[:, i, :]), ta)
        ln_done.append(tb)
        tc = A(lambda e: e.activation(sd[:, ts], mv[:, ts, 1], ACT.Sqrt, bias=eps[:, 0:1]), tb, t_eps)
        td = V(lambda e: e.reciprocal(rs[:, ts], sd[:, ts]), tc)
        for i in range(4):
            n = 4 * g + i
            t = V(lambda e, i=i, n=n: e.tensor_scalar(xn[:, g % 2, i, :], src[:, n, :], mv[:, n, 0:1], rs[:, n:n + 1],
                                                      ALU.subtract, ALU.mult), td, twrite)
        return t

    ln_done = []
    xn_free = [None, None]
    hT_free = [None, None]
    t_w = {}
    for g in range(8):
        b = g // 4
        t_xn = layernorm(g, x, t_x[g], xn_free[g % 2])
        t_h = []
        for dc in range(2):
            k = ring.take()

            def tr(e, dc=dc, k=k, g=g):
                for i in range(4):
                    mm = e.transpose(PS[:, k, i * P:i * P + P], xn[:, g % 2, i, dc * P:dc * P + P], ident[:, :])
                return mm
            t = T(tr, t_xn, t_id, rel[k])
            t = A(lambda e, dc=dc, k=k, b=b: e.activation(hT[:, dc, :], PS[:, k, :], ACT.Identity,
                                                          bias=modc[:, 0, dc, b:b + 1], scale=modc[:, 1, dc, b:b + 1]),
                  t, t_modc, hT_free[dc])
            rel[k] = [t]
            t_h.append(t)
        xn_free[g % 2] = t_h[1]
        cols = slice(g * 512, g * 512 + 512)
        for oc in range(2):
            k = ring.take()

            def proj(e, oc=oc, k=k):
                for dc in range(2):
                    mm = e.matmul(PS[:, k, :], wqkv[:, dc, oc * P:oc * P + P], hT[:, dc, :], start=(dc == 0), stop=(dc == 1))
                return mm
            tm = T(proj, t_h, t_wq, rel[k])
            ta = A(lambda e, oc=oc, k=k, b=b, g=g, cols=cols: e.activation(
                w2T[:, oc, cols], PS[:, k, :], ACT.Square, accum_out=ssq[:, oc, b, g % 4:g % 4 + 1]), tm)
            tv = V(lambda e, oc=oc, k=k, cols=cols: e.tensor_copy(wT[:, oc, cols], PS[:, k, :]), ta)
            rel[k] = [tv]
        hT_free = [tm, tm]
        t_w[b] = tv

    t_xp = {}
    for b in range(NB):
        t_xp[b] = G(lambda e, b=b: e.tensor_tensor(x[:, b * NT:b * NT + NT, :], x[:, b * NT:b * NT + NT, :],
                                                   bc(gab[:, b, :], NT, 1), ALU.add), t_gab, t_w[b], t_x, t_xp.get(b - 1))

    t_mt = V(lambda e: e.tensor_tensor(mask[:, :, :], mask[:, :, :], bc(tempB[:, :], 2, 1), ALU.mult), t_mk, t_tp)
    t_piT = [None, None]
    t_piE = t_junk = None
    lg_free = le_free = None
    t_x1 = []
    for b in range(NB):
        t = V(lambda e, b=b: e.tensor_reduce(n2[:, :, b], ssq[:, :, b, :], AX, ALU.add), t_w[b])
        t = V(lambda e, b=b: e.tensor_scalar(n2[:, :, b], n2[:, :, b], 1e-24, None, ALU.max), t)
        t = V(lambda e, b=b: e.reciprocal(n2[:, :, b], n2[:, :, b]), t)
        for oc in range(2):
            t_lb = V(lambda e, b=b, oc=oc: e.tensor_scalar(LB[:, oc, b, :], mask[:, oc, :], n2[:, oc, b:b + 1], None,
                                                           ALU.mult), t, t_mt)
        k = ring.take()
        pl = PS[:, k, 0:256].rearrange("p (t h) -> p t h", h=16)

        def logits(e, b=b, pl=pl):
            for i in range(NT):
                for oc in range(2):
                    mm = e.matmul(pl[:, i, :], w2T[:, oc, b * S + i * P:b * S + i * P + P], LB[:, oc, b, :],
                                  start=(oc == 0), stop=(oc == 1))
            return mm
        tl = T(logits, t_lb, rel[k])
        t = V(lambda e, b=b, pl=pl: e.tensor_reduce(lm[:, b, :, 0], pl, AX, ALU.max), tl)
        t = V(lambda e, b=b, pl=pl: e.tensor_tensor(lg[:, :, :], pl, bc(lm[:, b, :, 0], 16, 2), ALU.subtract), t, lg_free)
        rel[k] = [t]
        t = A(lambda e: e.activation(le[:, :, :], lg[:, :, :], ACT.Exp), t, le_free)
        lg_free = t
        ts = V(lambda e, b=b: e.tensor_reduce(lm[:, b, :, 1], le[:, :, :], AX, ALU.add), t)
        ts = V(lambda e, b=b: e.reciprocal(lm[:, b, :, 2], lm[:, b, :, 1]), ts)
        t_pi = V(lambda e, b=b: e.tensor_tensor(le[:, :, :], le[:, :, :], bc(lm[:, b, :, 2], 16, 2), ALU.mult), ts)
        t_d = []
        for g in range(4):
            cols = slice(b * S + g * 512, b * S + g * 512 + 512)
            t_pe = A(lambda e, g=g: e.activation(
                piE[:, :, :].rearrange("p t (h d) -> p (t h) d", d=16),
                bc(le[:, 4 * g:4 * g + 4, :].rearrange("p t h -> p (t h)"), 16, 2), ACT.Copy), t_pi, t_piE)
            for oc in range(2):
                k = ring.take()

                def tr(e, oc=oc, k=k):
                    for i in range(4):
                        mm = e.transpose(PS[:, k, i * P:i * P + P], piE[:, i, oc * P:oc * P + P], ident[:, :])
                    return mm
                t = T(tr, t_pe, rel[k])
                t_piE = t
                t = A(lambda e, oc=oc, k=k, b=b, g=g: e.activation(piT[:, oc, :], PS[:, k, :], ACT.Copy,
                                                                   accum_out=piS[:, oc, b, g:g + 1]), t, t_piT[oc])
                rel[k] = [t]
                t1 = V(lambda e, oc=oc, b=b, g=g, cols=cols: e.tensor_tensor_reduce(
                    out=junk[:, :], in0=piT[:, oc, :], in1=w2T[:, oc, cols], scale=1.0, scalar=0.0,
                    op0=ALU.mult, op1=ALU.add, accum_out=dS[:, oc, b, g:g + 1]), t, t_junk)
                t_junk = t1
                t_piT[oc] = V(lambda e, oc=oc, cols=cols: e.tensor_tensor(wT[:, oc, cols], wT[:, oc, cols], piT[:, oc, :],
                                                                          ALU.mult), t, t_w[b])
                t_d += [t, t1, t_piT[oc]]
        le_free = t_pe
        t1 = V(lambda e, b=b: e.tensor_reduce(cf[:, :, b, 0], piS[:, :, b, :], AX, ALU.add), t_d)
        t2 = V(lambda e, b=b: e.tensor_reduce(cf[:, :, b, 1], dS[:, :, b, :], AX, ALU.add), t_d)
        t = V(lambda e, b=b: e.tensor_scalar_add(cf[:, :, b, 0], cf[:, :, b, 0], 1e-8), t1)
        t = V(lambda e, b=b: e.reciprocal(cf[:, :, b, 0], cf[:, :, b, 0]), t)
        t = V(lambda e, b=b: e.tensor_tensor(cf[:, :, b, 1], cf[:, :, b, 1], cf[:, :, b, 0], ALU.mult), t, t2)
        t = V(lambda e, b=b: e.tensor_scalar_add(cf[:, :, b, 1], cf[:, :, b, 1], 1.0), t)
        t = V(lambda e, b=b: e.reciprocal(cf[:, :, b, 2], cf[:, :, b, 1]), t)
        for oc in range(2):
            t_ws = V(lambda e, b=b, oc=oc: e.tensor_scalar(wouts[:, oc, b, :], wout[:, oc, :], cf[:, oc, b, 2:3], -1.0,
                                                           ALU.mult, ALU.mult), t, t_wo)
        for oc in range(2):
            t_wg = V(lambda e, b=b, oc=oc: e.tensor_tensor(wouts[:, oc, b, :], wouts[:, oc, b, :], rows[:, b, 0, :],
                                                           ALU.mult), t_ws, t_rows)
        for i in range(NT // 2):
            k = ring.take()

            def oproj(e, b=b, i=i, k=k):
                for j in range(2):
                    n = b * S + (2 * i + j) * P
                    for oc in range(2):
                        mm = e.matmul(PS[:, k, j * D:j * D + D], wT[:, oc, n:n + P], wouts[:, oc, b, :],
                                      start=(oc == 0), stop=(oc == 1))
                return mm
            t = T(oproj, t_wg, t_d, rel[k])
            n = b * NT + 2 * i
            t = V(lambda e, n=n, k=k: e.tensor_tensor(x[:, n:n + 2, :], PS[:, k, :].rearrange("p (t d) -> p t d", d=D),
                                                      x[:, n:n + 2, :], ALU.add), t, t_xp[b])
            rel[k] = [t]
            t_x1.append(t)
    t_p1 = [t_x1[-1], t_piT[1], t_pe, t]
    c1.close()

    t_sp = [dma("sp", tokens(x1d, b), x[:, b * NT:b * NT + NT, :], t_x1[8 * b + 7]) for b in range(NB)]
    t_h2 = []
    sq_prev = None
    for g in range(8):
        b = g // 4
        ts = slice(4 * g, 4 * g + 4)
        t_xn = layernorm(g, x, t_x1[2 * g + 1], xn_free[g % 2])
        t = V(lambda e, g=g, b=b: e.tensor_tensor(xn[:, g % 2, :, :], xn[:, g % 2, :, :], bc(rows[:, b, 2, :], 4, 1),
                                                  ALU.mult), t_xn)
        t = V(lambda e, g=g, b=b, ts=ts: e.tensor_tensor(X2[:, ts, :], xn[:, g % 2, :, :], bc(rows[:, b, 1, :], 4, 1),
                                                         ALU.add), t)
        for i in range(4):
            n = 4 * g + i
            sq = A(lambda e, g=g, i=i, n=n: e.activation(xn[:, g % 2, i, :], X2[:, n, :], ACT.Square,
                                                         accum_out=ssq2[:, n:n + 1]), t)
        xn_free[g % 2] = sq
        t = A(lambda e, ts=ts: e.activation(rs2[:, ts], ssq2[:, ts], ACT.Sqrt, bias=eps[:, 1:2], scale=1.0 / D), sq)
        t_h2.append(V(lambda e, ts=ts: e.reciprocal(rs2[:, ts], rs2[:, ts]), t))
    t_p2 = [t_h2[-1], sq, t_sp]
    cX.close()

    c3 = ExitStack()
    cW = ExitStack()
    nxT = sb("nxT", [P, 2, S], c=cW)
    QA2 = sb("QA2", [P, S], F32R, c=cW)
    QB2 = sb("QB2", [P, S], F32R, c=cW)
    QA01 = sb("QA", [P, 2, S], F32R, c=c3)
    QB01 = sb("QB", [P, 2, S], F32R, c=c3)
    QA = [QA01[:, 0, :], QA01[:, 1, :], QA2[:, :]]
    QB = [QB01[:, 0, :], QB01[:, 1, :], QB2[:, :]]
    KA = sb("KA", [P, NB, S], F32R, c=c3)
    KB = sb("KB", [P, NB, S], F32R, c=c3)
    ktm = xT[:, :, :, :].rearrange("p a c n -> p (a c n)")
    VH = sb("VH", [P, NB * NT, 65], F32R, c=c3)
    VL = sb("VL", [P, NB * NT, 65], F32R, c=c3)
    PT = sb("PT", [P, 2, 1024], c=c3)
    PH = sb("PH", [P, 3, 1024], F32R, c=c3)
    PL = sb("PL", [P, 3, 1024], F32R, c=c3)
    O = sb("O", [65, S], c=c3)
    mx = sb("mx", [P, 2, 8, 4], c=c3)
    m16 = sb("m16", [P, 2, 8], c=c3)
    mT = sb("mT", [8, 2, P], F32R, c=c3)
    rz = sb("rz", [P, 2, 1], c=c3)
    wk = sb("wk", [P, 2, P], c=c3)
    wv = sb("wv", [P, 2, 64], c=c3)
    wqp = sb("wqp", [P, 2, D], c=c3)
    woa = sb("woa", [65, 4, 257], c=c3)
    qaf = [q.bitcast(F32) for q in QA]
    vhf, phf = VH[:, :, :].bitcast(F32), PH[:, :, :].bitcast(F32)

    t_wk = dma("sp", wk[:, :, :], I["wkcT2"].rearrange("(c p) n -> p c n", p=P), t_p1, t_p2)
    t_wv = dma("sp", wv[:, :, :], I["wvcT"].rearrange("(c p) n -> p c n", p=P), t_p1, t_p2)
    t_wqp = dma("sp", wqp[:, :, :], I["wqT"].rearrange("(c p) n -> p c n", p=P), t_p1, t_p2)
    t_woa = dma("sp", woa[:, :, :], I["woA"], t_p1, t_p2)
    t = G(lambda e: e.memset(KB[64:65, :, :].bitcast(F32), -1.0), t_p1, t_p2)
    t = G(lambda e: e.memset(VH[:, :, 64:65].bitcast(F32), 1.0), t)
    t_one = G(lambda e: e.memset(VL[:, :, 64:65].bitcast(F32), 0.0), t)

    st_nx = [None, None]
    t_nxT = {}
    nxT_free = {0: [t_p1, t_p2], 1: []}
    t_k, t_v, t_q = {}, {}, {}
    q_free = [[], [], []]
    ktm_free = [None]
    cnt = [0]

    def staged(*stages):
        return [lambda i=i, n=n, f=f: f(i - n) for i in range(NT + len(stages) - 1) for n, f in enumerate(stages)
                if 0 <= i - n < NT]

    def nx_jobs(b):
        held = {}

        def scale(i):
            n = b * NT + i
            s = cnt[0] % 2
            cnt[0] += 1
            if b:
                nxT_free[1] = [t_last_q[0]]
            held[i] = s, V(lambda e: e.tensor_scalar(nx[:, s, :], X2[:, n, :], rs2[:, n:n + 1], None, ALU.mult),
                           t_h2[n // 4], st_nx[s], t_p1, t_p2)

        def job(i):
            s, t = held[i]
            k = ring.take()

            def tr(e):
                for dc in range(2):
                    mm = e.transpose(PS[:, k, dc * P:dc * P + P], nx[:, s, dc * P:dc * P + P], ident[:, :])
                return mm
            t = T(tr, t, rel[k])
            st_nx[s] = t
            for dc in range(2):
                t2 = A(lambda e, dc=dc: e.activation(nxT[:, dc, i * P:i * P + P], PS[:, k, dc * P:dc * P + P], ACT.Copy,
                                                     scale=g1c[:, dc:dc + 1]), t, t_g1, nxT_free[b])
            rel[k] = [t2]
            t_nxT[b, i] = t2
        return staged(scale, job)

    def k_jobs(b):
        def job(c):
            k = ring.take()

            def mmk(e):
                for dc in range(2):
                    mm = e.matmul(PS[:, k, :], wk[:, dc, :], nxT[:, dc, c * 512:c * 512 + 512], start=(dc == 0), stop=(dc == 1))
                return mm
            t = T(mmk, t_wk, t_nxT[b, 4 * c + 3], rel[k])
            cols = slice(c * 512, c * 512 + 512)
            ta = A(lambda e: e.activation(KA[0:64, b, cols], PS[0:64, k, :], ACT.Copy), t, t_p1, t_p2)
            ta = A(lambda e: e.activation(KB[0:64, b, cols], PS[0:64, k, :], ACT.Copy), t)
            th = V(lambda e: e.tensor_copy(ktm[64:128, :].bitcast(F32R), PS[64:128, k, :]), ta, ktm_free[0], t_p1, t_p2)
            tv = V(lambda e: e.tensor_tensor(KA[64:128, b, cols], PS[64:128, k, :], ktm[64:128, :], ALU.subtract), th)
            ktm_free[0] = tv
            rel[k] = [tv]
            t_k[b, c] = tv
        return [lambda c=c: job(c) for c in range(4)]

    def v_jobs(b):
        def job(c):
            k = ring.take()

            def mmv(e):
                for i in range(4):
                    for dc in range(2):
                        mm = e.matmul(PS[:, k, i * 64:i * 64 + 64], nxT[:, dc, (4 * c + i) * P:(4 * c + i + 1) * P],
                                      wv[:, dc, :], start=(dc == 0), stop=(dc == 1))
                return mm
            t = T(mmv, t_wv, t_nxT[b, 4 * c + 3], rel[k])
            n = b * NT + 4 * c
            pv = PS[:, k, 0:256].rearrange("p (t d) -> p t d", d=64)
            t = A(lambda e: e.activation(VH[:, n:n + 4, 0:64], pv, ACT.Copy), t, t_one)
            t = V(lambda e: e.tensor_tensor(VL[:, n:n + 4, 0:64], pv, vhf[:, n:n + 4, 0:64], ALU.subtract), t)
            rel[k] = [t]
            t_v[b, c] = t
        return [lambda c=c: job(c) for c in range(4)]

    def q_jobs(b, pair):
        def job(c):
            k = ring.take()

            def mmq(e):
                for dc in range(2):
                    mm = e.matmul(PS[:, k, :], wqp[:, dc, pair * P:pair * P + P], nxT[:, dc, c * 512:c * 512 + 512],
                                  start=(dc == 0), stop=(dc == 1))
                return mm
            t = T(mmq, t_wqp, t_nxT[b, 4 * c + 3], rel[k])
            t_last_q[b] = t
            cols = slice(c * 512, c * 512 + 512)
            for j in range(2):
                s, r = (4 * b + 2 * pair + j) % 3, slice(64 * j, 64 * j + 64)
                ta = A(lambda e, s=s, r=r: e.activation(QA[s][0:64, cols], PS[r, k, :], ACT.Copy), t, q_free[s], t_p1, t_p2)
                ta = A(lambda e, s=s, r=r: e.activation(QA[s][64:128, cols], PS[r, k, :], ACT.Copy), t)
                tv = V(lambda e, s=s, r=r: e.tensor_tensor(QB[s][0:64, cols], PS[r, k, :], qaf[s][r, cols], ALU.subtract),
                       ta, q_free[s])
                t_q[b, 2 * pair + j, c] = tv
            rel[k] = [tv]
        return [lambda c=c: job(c) for c in range(4)]

    t_last_q = {}
    MJ = {}
    mx_free = [None, None]
    m_free = [None, None]
    t_m = {}

    def max_jobs(bh, half):
        b, h, qs = bh // 4, bh % 4, bh % 3
        s = (2 * bh + half) % 2
        last = []

        def job(i, c):
            k = ring.take()
            t = T(lambda e: e.matmul(PS[:, k, :], QA[qs][:, i * P:i * P + P], KA[:, b, c * 512:c * 512 + 512],
                                     start=True, stop=True), t_q[b, h, i // 4], t_k[b, c], rel[k])
            t = V(lambda e: e.tensor_reduce(mx[:, s, i % 8, c:c + 1], PS[:, k, :], AX, ALU.max), t, mx_free[s], t_p1, t_p2)
            rel[k] = [t]
            last[:] = [t]

        def rest():
            pass

        def close1():
            mx_free[s] = V(lambda e: e.tensor_reduce(m16[:, s, :], mx[:, s, :, :], AX, ALU.max), last, m_free[s])

        def close2():
            k = ring.take()
            t = T(lambda e: e.transpose(PS[0:8, k, 0:P], m16[:, s, :], ident[:, :]), mx_free[s], rel[k])
            t = V(lambda e: e.tensor_copy(mT[:, s, :], PS[0:8, k, 0:P]), t, m_free[s], t_p1, t_p2)
            rel[k] = [t]
            t_m[bh, half] = dma("sp", QB[qs][64:65, half * 1024:half * 1024 + 1024].bitcast(F32),
                                mT[:, s, :].bitcast(F32), t, q_free[qs])
            m_free[s] = t_m[bh, half]
        jobs = [lambda i=i, c=c: job(i, c) for i in range(8 * half, 8 * half + 8) for c in range(4)]
        return jobs + [close1, rest, rest, close2]

    O_free = [t_p1 + t_p2, []]
    t_O = {}
    rz_free = [None, None]
    t_X2 = {}

    def proj_jobs(bh):
        b, h = bh // 4, bh % 4

        def job(i):
            k = ring.take()
            s = i % 2
            n = b * NT + i
            t = T(lambda e: e.matmul(PS[:, k, 0:257], O[0:65, i * P:i * P + P], woa[0:65, h, :], start=True, stop=True),
                  t_O[bh, i // 8], t_woa, rel[k])
            O_free[i // 8] = [t]
            t = V(lambda e: e.reciprocal(rz[:, s, :], PS[:, k, 256:257]), t, rz_free[s], t_p1, t_p2)
            t = V(lambda e: e.scalar_tensor_tensor(X2[:, n, :], PS[:, k, 0:256], rz[:, s, :], X2[:, n, :],
                                                   ALU.mult, ALU.add), t, t_X2.get(n))
            rz_free[s] = t
            t_X2[n] = t
            rel[k] = [t]
        return [lambda i=i: job(i) for i in range(NT)]

    SB = [(0, 1), (2, 3)]
    pt_free, ph_free, pl_free = [None] * 2, [None] * 3, [None] * 3
    state = {}
    NSTEP = 32
    NMJ = 36

    def qk(gs):
        bh, i = divmod(gs, NSTEP)
        b, h, qs = bh // 4, bh % 4, bh % 3
        qc, kc = divmod(i, 16)
        bk = SB[gs % 2]

        def f(e):
            for n in range(2):
                q0 = qc * 1024 + n * 512
                e.matmul(PS[:, bk[n], :], KA[:, b, kc * P:kc * P + P], QA[qs][:, q0:q0 + 512], start=True, stop=False)
            for n in range(2):
                q0 = qc * 1024 + n * 512
                mm = e.matmul(PS[:, bk[n], :], KB[0:65, b, kc * P:kc * P + P], QB[qs][0:65, q0:q0 + 512],
                              start=False, stop=True)
            return mm
        t = T(f, t_m[bh, qc], [t_q[b, h, 2 * qc + c] for c in range(2)], t_k[b, kc // 4], t_one, rel[bk[0]], rel[bk[1]])
        if i == NSTEP - 1:
            q_free[qs] = [t]
        p, r = gs % 2, gs % 3
        t = A(lambda e: e.activation(PT[:, p, :], PS[:, bk[0]:bk[0] + 2, :].rearrange("p a n -> p (a n)"), ACT.Exp,
                                     scale=0.125), t, pt_free[p], t_p1, t_p2)
        rel[bk[0]], rel[bk[1]] = [t], [t]
        th = A(lambda e: e.activation(PH[:, r, :], PT[:, p, :], ACT.Copy), t, ph_free[r], t_p1, t_p2)
        state[gs] = (t, th)
        if gs % POOL_EVERY == POOL_EVERY - 1:
            low(G, gs)

    def low(put, gs):
        p, r = gs % 2, gs % 3
        t, th = state[gs]
        pt_free[p] = put(lambda e: e.tensor_tensor(PL[:, r, :], PT[:, p, :], phf[:, r, :], ALU.subtract), th, t, pl_free[r],
                         t_p1, t_p2)
        state[gs] = (th, pt_free[p])

    def av(gs, n):
        bh, i = divmod(gs, NSTEP)
        b = bh // 4
        qc, kc = divmod(i, 16)
        th, tl = state[gs]
        r = gs % 3
        c = slice(n * 512, n * 512 + 512)

        def f(e):
            e.matmul(PS[0:65, 4 + n, :], VH[:, b * NT + kc, :], PH[:, r, c], start=(kc == 0), stop=False)
            e.matmul(PS[0:65, 4 + n, :], VL[:, b * NT + kc, :], PH[:, r, c], start=False, stop=False)
            return e.matmul(PS[0:65, 4 + n, :], VH[:, b * NT + kc, :], PL[:, r, c], start=False, stop=(kc == 15))
        t = T(f, th, tl, t_v[b, kc // 4], rel[4 + n] if kc == 0 else None)
        if n == 1:
            ph_free[r] = pl_free[r] = t
        if kc == 15:
            q0 = qc * 1024 + n * 512
            t = A(lambda e: e.activation(O[:, q0:q0 + 512], PS[0:65, 4 + n, :], ACT.Copy), t, O_free[qc])
            t_O[bh, qc] = t
            rel[4 + n] = [t]

    def spread(jobs, a, b):
        return [(a + (b - a) * i / len(jobs), j) for i, j in enumerate(jobs)]

    def main(bh, jobs):
        jobs = sorted(jobs, key=lambda x: x[0])
        for i in range(NSTEP):
            gs = bh * NSTEP + i
            for part in range(3):
                if part == 0 and gs + 1 < 8 * NSTEP:
                    while i == NSTEP - 1 and jobs:
                        jobs.pop(0)[1]()
                    qk(gs + 1)
                elif part == 1:
                    if gs % POOL_EVERY != POOL_EVERY - 1:
                        low(V, gs)
                if part and gs >= 1:
                    av(gs - 1, part - 1)
                while jobs and jobs[0][0] <= 3 * i + part:
                    jobs.pop(0)[1]()

    c_z = pr.counter()
    for b in range(NB):
        zv = xbuf[b].rearrange("(n p a) d -> n p a d", p=P, a=3)
        for n in range(NTI // 3):
            t_zf = dma("sp", zv[n], bc(zero[:, :], 3, 1), t_z, t_p2, on=c_z)

    t_rs = {}
    t_rl = {}
    t_sc = {}
    t_gate = {}
    r_free = [None]
    sqt = [None]
    xT_free = [None, None]

    def b8(ap):
        return bc(ap, NE, 2)

    def norm_jobs(b):
        def job(i):
            n = b * NT + i
            s = cnt[0] % 2
            cnt[0] += 1
            sqt[0] = A(lambda e: e.activation(nx[:, s, :], X2[:, n, :], ACT.Square, accum_out=ssq2[:, n:n + 1]),
                       t_X2[n], st_nx[s], sqt[0])
            st_nx[s] = sqt[0]

        def close():
            ts = slice(b * NT, b * NT + NT)
            t = A(lambda e: e.activation(rs2[:, ts], ssq2[:, ts], ACT.Sqrt, bias=eps[:, 1:2], scale=1.0 / D), sqt[0],
                  (pr.sem["dve"], pr.n["dve"]))
            t_rs[b] = V(lambda e: e.reciprocal(rs2[:, ts], rs2[:, ts]), t)
        return [lambda i=i: job(i) for i in range(NT)] + [close]

    def rlog_jobs(b):
        held = {}

        def scale(i):
            n = b * NT + i
            s = cnt[0] % 2
            cnt[0] += 1
            held[i] = s, V(lambda e: e.tensor_scalar(nx[:, s, :], X2[:, n, :], rs2[:, n:n + 1], None, ALU.mult), t_rs[b],
                           st_nx[s])

        def first(i):
            s, t = held[i]
            k = ring.take()

            def tr(e):
                for dc in range(2):
                    mm = e.transpose(PS[:, k, dc * P:dc * P + P], nx[:, s, dc * P:dc * P + P], ident[:, :])
                return mm
            t = T(tr, t, rel[k])
            st_nx[s] = t
            t = A(lambda e: e.activation(xT[:, s, :, :], PS[:, k, 0:256].rearrange("p (c n) -> p c n", c=2), ACT.Copy),
                  t, xT_free[s], ktm_free[0])
            rel[k] = [t]
            held[i] = (s, t)

        def second(i):
            s, t = held[i]
            k = ring.take()

            def mm(e):
                for dc in range(2):
                    m = e.matmul(PS[:, k, 0:NE], xT[:, s, dc, :], wr[:, dc, :], start=(dc == 0), stop=(dc == 1))
                return m
            t = T(mm, t, t_wr, rel[k])
            xT_free[s] = t
            t_rl[b] = V(lambda e: e.tensor_tensor(r_l[:, i, :], PS[:, k, 0:NE], ebB[:, :], ALU.add), t, t_eb, r_free[0])
            rel[k] = [t_rl[b]]

        return staged(scale, first, second)

    def route_jobs(b):
        held = {}
        return [lambda: choose(b, held), lambda: None, lambda: None, lambda: place(b, held)]

    def choose(b, held):
        t = V(lambda e: e.tensor_reduce(rm[:, 0, :], r_l[:, :, :], AX, ALU.max), t_rl[b])
        t = V(lambda e: e.tensor_tensor(r_l[:, :, :], r_l[:, :, :], b8(rm[:, 0, :]), ALU.subtract), t)
        t = A(lambda e: e.activation(r_q[:, :, :], r_l[:, :, :], ACT.Exp), t)
        t = V(lambda e: e.tensor_reduce(rm[:, 1, :], r_q[:, :, :], AX, ALU.add), t)
        t = V(lambda e: e.reciprocal(rm[:, 1, :], rm[:, 1, :]), t)
        t = V(lambda e: e.tensor_tensor(r_q[:, :, :], r_q[:, :, :], b8(rm[:, 1, :]), ALU.mult), t)
        for r, (oh, col) in enumerate(((oh1, 2), (oh2, 3))):
            t = V(lambda e, col=col: e.tensor_reduce(rm[:, col, :], r_q[:, :, :], AX, ALU.max), t)
            t = V(lambda e, oh=oh, col=col: e.tensor_tensor(oh[:, :, :], r_q[:, :, :], b8(rm[:, col, :]), ALU.is_equal), t)
            t = V(lambda e, oh=oh: e.tensor_tensor(oh[:, :, :], oh[:, :, :], bc(pri[:, :], NT, 1), ALU.mult), t, t_pri)
            t = V(lambda e, oh=oh: e.tensor_reduce(rm[:, 4, :], oh[:, :, :], AX, ALU.max), t)
            t = V(lambda e, oh=oh: e.tensor_tensor(oh[:, :, :], oh[:, :, :], b8(rm[:, 4, :]), ALU.is_equal), t)
            if r == 0:
                t = V(lambda e: e.scalar_tensor_tensor(r_q[:, :, :], oh1[:, :, :], -4.0, r_q[:, :, :], ALU.mult, ALU.add), t)
        tm = V(lambda e: e.tensor_tensor(r_M[:, :, :], oh1[:, :, :].rearrange("p t e -> p e t"),
                                         oh2[:, :, :].rearrange("p t e -> p e t"), ALU.add), t)
        t = V(lambda e: e.tensor_tensor(rm[:, 5, :], rm[:, 3, :], rm[:, 2, :], ALU.subtract), t)
        t = A(lambda e: e.activation(rm[:, 5, :], rm[:, 5, :], ACT.Exp), t)
        t = V(lambda e: e.tensor_scalar_add(rm[:, 6, :], rm[:, 5, :], 1.0), t)
        t = V(lambda e: e.reciprocal(gate[:, b, 0, :], rm[:, 6, :]), t)
        t_gate[b] = V(lambda e: e.tensor_tensor(gate[:, b, 1, :], rm[:, 5, :], gate[:, b, 0, :], ALU.mult), t)
        held["M"] = tm

    def place(b, held):
        k = ring.take()

        def count(e):
            mv_ = r_M[:, :, :].rearrange("p e t -> p (e t)")
            e.matmul(PS[:, k, 0:128], tri[:, 0, :], mv_, start=True, stop=True)
            return e.matmul(PS[:, k, 128:256], tri[:, 1, :], mv_, start=True, stop=True)
        tc = T(count, held["M"], t_tri, rel[k])
        pre = PS[:, k, 0:128].rearrange("p (e t) -> p e t", t=NT)
        tot = PS[:, k, 128:256].rearrange("p (e t) -> p e t", t=NT)
        t = V(lambda e: e.tensor_copy(r_s[:, :, :], tot), tc)
        tn = V(lambda e: e.tensor_reduce(r_e[:, 0, :], r_s[:, :, :], AX, ALU.add), t)
        t1 = V(lambda e: e.memset(r_e[:, 5, :], 1.0), t)
        t1 = V(lambda e: e.memset(r_c[:, :, :], 1.0), t1)
        t1 = V(lambda e: e.tensor_tensor_scan(r_c[:, :, :].rearrange("p e t -> p (e t)"),
                                              r_c[:, :, :].rearrange("p e t -> p (e t)"),
                                              r_s[:, :, :].rearrange("p e t -> p (e t)"), 0.0, ALU.mult, ALU.add), t1)
        t1 = V(lambda e: e.tensor_tensor(r_c[:, :, :], r_c[:, :, :], r_s[:, :, :], ALU.subtract), t1)
        t1 = V(lambda e: e.tensor_tensor(r_c[:, :, :], r_c[:, :, :], pre, ALU.add), t1)
        rel[k] = [t1]
        t = V(lambda e: e.tensor_scalar_add(r_i[:, :], r_e[:, 0, :], 127.0), tn)
        t = V(lambda e: e.tensor_scalar(r_i[:, :], r_i[:, :], 7, 7, ALU.arith_shift_right, ALU.logical_shift_left), t)
        t = V(lambda e: e.tensor_copy(r_e[:, 1, :], r_i[:, :]), t)
        t = V(lambda e: e.tensor_tensor_scan(r_e[:, 2, :], r_e[:, 5, :], r_e[:, 1, :], 0.0, ALU.mult, ALU.add), t, t1)
        te = t
        t = V(lambda e: e.tensor_tensor(r_e[:, 3, :], r_e[:, 1, :], r_e[:, 0, :], ALU.subtract), t)
        t = V(lambda e: e.tensor_tensor_scan(r_e[:, 4, :], r_e[:, 5, :], r_e[:, 3, :], 0.0, ALU.mult, ALU.add), t)
        t = V(lambda e: e.tensor_tensor(r_e[:, 4, :], r_e[:, 4, :], r_e[:, 3, :], ALU.subtract), t)
        t = V(lambda e: e.tensor_tensor(r_c[:, :, :], r_c[:, :, :], bc(r_e[:, 4, :], NT, 2), ALU.add), t, t1)
        for j, oh in enumerate((oh1, oh2)):
            t2 = V(lambda e, oh=oh: e.tensor_tensor(r_M[:, :, :], oh[:, :, :].rearrange("p t e -> p e t"), r_c[:, :, :],
                                                    ALU.mult), t, tc)
            t2 = V(lambda e, j=j: e.tensor_reduce(rm[:, 7, :], r_M[:, :, :].rearrange("p e t -> p t e"), AX, ALU.add), t2)
            t = V(lambda e, j=j: e.tensor_copy(slot[:, b, j, :], rm[:, 7, :]), t2)
        t_slot[b] = t
        t = V(lambda e: e.tensor_tensor(r_t[:, :, :], bc(r_e[0:1, 2, :], NTI, 1), bc(thr[:, :], NE, 2), ALU.is_le), te, t_thr)
        t = V(lambda e: e.tensor_reduce(r_v[:, :], r_t[:, :, :], AX, ALU.add), t)
        t_texp[b] = V(lambda e: e.tensor_scalar(texp[:, b, :], r_v[:, :], float(NE - 1), None, ALU.min), t)
        r_free[0] = t_texp[b]

    t_slot, t_texp = {}, {}
    c_sc = [pr.counter() for _ in range(NB)]

    def scatter_jobs(b):
        def job(i):
            n = b * NT + i
            s = cnt[0] % 2
            cnt[0] += 1
            t = V(lambda e: e.tensor_scalar(nx[:, s, :], X2[:, n, :], rs2[:, n:n + 1], None, ALU.mult), t_rs[b], st_nx[s])
            for j in range(2):
                on = c_nx[s]
                t2 = pr.start("pool", lambda e, j=j: e.indirect_dma_start(
                    out=xbuf[b], out_offset=bass.IndirectOffsetOnAxis(ap=slot[:, b, j, i:i + 1], axis=0),
                    in_=nx[:, s, :], in_offset=None), [t, t_slot[b], t_zf], on)
            st_nx[s] = t2
            t_nxs[n] = t
            t_sc[b] = [(c[0], 16 * c[1]) for c in c_nx]
        return [lambda i=i: job(i) for i in range(NT)]

    t_nxs = {}
    c_nx = [pr.counter(), pr.counter()]

    wst = nxT[:, :, :].rearrange("p c n -> p (c n)")[:, 0:4 * 768].rearrange("p (s c n) -> p s c n", s=2, c=2)
    wsh = QA2[:, 0:2 * 768].rearrange("p (c n) -> p c n", c=2)
    wsl = QB2[:, 0:2 * 768].rearrange("p (c n) -> p c n", c=2)
    wd = I["wexp"].rearrange("e (c p) n -> e p c n", p=P)
    c_w = [pr.counter(), pr.counter()]
    t_raw, t_wsp, f_wst = {}, {}, [[], []]
    order = [NE] + list(range(NE))

    def load_w(ex):
        s = order.index(ex) % 2
        t_raw[ex] = dma("sp", wst[:, s, :, :], wd[ex], f_wst[s], t_last_q[1], on=c_w[s])

    def split_w(ex, hi, lo, free):
        s = order.index(ex) % 2
        t_wsp[ex] = []

        def rows(dc):
            t = t_raw[ex]
            t1 = A(lambda e: e.activation(hi[:, dc, 0:512], wst[:, s, dc, 0:512], ACT.Copy, scale=g2c[:, dc:dc + 1]),
                   t, t_g2, free)
            t_wsp[ex].append(V(lambda e: e.scalar_tensor_tensor(
                lo[:, dc, 0:512], wst[:, s, dc, 0:512], g2c[:, dc:dc + 1], hi[:, dc, 0:512].bitcast(F32),
                ALU.mult, ALU.subtract), t1, free))

        def last():
            t1 = A(lambda e: e.activation(hi[:, :, 512:768], wst[:, s, :, 512:768], ACT.Copy), t_raw[ex], free)
            t_wsp[ex].append(V(lambda e: e.tensor_tensor(lo[:, :, 512:768], wst[:, s, :, 512:768],
                                                         hi[:, :, 512:768].bitcast(F32), ALU.subtract), t1, free))
            f_wst[s] = list(t_wsp[ex])
            nxt = order.index(ex) + 2
            if nxt < len(order):
                load_w(order[nxt])
        return [lambda: rows(0), lambda: rows(1), last]

    def shared_jobs():
        def loads():
            load_w(NE)
            load_w(0)
        return [loads] + [lambda: None] * 4 + split_w(NE, wsh, wsl, q_free[2])

    for j in nx_jobs(0) + k_jobs(0) + v_jobs(0) + q_jobs(0, 0) + max_jobs(0, 0):
        j()
    ring = Ring([6, 7])
    NXJ = nx_jobs(1)
    qk(0)
    for bh in range(8):
        b, h = bh // 4, bh % 4
        jobs = spread(max_jobs(0, 1), 0, 40) if bh == 0 else spread(proj_jobs(bh - 1), 4, 46)
        if h % 2:
            nb, npair = (b, 1) if h == 1 else (b + 1, 0)
            if nb < NB:
                jobs += spread(q_jobs(nb, npair), 0, 16)
        if bh == 1:
            jobs += spread([lambda j=j: NXJ[j]() for j in range(2 * NT)], 20, 92)
        if bh == 2:
            jobs += spread([lambda j=j, f=f: f(1)[j]() for f in (k_jobs, v_jobs) for j in range(4)], 0, 80)
        if bh == 4:
            jobs += spread(norm_jobs(0), 48, 92)
        if bh == 5:
            jobs += spread(rlog_jobs(0), 0, 92)
        if bh == 6:
            jobs += spread(shared_jobs(), 70, 92)
        if bh == 6:
            jobs += spread(route_jobs(0), 4, 16) + spread(scatter_jobs(0), 24, 84)
        if bh < 7:
            at = 40 if bh == 0 else 17 if h % 2 else 2
            mid = (at + 92) / 2
            jobs += spread([lambda j=j, bh=bh: MJ[bh + 1, 0][j]() for j in range(NMJ)], at, mid)
            jobs += spread([lambda j=j, bh=bh: MJ[bh + 1, 1][j]() for j in range(NMJ)], mid, 92)
            for hf in range(2):
                MJ[bh + 1, hf] = max_jobs(bh + 1, hf)
        main(bh, jobs)
    av(8 * NSTEP - 1, 0)
    av(8 * NSTEP - 1, 1)
    t_main = (pr.sem["pe"], pr.n["pe"])
    ring = Ring([6, 7, 0, 1, 2, 3, 4, 5])
    for j in proj_jobs(7):
        j()
    t_p3 = [t_main, t_X2[31], (pr.sem["pe"], pr.n["pe"]), (pr.sem["act"], pr.n["act"]), (pr.sem["dve"], pr.n["dve"])]
    c3.close()

    c4 = ExitStack()
    wh = sb("wh", [P, NE, 2, 768], F32R, c=c4)
    wl = sb("wl", [P, NE, 2, 768], F32R, c=c4)
    NX = 4
    NG = 4
    xg = sb("xg", [P, NX, D], c=c4)
    xh = sb("xh", [P, 3, 2, P], F32R, c=c4)
    xl = sb("xl", [P, 3, 2, P], F32R, c=c4)
    xhf = xh[:, :, :, :].bitcast(F32)
    sg = sb("sg", [P, 2, D], c=c4)
    hg = sb("hg", [P, 2, D], c=c4)
    hh = sb("hh", [P, 3, 2, P], F32R, c=c4)
    hl = sb("hl", [P, 3, 2, P], F32R, c=c4)
    hhf = hh[:, :, :, :].bitcast(F32)
    yo = sb("yo", [P, 3, D], c=c4)
    y12 = sb("y12", [P, NG, 2, D], c=c4)
    xo = nxT[:, 1, 1024:2048].rearrange("p (s d) -> p s d", d=D)

    def split_jobs(ex):
        return split_w(ex, wh[:, ex, :, :], wl[:, ex, :, :], t_p3)

    tiles = ([(None, i) for i in range(NT)] + [(0, i) for i in range(NTI)] + [(1, i) for i in range(NTI)]
             + [(None, NT + i) for i in range(NT)])
    NTL = len(tiles)
    tring, hring, yring = Ring([0, 1]), Ring([3, 4]), Ring([5, 6])
    ring = Ring([2, 7])
    c_x = [pr.counter() for _ in range(NX)]
    c_y = [pr.counter() for _ in range(3)]
    f_xg, f_x, f_sg, f_hg, f_h, f_yo = [t_p3] * NX, [t_p3] * 3, [t_p3] * 2, [t_p3] * 2, [t_p3] * 3, [t_p3] * 3
    d_xg, d_x, d_hg, d_h = {}, {}, {}, {}
    t_ys = {}
    t_yo = {0: [], 1: []}
    regs = {}

    def expert(s, e):
        return None if tiles[s][0] is None else regs[s]

    def fetch(s):
        g, i = tiles[s]
        q = s % NX
        if g is None:
            d_xg[s] = V(lambda e: e.tensor_scalar(xg[:, q, :], X2[:, i, :], rs2[:, i:i + 1], None, ALU.mult),
                        t_rs[i // NT], f_xg[q], t_p3)
        else:
            d_xg[s] = dma("sp", xg[:, q, :], xbuf[g][i * P:i * P + P, :], t_sc[g], t_zf, f_xg[q], t_p3, on=c_x[q])

    def split_x(s):
        q, r = s % NX, s % 3
        k = tring.take()

        def tr(e):
            for dc in range(2):
                mm = e.transpose(PS[:, k, dc * P:dc * P + P], xg[:, q, dc * P:dc * P + P], ident[:, :])
            return mm
        t = T(tr, d_xg[s], rel[k])
        f_xg[q] = t
        pv = PS[:, k, 0:256].rearrange("p (c n) -> p c n", c=2)
        ta = A(lambda e: e.activation(xh[:, r, :, :], pv, ACT.Copy), t, f_x[r])
        tv = V(lambda e: e.tensor_tensor(xl[:, r, :, :], pv, xhf[:, r, :, :], ALU.subtract), ta, f_x[r])
        rel[k] = [tv]
        d_x[s] = tv

    def up(s):
        r, q = s % 3, s % 2
        k = hring.take()
        g, i = tiles[s]
        if g is not None:
            def ld(e):
                regs[s] = e.value_load(texp[0:1, g, i:i + 1], min_val=0, max_val=NE - 1)
            pr.do("pe", ld, t_texp[g])

        def f(e):
            ex = expert(s, e)
            n = 0
            for dc in range(2):
                for w, a in ((0, xh), (0, xl), (1, xh)):
                    mm = e.matmul(PS[:, k, :], a[:, r, dc, :], wsel(w, ex, dc, 0, 512), start=(n == 0), stop=(n == 5))
                    n += 1
            return mm
        t = T(f, d_x[s], t_wsp[NE] if g is None else [t_wsp[ex] for ex in range(NE)], rel[k])
        f_x[r] = t
        ta = A(lambda e: e.activation(sg[:, q, :], PS[:, k, 0:256], ACT.Silu), t, f_sg[q])
        tv = V(lambda e: e.tensor_tensor(hg[:, q, :], PS[:, k, 256:512], sg[:, q, :], ALU.mult), ta, f_hg[q])
        f_sg[q] = tv
        rel[k] = [tv]
        d_hg[s] = tv

    def wsel(w, ex, dc, a, b):
        if ex is None:
            return (wsh, wsl)[w][:, dc, a:b]
        return (wh, wl)[w][:, bass.ds(ex, 1), dc, a:b].rearrange("p o n -> p (o n)")

    def split_h(s):
        q, r = s % 2, s % 3
        k = tring.take()

        def tr(e):
            for dc in range(2):
                mm = e.transpose(PS[:, k, dc * P:dc * P + P], hg[:, q, dc * P:dc * P + P], ident[:, :])
            return mm
        t = T(tr, d_hg[s], rel[k])
        f_hg[q] = t
        pv = PS[:, k, 0:256].rearrange("p (c n) -> p c n", c=2)
        ta = A(lambda e: e.activation(hh[:, r, :, :], pv, ACT.Copy), t, f_h[r])
        tv = V(lambda e: e.tensor_tensor(hl[:, r, :, :], pv, hhf[:, r, :, :], ALU.subtract), ta, f_h[r])
        rel[k] = [tv]
        d_h[s] = tv

    def down(s):
        g, i = tiles[s]
        r = s % 3
        k = yring.take()

        def f(e):
            ex = expert(s, e)
            n = 0
            for fc in range(2):
                for a, w in ((hh, 0), (hh, 1), (hl, 0)):
                    mm = e.matmul(PS[:, k, 0:256], a[:, r, fc, :], wsel(w, ex, fc, 512, 768), start=(n == 0), stop=(n == 5))
                    n += 1
            return mm
        t = T(f, d_h[s], rel[k])
        f_h[r] = t
        if g is None:
            t = V(lambda e: e.tensor_tensor(X2[:, i, :], PS[:, k, 0:256], X2[:, i, :], ALU.add), t, t_nxs[i], d_xg[s])
            t_X2[i] = t
        else:
            t = A(lambda e: e.activation(yo[:, r, :], PS[:, k, 0:256], ACT.Copy), t, f_yo[r])
            f_yo[r] = dma("act", ybuf[g][i * P:i * P + P, :], yo[:, r, :], t, on=c_y[r])
            t_yo[g] = [f_yo[x] for x in range(3)]
        rel[k] = [t]

    c_g = [pr.counter() for _ in range(NG)]
    c_xo = [pr.counter() for _ in range(NG)]
    f_g, f_xo = [t_p3] * NG, [t_p3] * NG
    d_xo = {}
    t_fin = []
    c_out = pr.counter()
    d_g = {}

    def gather(n):
        b, i, s = n // NT, n % NT, n % NG
        d_xo[n] = dma("sp", xo[:, s, :], tokens(x1d, b)[:, i, :], f_xo[s], t_sp, on=c_xo[s])
        for j in range(2):
            d_g[n] = pr.start("pool", lambda e, j=j: e.indirect_dma_start(
                out=y12[:, s, j, :], out_offset=None, in_=ybuf[b],
                in_offset=bass.IndirectOffsetOnAxis(ap=slot[:, b, j, i:i + 1], axis=0)),
                [t_yo[b], f_g[s], t_slot[b]], c_g[s])

    def finish(n):
        b, i, s = n // NT, n % NT, n % NG
        t = V(lambda e: e.scalar_tensor_tensor(X2[:, n, :], y12[:, s, 0, :], gate[:, b, 0, i:i + 1], X2[:, n, :],
                                               ALU.mult, ALU.add), d_g[n], t_gate[b], t_X2[n])
        t = V(lambda e: e.scalar_tensor_tensor(X2[:, n, :], y12[:, s, 1, :], gate[:, b, 1, i:i + 1], X2[:, n, :],
                                               ALU.mult, ALU.add), t)
        f_g[s] = t
        t = V(lambda e: e.tensor_tensor(X2[:, n, :], X2[:, n, :], gb[:, b, :], ALU.mult), t)
        t = V(lambda e: e.tensor_tensor(X2[:, n, :], X2[:, n, :], xo[:, s, :], ALU.add), t, d_xo[n])
        f_xo[s] = t
        t_fin.append(dma("sp", tokens(out, b)[:, i, :], X2[:, n, :], t, on=c_out))

    def combine_jobs(b):
        def job(i):
            if i < NT:
                gather(b * NT + i)
            if i >= NG - 1:
                finish(b * NT + i - NG + 1)
        return [lambda i=i: job(i) for i in range(NT + NG - 1)]

    side = [(-2, 2, lambda: [j for ex in range(NE) for j in split_jobs(ex)]),
            (12, 3, lambda: norm_jobs(1) + rlog_jobs(1) + route_jobs(1) + scatter_jobs(1)),
            (NT + NTI + 3, 1, lambda: combine_jobs(0)),
            (NT + 2 * NTI + 2, 1, lambda: combine_jobs(1))]
    todo = []
    for s in range(-2, NTL + 2):
        for at, n, make in side:
            if s == at:
                todo.append((n, make()))
        if s == -2:
            for q in range(2):
                fetch(q)
        if 0 <= s + 4 < NTL and s + 4 >= 2:
            fetch(s + 4)
        if 0 <= s + 2 < NTL:
            split_x(s + 2)
        if 0 <= s + 1 < NTL:
            up(s + 1)
        if 0 <= s < NTL:
            split_h(s)
        for n, jobs in todo:
            for _ in range(min(n, len(jobs))):
                jobs.pop(0)()
        if 0 <= s - 1 < NTL:
            down(s - 1)
    for n, jobs in todo:
        while jobs:
            jobs.pop(0)()
    pr.wait("sp", t_fin[-1])
    c4.close()
    cW.close()

    block = ctx.enter_context(nc.Block())

    @block.sync
    def _(eng):
        pr.play("sp", eng)

    @block.scalar
    def _(eng):
        pr.play("act", eng)

    @block.vector
    def _(eng):
        pr.play("dve", eng)

    @block.gpsimd
    def _(eng):
        pr.play("pool", eng)

    @block.tensor
    def _(eng):
        pr.play("pe", eng)


def kernel(**inputs):
    import numpy as np
    import concourse.bacc as bacc
    from concourse.bass_utils import run_bass_kernel_spmd

    a = {k: np.asarray(v) for k, v in inputs.items()}

    def tr(w):
        return np.ascontiguousarray(np.swapaxes(w, -1, -2))

    mask = np.zeros((D, 16), np.float32)
    mask[np.arange(D), np.arange(D) // 16] = 1.0
    woa = np.zeros((65, 4, 257), np.float32)
    woa[0:64, :, 0:256] = tr(a["L0_ffn_Wo"]).reshape(4, 64, D).transpose(1, 0, 2)
    woa[64, :, 256] = 1.0
    wexp = np.zeros((NE + 1, D, 768), np.float32)
    for i, (e, s) in enumerate((("eW1", "sW1"), ("eW3", "sW3"), ("eW2", "sW2"))):
        wexp[:NE, :, i * D:i * D + D] = tr(a["L0_ffn_" + e])
        wexp[NE, :, i * D:i * D + D] = tr(a["L0_ffn_" + s])
    wk = tr(a["L0_ffn_Wkc"])
    arrays = {
        "x": a["L0_attn_x"], "cT": tr(a["L0_c"]), "wmod": a["L0_wmod"],
        "wqkvT": tr(a["L0_attn_Wqkv"]), "woutT": tr(a["L0_attn_Wout"]), "bout": a["L0_attn_bout"],
        "temp": a["L0_attn_temp"], "g1": tr(a["L0_ffn_g1"].reshape(2, P)), "g2": tr(a["L0_ffn_g2"].reshape(2, P)),
        "wqT": tr(a["L0_ffn_Wq"]), "wkcT2": np.concatenate([wk, wk], axis=1), "wvcT": tr(a["L0_ffn_Wvc"]),
        "woA": woa, "wrT": tr(a["L0_ffn_Wr"]), "ebias": a["L0_ffn_expert_bias"], "wexp": wexp,
        "ident": np.eye(P, dtype=np.float32),
        "tri": np.stack([np.triu(np.ones((P, P), np.float32), 1), np.ones((P, P), np.float32)], axis=1),
        "thr": (np.arange(NTI) * P).astype(np.float32).reshape(1, NTI), "mask": mask,
        "pri": np.arange(NE, 0, -1).astype(np.float32),
    }
    nc = bacc.Bacc("TRN2", target_bir_lowering=False, num_devices=1)
    I, feeds = {}, {}
    for n, v in arrays.items():
        v = np.ascontiguousarray(v)
        feeds["in_" + n] = v
        I[n] = nc.dram_tensor("in_" + n, v.shape, mybir.dt.from_np(v.dtype), kind="ExternalInput").ap()
    out = nc.dram_tensor("out_0", (NB, S, D), F32, kind="ExternalOutput").ap()
    build(nc, I, out)
    r = run_bass_kernel_spmd(nc, [feeds], core_ids=[0])
    return r.results[0]["out_0"]
```

```python
from contextlib import ExitStack

import concourse.bass as bass
from concourse import mybir

ALU = mybir.AluOpType
ACT = mybir.ActivationFunctionType
F32 = mybir.dt.float32
F32R = mybir.dt.float32r
AX = mybir.AxisListType.X

P = 128
D = 256
NB = 2
NT = 16
S = 2048
NE = 8
EPS_LN = 1e-5
EPS_RMS = 1e-6
POOL_EVERY = 4
NNX = 3
NTI = 39


class Prog:

    def __init__(self, nc, ctx):
        self.nc, self.ctx = nc, ctx
        self.q = {k: [] for k in ("pe", "act", "dve", "pool", "sp")}
        self.sem = {k: ctx.enter_context(nc.semaphore("s_" + k)) for k in ("pe", "act", "dve", "pool")}
        self.n = {k: 0 for k in self.sem}
        self.dsem = 0

    def put(self, k, fn, waits):
        self.n[k] += 1
        self.q[k].append((flat(waits), fn, self.sem[k], 1))
        return (self.sem[k], self.n[k])

    def T(self, fn, *w):
        return self.put("pe", fn, w)

    def A(self, fn, *w):
        return self.put("act", fn, w)

    def V(self, fn, *w):
        return self.put("dve", fn, w)

    def G(self, fn, *w):
        return self.put("pool", fn, [w, (self.sem["pool"], self.n["pool"])])

    def counter(self):
        self.dsem += 1
        return [self.ctx.enter_context(self.nc.semaphore(f"d{self.dsem}")), 0]

    def dma(self, k, out, in_, *w, on=None):
        return self.start(k, lambda e: e.dma_start(out, in_), w, on)

    def start(self, k, fn, w, on=None):
        on = on or self.counter()
        on[1] += 1
        self.q[k].append((flat(w), fn, on[0], 16))
        return (on[0], 16 * on[1])

    def do(self, k, fn, *w):
        self.q[k].append((flat(w), fn, None, 0))

    def wait(self, k, *w):
        self.q[k].append((flat(w), None, None, 0))

    def play(self, k, eng):
        seen = {}
        for waits, fn, sem, inc in self.q[k]:
            for s, v in waits:
                if seen.get(s.num, 0) < v:
                    eng.wait_ge(s, v)
                    seen[s.num] = v
            if fn is not None:
                ins = fn(eng)
                if sem is not None:
                    ins.then_inc(sem, inc)


def flat(x):
    out = []
    for y in x:
        if y is None:
            continue
        if isinstance(y, list) or isinstance(y, tuple) and (not y or not isinstance(y[-1], int)):
            out += flat(y)
        else:
            out.append(y)
    return out


def bc(ap, n, axis):
    return ap.unsqueeze(axis).to_broadcast(list(ap.shape[:axis]) + [n] + list(ap.shape[axis:]))


def build(nc, I, out):
    with ExitStack() as ctx:
        _build(nc, ctx, I, out)


def _build(nc, ctx, I, out):
    pr = Prog(nc, ctx)
    T, A, V, G, dma = pr.T, pr.A, pr.V, pr.G, pr.dma

    def sb(name, shape, dt=F32, c=None):
        return (c or ctx).enter_context(nc.sbuf_tensor(name, shape, dt))

    PS = ctx.enter_context(nc.psum_tensor("PS", [P, 8, 512], F32))
    rel = {i: [] for i in range(8)}

    class Ring:
        def __init__(self, banks):
            self.banks, self.i, self.held = banks, 0, set()

        def take(self):
            while True:
                b = self.banks[self.i % len(self.banks)]
                self.i += 1
                if b not in self.held:
                    return b

        def hold(self, b):
            self.held.add(b)

        def free(self, b):
            self.held.discard(b)

    ident = sb("ident", [P, P])
    X2 = sb("X2", [P, NB * NT, D])
    gb = sb("gb", [P, NB, D])
    g1c = sb("g1c", [P, 2])
    g2c = sb("g2c", [P, 2])
    eps = sb("eps", [P, 2])
    ssq2 = sb("ssq2", [P, NB * NT])
    rs2 = sb("rs2", [P, NB * NT])
    x1d = nc.dram_tensor("x1_scratch", [NB, S, D], F32, kind="Internal").ap()

    tri = sb("tri", [P, 2, P])
    ebB = sb("ebB", [P, NE])
    pri = sb("pri", [P, NE])
    thr = sb("thr", [1, NTI])
    wr = sb("wr", [P, 2, NE])
    r_l = sb("r_l", [P, NT, NE])
    r_q = sb("r_q", [P, NT, NE])
    r_M = sb("r_M", [P, NE, NT])
    r_s = r_l[:, :, :].rearrange("p t e -> p (t e)").rearrange("p (e t) -> p e t", e=NE)
    r_c = r_q[:, :, :].rearrange("p t e -> p (t e)").rearrange("p (e t) -> p e t", e=NE)
    r_e = sb("r_e", [P, 6, NE])
    r_i = sb("r_i", [P, NE], mybir.dt.int32)
    with ExitStack() as c:
        qst = sb("qst", [P, 512], c=c)
    r_t = sb("r_t", [1, NTI, NE])
    r_v = sb("r_v", [1, NTI])
    rm = sb("rm", [P, 8, NT])
    oh1 = sb("oh1", [P, NT, NE])
    oh2 = sb("oh2", [P, NT, NE])
    gate = sb("gate", [P, NB, 2, NT])
    slot = sb("slot", [P, NB, 2, NT], mybir.dt.int32)
    texp = sb("texp", [1, NB, NTI], mybir.dt.int32)
    nx = sb("nx", [P, NNX, D])
    xT = sb("xT", [P, 2, 2, P])
    zero = xT[:, 0, :, :].rearrange("p c n -> p (c n)")
    xbuf = [nc.dram_tensor(f"xbuf{b}", [NTI * P, D], F32, kind="Internal").ap() for b in range(NB)]
    ybuf = [nc.dram_tensor(f"ybuf{b}", [NTI * P, D], F32, kind="Internal").ap() for b in range(NB)]

    t_id = dma("sp", ident[:, :], I["ident"])
    t_tri = dma("act", tri[:, :, :], I["tri"])
    t_thr = dma("act", thr[:, :], I["thr"])
    t_wr0 = dma("act", wr[:, :, :], I["wrT"].rearrange("(c p) n -> p c n", p=P))
    t_eb = dma("act", ebB[:, :], I["ebias"].unsqueeze(0).to_broadcast([P, NE]))
    t_pri = dma("act", pri[:, :], I["pri"].unsqueeze(0).to_broadcast([P, NE]))
    t_g1 = dma("act", g1c[:, :], I["g1"])
    t_g2 = dma("act", g2c[:, :], I["g2"])
    V(lambda e: e.memset(eps[:, 0:1], EPS_LN))
    t_eps = V(lambda e: e.memset(eps[:, 1:2], EPS_RMS))
    for dc in range(2):
        t_wr = V(lambda e, dc=dc: e.tensor_scalar(wr[:, dc, :], wr[:, dc, :], g2c[:, dc:dc + 1], None, ALU.mult), t_wr0, t_g2)
    t_z = G(lambda e: e.memset(zero, 0.0))

    def tokens(ap, b):
        return ap[b].rearrange("(p t) d -> p t d", t=NT)

    W = []
    with ExitStack() as c:
        nxT = sb("nxT", [P, 2, S], c=c)
        KA0 = sb("KA0", [P, S], F32R, c=c)
        KB0 = sb("KB0", [P, S], F32R, c=c)
    W.append(sb("w0", [P, 2, 2, S]))
    with ExitStack() as c:
        Q01 = [sb(f"Q{i}", [P, S], F32R, c=c) for i in range(4)]
    with ExitStack() as c:
        NX = NG = 4
        xg = sb("xg", [P, NX, D], c=c)
        xh = sb("xh", [P, 3, 2, P], F32R, c=c)
        xl = sb("xl", [P, 3, 2, P], F32R, c=c)
        sg = sb("sg", [P, 2, D], c=c)
        hg = sb("hg", [P, 2, D], c=c)
        hh = sb("hh", [P, 3, 2, P], F32R, c=c)
        hl = sb("hl", [P, 3, 2, P], F32R, c=c)
        yo = sb("yo", [P, 3, D], c=c)
        y12 = sb("y12", [P, NG, 2, D], c=c)
    W.append(sb("w1", [P, 2, 2, S]))
    wT, w2T = [w[:, 0, :, :] for w in W], [w[:, 1, :, :] for w in W]
    c3 = ExitStack()
    VH = sb("VH", [P, NB * NT, 65], F32R, c=c3)
    VL = sb("VL", [P, NB * NT, 65], F32R, c=c3)
    mx = sb("mx", [P, 2, 8, 4], c=c3)
    m16 = sb("m16", [P, 2, 8], c=c3)
    mT = sb("mT", [8, 2, P], F32R, c=c3)
    rz = sb("rz", [P, 2, 1], c=c3)
    wk = sb("wk", [P, 2, P], c=c3)
    wv = sb("wv", [P, 2, 64], c=c3)
    wqp = sb("wqp", [P, 2, D], c=c3)

    c1 = ExitStack()
    x = sb("x", [P, NB * NT, D], c=c1)
    rows = sb("rows", [P, NB, 3, D], c=c1)
    st = sb("st", [P, 4, 6], c=c1)
    mv = sb("mv", [P, NB * NT, 2], c=c1)
    sd = sb("sd", [P, NB * NT], c=c1)
    rs = sb("rs", [P, NB * NT], c=c1)
    nm = sb("nm", [P, NB * NT], c=c1)
    NXN = 3
    xn = sb("xn", [P, NXN, 4, D], c=c1)
    cT = sb("cT", [P, 2, NB], c=c1)
    sil = sb("sil", [P, 2, NB], c=c1)
    sc = sb("sc", [P, 2, NB], c=c1)
    modc = sb("modc", [P, 2, 2, NB], c=c1)
    gab = sb("gab", [P, NB, D], c=c1)
    boutB = sb("boutB", [P, D], c=c1)
    wqkv = sb("wqkv", [P, 2, D], c=c1)
    wout = sb("wout", [P, 2, D], c=c1)
    wouts = sb("wouts", [P, 2, NB, D], c=c1)
    mask = sb("mask", [P, 2, 16], c=c1)
    tempB = sb("tempB", [P, 16], c=c1)
    LB = sb("LB", [P, 2, NB, 16], c=c1)
    ssq = sb("ssq", [P, 2, NB, 4], c=c1)
    n2 = sb("n2", [P, 2, NB], c=c1)
    piS = sb("piS", [P, 2, NB, 4], c=c1)
    dS = sb("dS", [P, 2, NB, 4], c=c1)
    cf = sb("cf", [P, 2, NB, 3], c=c1)
    lT = sb("lT", [16, 2, 512], c=c1)
    le = sb("le", [P, NB, NT, 16], c=c1)
    lm = sb("lm", [P, NB, NT, 3], c=c1)
    hT = X2[:, 0:8, :].rearrange("p a d -> p (a d)").rearrange("p (r c n) -> p r c n", r=2, c=2)
    silB = X2[:, 8:10, :].rearrange("p c (b n) -> p c b n", b=NB)
    gtmp = X2[:, 10:12, :]
    piE = X2[:, NT:NT + 8, :].rearrange("p (r t) d -> p r t d", r=2)
    piT = X2[:, NT + 8:2 * NT, :].rearrange("p a d -> p (a d)").rearrange("p (r c n) -> p r c n", r=2, c=2)
    junk = sb("junk", [P, 512], c=c1)
    wmod = W[1][:, :, :, :].rearrange("p a c n -> p (a c n)")[:, 0:12 * D].rearrange("p (c n) -> p c n", c=2)

    wms = I["wmod"].rearrange("(c p) n -> p c n", p=P)
    t_x = [None] * 8

    def load_x(g):
        b, i = divmod(g, 4)
        t_x[g] = dma("sp", x[:, 4 * g:4 * g + 4, :], tokens(I["x"], b)[:, 4 * i:4 * i + 4, :])
    t_c = dma("sp", cT[:, :, :], I["cT"].rearrange("(c p) b -> p c b", p=P))
    load_x(0)
    t_wm = [dma("sp", wmod[:, :, 0:512], wms[:, :, 0:512])]
    load_x(1)
    t_wq = dma("act", wqkv[:, :, :], I["wqkvT"].rearrange("(c p) n -> p c n", p=P))
    load_x(2)
    t_wm.append(dma("sp", wmod[:, :, 512:1536], wms[:, :, 512:1536]))
    for g in range(3, 8):
        load_x(g)
    t_mk = dma("act", mask[:, :, :], I["mask"].rearrange("(c p) n -> p c n", p=P))
    t_tp = dma("act", tempB[:, :], I["temp"].rearrange("h o -> o h").to_broadcast([P, 16]))
    t_wo = dma("act", wout[:, :, :], I["woutT"].rearrange("(c p) n -> p c n", p=P))
    t_bo = dma("act", boutB[:, :], I["bout"].unsqueeze(0).to_broadcast([P, D]))
    fold_g1, t_wg1 = [], []
    t_wk = dma("act", wk[:, :, :], I["wkcT2"].rearrange("(c p) n -> p c n", p=P))
    t_wv = dma("act", wv[:, :, :], I["wvcT"].rearrange("(c p) n -> p c n", p=P))
    t_wqp = dma("act", wqp[:, :, :], I["wqT"].rearrange("(c p) n -> p c n", p=P))
    for dc in range(2):
        for w, t in ((wk, t_wk), (wv, t_wv), (wqp, t_wqp)):
            fold_g1.append(lambda w=w, t=t, dc=dc: V(
                lambda e: e.tensor_scalar(w[:, dc, :], w[:, dc, :], g1c[:, dc:dc + 1], None, ALU.mult), t, t_g1))
    t = G(lambda e: e.memset(VH[:, :, 64:65].bitcast(F32), 1.0))
    t_one = G(lambda e: e.memset(VL[:, :, 64:65].bitcast(F32), 0.0), t)

    ring = Ring([0, 1, 2, 3, 4, 5, 6, 7])
    t_modc, t_gab, t_rows, t_mr = [], {}, {0: [], 1: []}, []
    gt_free = [None]
    t_sil = {}

    def silu():
        t = A(lambda e: e.activation(sc[:, :, :], cT[:, :, :], ACT.Exp, scale=-1.0), t_c)
        t = V(lambda e: e.tensor_scalar_add(sc[:, :, :], sc[:, :, :], 1.0), t)
        t = V(lambda e: e.reciprocal(sc[:, :, :], sc[:, :, :]), t)
        t_sil[0] = V(lambda e: e.tensor_tensor(sil[:, :, :], sc[:, :, :], cT[:, :, :], ALU.mult), t)
        t_sil[1] = V(lambda e: e.tensor_copy(silB[:, :, :, :], bc(sil[:, :, :], P, 3)), t_sil[0])

    def mod_cols():
        k = ring.take()

        def f(e):
            for i in range(2):
                for j in range(2):
                    for c in range(2):
                        mm = e.matmul(PS[:, k, (i * 2 + j) * 2:(i * 2 + j) * 2 + 2],
                                      wmod[:, c, i * D + j * P:i * D + j * P + P], sil[:, c, :],
                                      start=(c == 0), stop=(c == 1))
            return mm
        t = T(f, t_wm[0], t_sil[0], rel[k])
        pm = PS[:, k, 0:8].rearrange("p (i j b) -> p i j b", i=2, j=2)
        t_modc.append(V(lambda e: e.tensor_copy(modc[:, 0, :, :], pm[:, 0, :, :]), t))
        t_modc.append(V(lambda e: e.tensor_scalar_add(modc[:, 1, :, :], pm[:, 1, :, :], 1.0), t))
        rel[k] = list(t_modc)
        t_mr.append(t)

    def away(src, dst, t_mr):
        t1 = V(lambda e: e.tensor_scalar(gtmp[:, 0, :], src, 0.0, 2.0, ALU.is_ge, ALU.mult), t_mr, gt_free[0])
        t2 = V(lambda e: e.tensor_scalar(gtmp[:, 1, :], src, -1.0, None, ALU.mult), t_mr, gt_free[0])
        t2 = V(lambda e: e.scalar_tensor_tensor(gtmp[:, 1, :], src, 0.25, gtmp[:, 1, :], ALU.max, ALU.max), t2)
        gt_free[0] = V(lambda e: e.scalar_tensor_tensor(dst, gtmp[:, 0, :], -1.0, gtmp[:, 1, :], ALU.add, ALU.mult), t1, t2)
        return gt_free[0]

    def mod_rows(b, n):
        k = ring.take()

        def f(e):
            for c in range(2):
                mm = e.matmul(PS[:, k, :], silB[:, c, b, :], wmod[:, c, 2 * D + n * 512:2 * D + n * 512 + 512],
                              start=(c == 0), stop=(c == 1))
            return mm
        t = T(f, t_wm, t_sil[1], rel[k])
        t_mr.append(t)
        if n == 0:
            t1 = away(PS[:, k, 0:D], rows[:, b, 0, :], t)
            t2 = V(lambda e: e.tensor_copy(rows[:, b, 1, :], PS[:, k, D:512]), t)
            t_gab[b] = V(lambda e: e.tensor_tensor(gab[:, b, :], rows[:, b, 0, :], boutB[:, :], ALU.mult), t1, t_bo)
        else:
            t1 = V(lambda e: e.tensor_scalar_add(rows[:, b, 2, :], PS[:, k, 0:D], 1.0), t)
            t2 = away(PS[:, k, D:512], gb[:, b, :], t)
        t_rows[b] += [t1, t2]
        rel[k] = [t1, t2]

    t_bn, t_rt, t_xn, ln_done = {}, {}, {}, [None]
    xn_free = [None] * NXN
    xn_i = [0]

    def stats(key, g, src):
        ts = slice(4 * g, 4 * g + 4)
        for i in range(4):
            ta = V(lambda e, i=i: e.bn_stats(st[:, i, :], x[:, 4 * g + i, :]), src(), ln_done[0])
        for i in range(4):
            tb = V(lambda e, i=i: e.bn_aggr(mv[:, 4 * g + i, :], st[:, i, :]), ta)
        ln_done[0] = tb
        t_bn[key, g] = tb

    def root(key, g):
        ts = slice(4 * g, 4 * g + 4)
        t_rt[key, g] = A(lambda e: e.activation(sd[:, ts], mv[:, ts, 1], ACT.Sqrt, bias=eps[:, 0:1]), t_bn[key, g], t_eps)

    def norm1(g):
        ts = slice(4 * g, 4 * g + 4)
        q = xn_i[0] % NXN
        xn_i[0] += 1
        t1 = V(lambda e: e.reciprocal(rs[:, ts], sd[:, ts]), t_rt[1, g])
        for i in range(4):
            n = 4 * g + i
            t = V(lambda e, i=i, n=n: e.tensor_scalar(xn[:, q, i, :], x[:, n, :], mv[:, n, 0:1], rs[:, n:n + 1],
                                                      ALU.subtract, ALU.mult), t1, xn_free[q])
        t_xn[1, g] = (q, t)

    hT_free = [None, None]
    did = set()
    t_h, t_w = {}, {0: [], 1: []}

    def turn(g):
        assert len(t_modc) == 2 and (g < 2 or g - 2 in did)
        b, r = g // 4, g % 2
        q, tx = t_xn[1, g]
        t_h[g] = []
        for dc in range(2):
            k = ring.take()

            def tr(e, dc=dc, k=k):
                for i in range(4):
                    mm = e.transpose(PS[:, k, i * P:i * P + P], xn[:, q, i, dc * P:dc * P + P], ident[:, :])
                return mm
            t = T(tr, tx, t_id, rel[k])
            xn_free[q] = t
            t = A(lambda e, dc=dc, k=k: e.activation(hT[:, r, dc, :], PS[:, k, :], ACT.Identity,
                                                     bias=modc[:, 0, dc, b:b + 1], scale=modc[:, 1, dc, b:b + 1]),
                  t, t_modc, hT_free[r])
            rel[k] = [t]
            t_h[g].append(t)

    def project(g):
        assert g < 4 or len(t_mr) == 5
        did.add(g)
        b, r = g // 4, g % 2
        cols = slice(g % 4 * 512, g % 4 * 512 + 512)
        for oc in range(2):
            k = ring.take()

            def f(e, oc=oc, k=k):
                for dc in range(2):
                    mm = e.matmul(PS[:, k, :], wqkv[:, dc, oc * P:oc * P + P], hT[:, r, dc, :], start=(dc == 0), stop=(dc == 1))
                return mm
            tm = T(f, t_h[g], t_wq, rel[k])
            after = [tm, t_mr if b else None]

            def copy(w):
                return V(lambda e, oc=oc, k=k: e.tensor_copy(wT[b][:, oc, cols], PS[:, k, :]), w)

            def square(w):
                return A(lambda e, oc=oc, k=k: e.activation(w2T[b][:, oc, cols], PS[:, k, :], ACT.Square,
                                                            accum_out=ssq[:, oc, b, g % 4:g % 4 + 1]), w)
            t = copy(square(after)) if oc == 0 else square(copy(after))
            rel[k] = [t]
            t_w[b].append(t)
        hT_free[r] = tm

    t_mt, t_lb, t_le, t_pi = [], {}, {}, {}
    t_xp = {}

    def add_bias(g):
        b = g // 4
        t_xp[g] = G(lambda e: e.tensor_tensor(x[:, 4 * g:4 * g + 4, :], x[:, 4 * g:4 * g + 4, :], bc(gab[:, b, :], 4, 1),
                                              ALU.add), t_gab[b], t_xn[1, g][1])

    def scales(b):
        assert len(t_w[b]) == 8
        if b == 0:
            t_mt.append(V(lambda e: e.tensor_tensor(mask[:, :, :], mask[:, :, :], bc(tempB[:, :], 2, 1), ALU.mult), t_mk, t_tp))
        t = V(lambda e: e.tensor_reduce(n2[:, :, b], ssq[:, :, b, :], AX, ALU.add), t_w[b])
        t = V(lambda e: e.tensor_scalar(n2[:, :, b], n2[:, :, b], 1e-24, None, ALU.max), t)
        t = V(lambda e: e.reciprocal(n2[:, :, b], n2[:, :, b]), t)
        for oc in range(2):
            t_lb[b] = V(lambda e, oc=oc: e.tensor_scalar(LB[:, oc, b, :], mask[:, oc, :], n2[:, oc, b:b + 1], None,
                                                         ALU.mult), t, t_mt)

    t_lt = {}
    lt_free = [None, None]

    def logits(b, g):
        k, r = ring.take(), g % 2

        def f(e):
            for oc in range(2):
                mm = e.matmul(PS[0:16, k, :], LB[:, oc, b, :], w2T[b][:, oc, g * 512:g * 512 + 512],
                              start=(oc == 0), stop=(oc == 1))
            return mm
        t = T(f, t_lb[b], rel[k])
        t_lt[b, g] = A(lambda e: e.activation(lT[:, r, :], PS[0:16, k, :], ACT.Copy), t, lt_free[r])
        rel[k] = [t_lt[b, g]]

    def turn_logits(b, g):
        k, r = ring.take(), g % 2
        ts = slice(4 * g, 4 * g + 4)

        def f(e):
            for i in range(4):
                mm = e.transpose(PS[:, k, i * 16:i * 16 + 16], lT[:, r, i * P:i * P + P], ident[0:16, 0:16])
            return mm
        tl = T(f, t_lt[b, g], t_id, rel[k])
        lt_free[r] = tl
        pl = PS[:, k, 0:64].rearrange("p (t h) -> p t h", h=16)
        t = V(lambda e: e.tensor_reduce(lm[:, b, ts, 0], pl, AX, ALU.max), tl)
        t = V(lambda e: e.tensor_tensor(le[:, b, ts, :], pl, bc(lm[:, b, ts, 0], 16, 2), ALU.subtract), t)
        rel[k] = [t]
        t_le[b, g] = A(lambda e: e.activation(le[:, b, ts, :], le[:, b, ts, :], ACT.Exp), t)

    def softmax(b, g):
        ts = slice(4 * g, 4 * g + 4)
        t = V(lambda e: e.tensor_reduce(lm[:, b, ts, 1], le[:, b, ts, :], AX, ALU.add), t_le[b, g])
        t = V(lambda e: e.reciprocal(lm[:, b, ts, 2], lm[:, b, ts, 1]), t)
        t_pi[b, g] = V(lambda e: e.tensor_tensor(le[:, b, ts, :], le[:, b, ts, :], bc(lm[:, b, ts, 2], 16, 2), ALU.mult), t)

    t_pE, t_pT, t_d = {}, {}, {0: [], 1: []}
    pE_free, pT_free = [None, None], [[], []]
    t_junk = [None]

    def spread_pi(b, g):
        r = g % 2
        t_pE[b, g] = A(lambda e: e.activation(
            piE[:, r, :, :].rearrange("p t (h d) -> p (t h) d", d=16),
            bc(le[:, b, 4 * g:4 * g + 4, :].rearrange("p t h -> p (t h)"), 16, 2), ACT.Copy), t_pi[b, g], pE_free[r])

    def turn_pi(b, g):
        r = g % 2
        t_pT[b, g] = []
        for oc in range(2):
            k = ring.take()

            def tr(e, oc=oc, k=k):
                for i in range(4):
                    mm = e.transpose(PS[:, k, i * P:i * P + P], piE[:, r, i, oc * P:oc * P + P], ident[:, :])
                return mm
            t = T(tr, t_pE[b, g], rel[k])
            pE_free[r] = t
            t = A(lambda e, oc=oc, k=k: e.activation(piT[:, r, oc, :], PS[:, k, :], ACT.Copy,
                                                     accum_out=piS[:, oc, b, g:g + 1]), t, pT_free[r])
            rel[k] = [t]
            t_pT[b, g].append(t)
            t_d[b].append(t)

    def dots(b, g):
        r = g % 2
        cols = slice(g * 512, g * 512 + 512)
        pT_free[r] = []
        for oc in range(2):
            t_junk[0] = V(lambda e, oc=oc: e.tensor_tensor_reduce(
                out=junk[:, :], in0=piT[:, r, oc, :], in1=w2T[b][:, oc, cols], scale=1.0, scalar=0.0,
                op0=ALU.mult, op1=ALU.add, accum_out=dS[:, oc, b, g:g + 1]), t_pT[b, g][oc], t_junk[0])
            t = G(lambda e, oc=oc: e.tensor_tensor(wT[b][:, oc, cols], wT[b][:, oc, cols], piT[:, r, oc, :], ALU.mult),
                  t_pT[b, g][oc], t_w[b])
            pT_free[r] += [t_junk[0], t]
            t_d[b] += [t_junk[0], t]

    t_wg, t_x1, t_o = {}, {}, {}

    def fold(b):
        assert len(t_d[b]) == 24 and len(t_rows[b]) == 4
        t1 = V(lambda e: e.tensor_reduce(cf[:, :, b, 0], piS[:, :, b, :], AX, ALU.add), t_d[b])
        t2 = V(lambda e: e.tensor_reduce(cf[:, :, b, 1], dS[:, :, b, :], AX, ALU.add), t_d[b])
        t = V(lambda e: e.tensor_scalar_add(cf[:, :, b, 0], cf[:, :, b, 0], 1e-8), t1)
        t = V(lambda e: e.reciprocal(cf[:, :, b, 0], cf[:, :, b, 0]), t)
        t = V(lambda e: e.tensor_tensor(cf[:, :, b, 1], cf[:, :, b, 1], cf[:, :, b, 0], ALU.mult), t, t2)
        t = V(lambda e: e.tensor_scalar_add(cf[:, :, b, 1], cf[:, :, b, 1], 1.0), t)
        t = V(lambda e: e.reciprocal(cf[:, :, b, 2], cf[:, :, b, 1]), t)
        for oc in range(2):
            t1 = V(lambda e, oc=oc: e.tensor_scalar(wouts[:, oc, b, :], wout[:, oc, :], cf[:, oc, b, 2:3], -1.0,
                                                    ALU.mult, ALU.mult), t, t_wo)
        for oc in range(2):
            t_wg[b] = V(lambda e, oc=oc: e.tensor_tensor(wouts[:, oc, b, :], wouts[:, oc, b, :], rows[:, b, 0, :],
                                                         ALU.mult), t1, t_rows[b])

    def oproj(b, i):
        k = ring.take()

        def f(e):
            for j in range(2):
                n = (2 * i + j) * P
                for oc in range(2):
                    mm = e.matmul(PS[:, k, j * D:j * D + D], wT[b][:, oc, n:n + P], wouts[:, oc, b, :],
                                  start=(oc == 0), stop=(oc == 1))
            return mm
        t = T(f, t_wg[b], t_d[b], rel[k])
        if i == 7:
            t_o[b] = t
        n = b * NT + 2 * i
        t = V(lambda e: e.tensor_tensor(x[:, n:n + 2, :], PS[:, k, :].rearrange("p (t d) -> p t d", d=D),
                                        x[:, n:n + 2, :], ALU.add), t, t_xp[n // 4])
        rel[k] = [t]
        t_x1[8 * b + i] = t

    t_h2, t_sq, t_sp = {}, {}, []

    def norm2(g):
        b = g // 4
        ts = slice(4 * g, 4 * g + 4)
        q = xn_i[0] % NXN
        xn_i[0] += 1
        t = V(lambda e: e.reciprocal(rs[:, ts], sd[:, ts]), t_rt[2, g])
        t = V(lambda e: e.scalar_tensor_tensor(nm[:, ts], mv[:, ts, 0], -1.0, rs[:, ts], ALU.mult, ALU.mult), t)
        for i in range(4):
            n = 4 * g + i
            ta = A(lambda e, i=i, n=n: e.activation(xn[:, q, i, :], x[:, n, :], ACT.Identity, bias=nm[:, n:n + 1],
                                                    scale=rs[:, n:n + 1]), t, xn_free[q])
        t_xn[2, g] = (q, ta)

    def shift2(g):
        b = g // 4
        ts = slice(4 * g, 4 * g + 4)
        assert len(t_rows[0]) == len(t_rows[1]) == 4
        q, t = t_xn[2, g]
        t = V(lambda e: e.tensor_tensor(xn[:, q, :, :], xn[:, q, :, :], bc(rows[:, b, 2, :], 4, 1), ALU.mult), t, t_rows[b])
        t_xn[3, g] = (q, G(lambda e: e.tensor_tensor(X2[:, ts, :], xn[:, q, :, :], bc(rows[:, b, 1, :], 4, 1), ALU.add), t,
                           list(t_rows.values()), t_d[1] if b else hT_free))

    def squares(g):
        ts = slice(4 * g, 4 * g + 4)
        q, t = t_xn[3, g]
        for i in range(4):
            n = 4 * g + i
            sq = A(lambda e, i=i, n=n: e.activation(xn[:, q, i, :], X2[:, n, :], ACT.Square, accum_out=ssq2[:, n:n + 1]), t)
        xn_free[q] = sq
        t_sq[g] = A(lambda e: e.activation(rs2[:, ts], ssq2[:, ts], ACT.Sqrt, bias=eps[:, 1:2], scale=1.0 / D), sq)

    def rsqrt2(g):
        ts = slice(4 * g, 4 * g + 4)
        t_h2[g] = V(lambda e: e.reciprocal(rs2[:, ts], rs2[:, ts]), t_sq[g])

    def spill(b):
        t_sp.append(dma("sp", tokens(x1d, b), x[:, b * NT:b * NT + NT, :], [t_x1[8 * b + i] for i in range(8)]))

    QA = [Q01[i][:, :] for i in range(2)]
    QB = [Q01[i][:, :] for i in range(2, 4)]
    KA, KB = [KA0[:, :]], [KB0[:, :]]
    vhf = VH[:, :, :].bitcast(F32)
    qaf = [q.bitcast(F32) for q in QA]
    t_neg = {}

    def minus_one(b):
        t_neg[b] = G(lambda e: e.memset(KB[b][64:65, :].bitcast(F32), -1.0), k_free(b))

    def k_free(b):
        return t_o[0] if b == 0 else t_p1

    st_nx = [None] * NNX
    t_nxT = {}
    nxT_free = {1: []}
    t_k, t_v, t_q = {}, {}, {}
    q_free = [[], [], []]
    cnt = [0]

    def staged(*stages):
        return [lambda i=i, n=n, f=f: f(i - n) for i in range(NT + len(stages) - 1) for n, f in enumerate(stages)
                if 0 <= i - n < NT]

    def nx_jobs(b):
        held = {}

        def scale(i):
            n = b * NT + i
            s = cnt[0] % NNX
            cnt[0] += 1
            nxT_free[b] = [t_last_q[0]] if b else [t_o[0]]
            held[i] = s, V(lambda e: e.tensor_scalar(nx[:, s, :], X2[:, n, :], rs2[:, n:n + 1], None, ALU.mult),
                           t_h2[n // 4], st_nx[s])

        def job(i):
            s, t = held[i]
            k = ring.take()

            def tr(e):
                for dc in range(2):
                    mm = e.transpose(PS[:, k, dc * P:dc * P + P], nx[:, s, dc * P:dc * P + P], ident[:, :])
                return mm
            t = T(tr, t, rel[k])
            st_nx[s] = t
            t2 = A(lambda e: e.activation(nxT[:, :, i * P:i * P + P], PS[:, k, 0:256].rearrange("p (c n) -> p c n", c=2),
                                          ACT.Copy), t, nxT_free[b])
            rel[k] = [t2]
            t_nxT[b, i] = t2
        return staged(scale, job)

    def k_jobs(b):
        def job(c):
            k = ring.take()

            def mmk(e):
                for dc in range(2):
                    mm = e.matmul(PS[:, k, :], wk[:, dc, :], nxT[:, dc, c * 512:c * 512 + 512], start=(dc == 0), stop=(dc == 1))
                return mm
            t = T(mmk, t_wg1, t_nxT[b, 4 * c + 3], rel[k])
            cols = slice(c * 512, c * 512 + 512)
            ta = A(lambda e: e.activation(KA[b][:, cols], PS[:, k, :], ACT.Copy), t, k_free(b))
            tv = V(lambda e: e.tensor_tensor(KA[b][64:128, cols], PS[64:128, k, :], KA[b][64:128, cols].bitcast(F32),
                                             ALU.subtract), ta)
            rel[k] = [tv]
            tg = G(lambda e: e.tensor_copy(KB[b][0:64, cols], KA[b][0:64, cols]), ta, k_free(b))
            t_k[b, c] = [tv, tg]
        return [lambda c=c: job(c) for c in range(4)]

    def v_jobs(b):
        def job(c):
            k = ring.take()

            def mmv(e):
                for i in range(4):
                    for dc in range(2):
                        mm = e.matmul(PS[:, k, i * 64:i * 64 + 64], nxT[:, dc, (4 * c + i) * P:(4 * c + i + 1) * P],
                                      wv[:, dc, :], start=(dc == 0), stop=(dc == 1))
                return mm
            t = T(mmv, t_wg1, t_nxT[b, 4 * c + 3], rel[k])
            n = b * NT + 4 * c
            pv = PS[:, k, 0:256].rearrange("p (t d) -> p t d", d=64)
            t = A(lambda e: e.activation(VH[:, n:n + 4, 0:64], pv, ACT.Copy), t, t_one)
            t = V(lambda e: e.tensor_tensor(VL[:, n:n + 4, 0:64], pv, vhf[:, n:n + 4, 0:64], ALU.subtract), t)
            rel[k] = [t]
            t_v[b, c] = t
        return [lambda c=c: job(c) for c in range(4)]

    def q_jobs(b, pair):
        held = {}

        def job(c):
            k = ring.take()

            def mmq(e):
                for dc in range(2):
                    mm = e.matmul(PS[:, k, :], wqp[:, dc, pair * P:pair * P + P], nxT[:, dc, c * 512:c * 512 + 512],
                                  start=(dc == 0), stop=(dc == 1))
                return mm
            t = T(mmq, t_wg1, t_nxT[b, 4 * c + 3], rel[k])
            t_last_q[b] = t
            if b == 0 and pair == 0:
                q_free[0] = q_free[1] = t_o[1]
            held[c] = rel[k] = [A(lambda e: e.activation(qst[:, :], PS[:, k, :], ACT.Copy), t, qst_free)]

        def high(c):
            cols = slice(c * 512, c * 512 + 512)
            parts = []
            for j in range(2):
                s, r, o = (4 * b + 2 * pair + j) % 3, slice(64 * j, 64 * j + 64), slice(64 - 64 * j, 128 - 64 * j)
                ta = A(lambda e, s=s, r=r: e.activation(QA[s][r, cols], qst[r, :], ACT.Copy), held[c], q_free[s])
                tg = G(lambda e, s=s, r=r, o=o: e.tensor_copy(QA[s][o, cols], QA[s][r, cols]), ta, q_free[s])
                parts.append((s, r, j, ta, tg))
            held[c] = parts

        def low(c):
            cols = slice(c * 512, c * 512 + 512)
            for s, r, j, ta, tg in held[c]:
                tv = V(lambda e, s=s, r=r: e.tensor_tensor(QB[s][0:64, cols], qst[r, :], qaf[s][r, cols], ALU.subtract),
                       ta, q_free[s])
                t_q[b, 2 * pair + j, c] = [tv, tg]
            qst_free[:] = [tv]
        return [lambda c=c, f=f: f(c) for c in range(4) for f in (job, high, low)]

    qst_free = []
    t_last_q = {}
    mx_free = [None, None]
    m_free = [None, None]
    t_m = {}

    def max_jobs(bh, half):
        b, h, qs = bh // 4, bh % 4, bh % 3
        s = (2 * bh + half) % 2
        last = []

        def job(i, c):
            k = ring.take()
            t = T(lambda e: e.matmul(PS[:, k, :], QA[qs][:, i * P:i * P + P], KA[b][:, c * 512:c * 512 + 512],
                                     start=True, stop=True), t_q[b, h, i // 4], t_k[b, c], rel[k])
            t = V(lambda e: e.tensor_reduce(mx[:, s, i % 8, c:c + 1], PS[:, k, :], AX, ALU.max), t, mx_free[s])
            rel[k] = [t]
            last[:] = [t]

        def rest():
            pass

        def close1():
            mx_free[s] = V(lambda e: e.tensor_reduce(m16[:, s, :], mx[:, s, :, :], AX, ALU.max), last, m_free[s])

        def close2():
            k = ring.take()
            t = T(lambda e: e.transpose(PS[0:8, k, 0:P], m16[:, s, :], ident[:, :]), mx_free[s], rel[k])
            t = V(lambda e: e.tensor_copy(mT[:, s, :], PS[0:8, k, 0:P]), t, m_free[s])
            rel[k] = [t]
            t_m[bh, half] = dma("sp", QB[qs][64:65, half * 1024:half * 1024 + 1024].bitcast(F32),
                                mT[:, s, :].bitcast(F32), t, q_free[qs])
            m_free[s] = t_m[bh, half]
        jobs = [lambda i=i, c=c: job(i, c) for i in range(8 * half, 8 * half + 8) for c in range(4)]
        return jobs + [close1, rest, rest, close2]

    O_free = [[], []]
    t_O = {}
    rz_free = [None, None]
    t_X2 = {}

    def proj_jobs(bh):
        b, h = bh // 4, bh % 4

        def job(i):
            k = ring.take()
            s = i % 2
            n = b * NT + i
            t = T(lambda e: e.matmul(PS[:, k, 0:257], O[0:65, i * P:i * P + P], woa[0:65, h, :], start=True, stop=True),
                  t_O[bh, i // 8], t_woa, rel[k])
            O_free[i // 8] = [t]
            t = V(lambda e: e.reciprocal(rz[:, s, :], PS[:, k, 256:257]), t, rz_free[s])
            t = V(lambda e: e.scalar_tensor_tensor(X2[:, n, :], PS[:, k, 0:256], rz[:, s, :], X2[:, n, :],
                                                   ALU.mult, ALU.add), t, t_X2.get(n))
            rz_free[s] = t
            t_X2[n] = t
            rel[k] = [t]
        return [lambda i=i: job(i) for i in range(NT)]

    SB = [(0, 1), (2, 3)]
    pt_free, ph_free, pl_free = [None] * 2, [None] * 3, [None] * 3
    state = {}
    NSTEP = 32

    def qk(gs):
        bh, i = divmod(gs, NSTEP)
        b, h, qs = bh // 4, bh % 4, bh % 3
        qc, kc = divmod(i, 16)
        bk = SB[gs % 2]

        def f(e):
            for n in range(2):
                q0 = qc * 1024 + n * 512
                e.matmul(PS[:, bk[n], :], KA[b][:, kc * P:kc * P + P], QA[qs][:, q0:q0 + 512], start=True, stop=False)
            for n in range(2):
                q0 = qc * 1024 + n * 512
                mm = e.matmul(PS[:, bk[n], :], KB[b][0:65, kc * P:kc * P + P], QB[qs][0:65, q0:q0 + 512],
                              start=False, stop=True)
            return mm
        t = T(f, t_m[bh, qc], [t_q[b, h, 2 * qc + c] for c in range(2)], t_k[b, kc // 4], t_neg[b], rel[bk[0]], rel[bk[1]])
        if i == NSTEP - 1:
            q_free[qs] = [t]
        p, r = gs % 2, gs % 3
        t = A(lambda e: e.activation(PT[:, p, :], PS[:, bk[0]:bk[0] + 2, :].rearrange("p a n -> p (a n)"), ACT.Exp,
                                     scale=0.125), t, pt_free[p], t_p1)
        rel[bk[0]], rel[bk[1]] = [t], [t]
        th = A(lambda e: e.activation(PH[:, r, :], PT[:, p, :], ACT.Copy), t, ph_free[r], t_p1)
        state[gs] = (t, th)
        if by_pool(gs):
            low(G, gs)

    def by_pool(gs):
        return gs % POOL_EVERY == POOL_EVERY - 1 and gs < 7 * NSTEP + 20

    def low(put, gs):
        p, r = gs % 2, gs % 3
        t, th = state[gs]
        pt_free[p] = put(lambda e: e.tensor_tensor(PL[:, r, :], PT[:, p, :], phf[:, r, :], ALU.subtract), th, t, pl_free[r], t_p1)
        state[gs] = (th, pt_free[p])

    def av(gs, n):
        bh, i = divmod(gs, NSTEP)
        b = bh // 4
        qc, kc = divmod(i, 16)
        th, tl = state[gs]
        r = gs % 3
        c = slice(n * 512, n * 512 + 512)

        def f(e):
            e.matmul(PS[0:65, 4 + n, :], VH[:, b * NT + kc, :], PH[:, r, c], start=(kc == 0), stop=False)
            e.matmul(PS[0:65, 4 + n, :], VL[:, b * NT + kc, :], PH[:, r, c], start=False, stop=False)
            return e.matmul(PS[0:65, 4 + n, :], VH[:, b * NT + kc, :], PL[:, r, c], start=False, stop=(kc == 15))
        t = T(f, th, tl, t_v[b, kc // 4], rel[4 + n] if kc == 0 else None)
        if n == 1:
            ph_free[r] = pl_free[r] = t
        if kc == 15:
            q0 = qc * 1024 + n * 512
            t = A(lambda e: e.activation(O[:, q0:q0 + 512], PS[0:65, 4 + n, :], ACT.Copy), t, O_free[qc], t_p1)
            t_O[bh, qc] = t
            rel[4 + n] = [t]

    def spread(jobs, a, b):
        return [(a + (b - a) * i / len(jobs), j) for i, j in enumerate(jobs)]

    def main(bh, jobs):
        jobs = sorted(jobs, key=lambda x: x[0])
        for i in range(NSTEP):
            gs = bh * NSTEP + i
            if not by_pool(gs):
                low(V, gs)
            for part in range(3):
                if part == 0 and gs + 1 < 8 * NSTEP:
                    while i == NSTEP - 1 and jobs:
                        jobs.pop(0)[1]()
                    qk(gs + 1)
                if part and gs >= 1:
                    av(gs - 1, part - 1)
                while jobs and jobs[0][0] <= 3 * i + part:
                    jobs.pop(0)[1]()

    c_z = pr.counter()
    t_zf = []

    def zero_fill():
        for b in range(NB):
            zv = xbuf[b].rearrange("(n p a) d -> n p a d", p=P, a=3)
            for n in range(NTI // 3):
                t_zf[:] = [dma("sp", zv[n], bc(zero, 3, 1), t_z, t_p1, on=c_z)]

    t_rs = {}
    t_rl = {}
    t_sc = {}
    t_gate = {}
    r_free = [None]
    sqt = [None]
    xT_free = [None, None]

    def b8(ap):
        return bc(ap, NE, 2)

    def norm_jobs(b):
        def job(i):
            n = b * NT + i
            s = cnt[0] % NNX
            cnt[0] += 1
            sqt[0] = A(lambda e: e.activation(nx[:, s, :], X2[:, n, :], ACT.Square, accum_out=ssq2[:, n:n + 1]),
                       t_X2[n], st_nx[s], sqt[0])
            st_nx[s] = sqt[0]

        def close():
            ts = slice(b * NT, b * NT + NT)
            t = A(lambda e: e.activation(rs2[:, ts], ssq2[:, ts], ACT.Sqrt, bias=eps[:, 1:2], scale=1.0 / D), sqt[0],
                  (pr.sem["dve"], pr.n["dve"]))
            t_rs[b] = V(lambda e: e.reciprocal(rs2[:, ts], rs2[:, ts]), t)
        return [lambda i=i: job(i) for i in range(NT)] + [close]

    def rlog_jobs(b):
        held = {}

        def scale(i):
            n = b * NT + i
            s = cnt[0] % NNX
            cnt[0] += 1
            held[i] = s, V(lambda e: e.tensor_scalar(nx[:, s, :], X2[:, n, :], rs2[:, n:n + 1], None, ALU.mult), t_rs[b],
                           st_nx[s])

        def first(i):
            s, t = held[i]
            k = ring.take()

            def tr(e):
                for dc in range(2):
                    mm = e.transpose(PS[:, k, dc * P:dc * P + P], nx[:, s, dc * P:dc * P + P], ident[:, :])
                return mm
            t = T(tr, t, rel[k])
            st_nx[s] = t
            t = A(lambda e: e.activation(xT[:, i % 2, :, :], PS[:, k, 0:256].rearrange("p (c n) -> p c n", c=2), ACT.Copy),
                  t, xT_free[i % 2], t_zf)
            rel[k] = [t]
            held[i] = (s, t)

        def second(i):
            s, t = held[i]
            k = ring.take()

            def mm(e):
                for dc in range(2):
                    m = e.matmul(PS[:, k, 0:NE], xT[:, i % 2, dc, :], wr[:, dc, :], start=(dc == 0), stop=(dc == 1))
                return m
            t = T(mm, t, t_wr, rel[k])
            xT_free[i % 2] = t
            t_rl[b] = V(lambda e: e.tensor_tensor(r_l[:, i, :], PS[:, k, 0:NE], ebB[:, :], ALU.add), t, t_eb, r_free[0])
            rel[k] = [t_rl[b]]

        return staged(scale, first, second)

    def route_jobs(b, n):
        held = {}
        parts = choose(b, held), place(b, held)

        def go(part):
            for _ in range(n):
                next(part, None)
        return [lambda: go(parts[0])] * -(-26 // n) + [lambda: go(parts[1])] * -(-26 // n)

    def choose(b, held):
        t = V(lambda e: e.tensor_reduce(rm[:, 0, :], r_l[:, :, :], AX, ALU.max), t_rl[b])
        yield
        t = V(lambda e: e.tensor_tensor(r_l[:, :, :], r_l[:, :, :], b8(rm[:, 0, :]), ALU.subtract), t)
        yield
        t = A(lambda e: e.activation(r_q[:, :, :], r_l[:, :, :], ACT.Exp), t)
        t = V(lambda e: e.tensor_reduce(rm[:, 1, :], r_q[:, :, :], AX, ALU.add), t)
        yield
        t = V(lambda e: e.reciprocal(rm[:, 1, :], rm[:, 1, :]), t)
        yield
        t = V(lambda e: e.tensor_tensor(r_q[:, :, :], r_q[:, :, :], b8(rm[:, 1, :]), ALU.mult), t)
        yield
        for r, (oh, col) in enumerate(((oh1, 2), (oh2, 3))):
            t = V(lambda e, col=col: e.tensor_reduce(rm[:, col, :], r_q[:, :, :], AX, ALU.max), t)
            yield
            t = V(lambda e, oh=oh, col=col: e.tensor_tensor(oh[:, :, :], r_q[:, :, :], b8(rm[:, col, :]), ALU.is_equal), t)
            yield
            t = V(lambda e, oh=oh: e.tensor_tensor(oh[:, :, :], oh[:, :, :], bc(pri[:, :], NT, 1), ALU.mult), t, t_pri)
            yield
            t = V(lambda e, oh=oh: e.tensor_reduce(rm[:, 4, :], oh[:, :, :], AX, ALU.max), t)
            yield
            t = V(lambda e, oh=oh: e.tensor_tensor(oh[:, :, :], oh[:, :, :], b8(rm[:, 4, :]), ALU.is_equal), t)
            yield
            if r == 0:
                t = V(lambda e: e.scalar_tensor_tensor(r_q[:, :, :], oh1[:, :, :], -4.0, r_q[:, :, :], ALU.mult, ALU.add), t)
                yield
        tm = V(lambda e: e.tensor_tensor(r_M[:, :, :], oh1[:, :, :].rearrange("p t e -> p e t"),
                                         oh2[:, :, :].rearrange("p t e -> p e t"), ALU.add), t)
        t = V(lambda e: e.tensor_tensor(rm[:, 5, :], rm[:, 3, :], rm[:, 2, :], ALU.subtract), t)
        yield
        t = A(lambda e: e.activation(rm[:, 5, :], rm[:, 5, :], ACT.Exp), t)
        t = V(lambda e: e.tensor_scalar_add(rm[:, 6, :], rm[:, 5, :], 1.0), t)
        yield
        t = V(lambda e: e.reciprocal(gate[:, b, 0, :], rm[:, 6, :]), t)
        yield
        t_gate[b] = V(lambda e: e.tensor_tensor(gate[:, b, 1, :], rm[:, 5, :], gate[:, b, 0, :], ALU.mult), t)
        held["M"] = tm

    def place(b, held):
        k = ring.take()
        ring.hold(k)

        def count(e):
            mv_ = r_M[:, :, :].rearrange("p e t -> p (e t)")
            e.matmul(PS[:, k, 0:128], tri[:, 0, :], mv_, start=True, stop=True)
            return e.matmul(PS[:, k, 128:256], tri[:, 1, :], mv_, start=True, stop=True)
        tc = T(count, held["M"], t_tri, rel[k])
        pre = PS[:, k, 0:128].rearrange("p (e t) -> p e t", t=NT)
        tot = PS[:, k, 128:256].rearrange("p (e t) -> p e t", t=NT)
        t = V(lambda e: e.tensor_copy(r_s[:, :, :], tot), tc)
        yield
        tn = V(lambda e: e.tensor_reduce(r_e[:, 0, :], r_s[:, :, :], AX, ALU.add), t)
        yield
        t1 = V(lambda e: e.memset(r_e[:, 5, :], 1.0), t)
        yield
        t1 = V(lambda e: e.memset(r_c[:, :, :], 1.0), t1)
        yield
        t1 = V(lambda e: e.tensor_tensor_scan(r_c[:, :, :].rearrange("p e t -> p (e t)"),
                                              r_c[:, :, :].rearrange("p e t -> p (e t)"),
                                              r_s[:, :, :].rearrange("p e t -> p (e t)"), 0.0, ALU.mult, ALU.add), t1)
        yield
        t1 = V(lambda e: e.tensor_tensor(r_c[:, :, :], r_c[:, :, :], r_s[:, :, :], ALU.subtract), t1)
        yield
        t1 = V(lambda e: e.tensor_tensor(r_c[:, :, :], r_c[:, :, :], pre, ALU.add), t1)
        yield
        rel[k] = [t1]
        ring.free(k)
        t = V(lambda e: e.tensor_scalar_add(r_i[:, :], r_e[:, 0, :], 127.0), tn)
        yield
        t = V(lambda e: e.tensor_scalar(r_i[:, :], r_i[:, :], 7, 7, ALU.arith_shift_right, ALU.logical_shift_left), t)
        yield
        t = V(lambda e: e.tensor_copy(r_e[:, 1, :], r_i[:, :]), t)
        yield
        t = V(lambda e: e.tensor_tensor_scan(r_e[:, 2, :], r_e[:, 5, :], r_e[:, 1, :], 0.0, ALU.mult, ALU.add), t, t1)
        yield
        te = t
        t = V(lambda e: e.tensor_tensor(r_e[:, 3, :], r_e[:, 1, :], r_e[:, 0, :], ALU.subtract), t)
        yield
        t = V(lambda e: e.tensor_tensor_scan(r_e[:, 4, :], r_e[:, 5, :], r_e[:, 3, :], 0.0, ALU.mult, ALU.add), t)
        yield
        t = V(lambda e: e.tensor_tensor(r_e[:, 4, :], r_e[:, 4, :], r_e[:, 3, :], ALU.subtract), t)
        yield
        t = V(lambda e: e.tensor_tensor(r_c[:, :, :], r_c[:, :, :], bc(r_e[:, 4, :], NT, 2), ALU.add), t, t1)
        yield
        for j, oh in enumerate((oh1, oh2)):
            t2 = V(lambda e, oh=oh: e.tensor_tensor(r_M[:, :, :], oh[:, :, :].rearrange("p t e -> p e t"), r_c[:, :, :],
                                                    ALU.mult), t, tc)
            yield
            t2 = V(lambda e, j=j: e.tensor_reduce(rm[:, 7, :], r_M[:, :, :].rearrange("p e t -> p t e"), AX, ALU.add), t2)
            yield
            t = V(lambda e, j=j: e.tensor_copy(slot[:, b, j, :], rm[:, 7, :]), t2)
            yield
        t_slot[b] = t
        t = V(lambda e: e.tensor_tensor(r_t[:, :, :], bc(r_e[0:1, 2, :], NTI, 1), bc(thr[:, :], NE, 2), ALU.is_le), te, t_thr)
        yield
        t = V(lambda e: e.tensor_reduce(r_v[:, :], r_t[:, :, :], AX, ALU.add), t)
        yield
        t_texp[b] = V(lambda e: e.tensor_scalar(texp[:, b, :], r_v[:, :], float(NE - 1), None, ALU.min), t)
        r_free[0] = t_texp[b]

    t_slot, t_texp = {}, {}

    def scatter_jobs(b):
        def job(i):
            n = b * NT + i
            s = cnt[0] % NNX
            cnt[0] += 1
            t = V(lambda e: e.tensor_scalar(nx[:, s, :], X2[:, n, :], rs2[:, n:n + 1], None, ALU.mult), t_rs[b], st_nx[s])
            for j in range(2):
                on = c_nx[s]
                t2 = pr.start("pool", lambda e, j=j: e.indirect_dma_start(
                    out=xbuf[b], out_offset=bass.IndirectOffsetOnAxis(ap=slot[:, b, j, i:i + 1], axis=0),
                    in_=nx[:, s, :], in_offset=None), [t, t_slot[b], t_zf], on)
            st_nx[s] = t2
            t_nxs[n] = t
            t_sc[b] = [(c[0], 16 * c[1]) for c in c_nx]
        return [lambda i=i: job(i) for i in range(NT)]

    t_nxs = {}
    c_nx = [pr.counter() for _ in range(NNX)]

    wst = nxT[:, :, :].rearrange("p c n -> p (c n)")[:, 0:4 * 768].rearrange("p (s c n) -> p s c n", s=2, c=2)
    wsh = KA0[:, 0:2 * 768].rearrange("p (c n) -> p c n", c=2)
    wsl = KB0[:, 0:2 * 768].rearrange("p (c n) -> p c n", c=2)
    wd = I["wexp"].rearrange("e (c p) n -> e p c n", p=P)
    c_w = [pr.counter(), pr.counter()]
    t_raw, t_wsp, f_wst = {}, {}, [[], []]
    order = [NE] + list(range(NE))

    def load_w(ex):
        s = order.index(ex) % 2
        t_raw[ex] = dma("sp", wst[:, s, :, :], wd[ex], f_wst[s], t_last_q[1], on=c_w[s])

    def split_w(ex, hi, lo, free):
        s = order.index(ex) % 2
        t_wsp[ex] = []

        def rows(dc):
            t = t_raw[ex]
            t1 = A(lambda e: e.activation(hi[:, dc, 0:512], wst[:, s, dc, 0:512], ACT.Copy, scale=g2c[:, dc:dc + 1]),
                   t, t_g2, free)
            t_wsp[ex].append(V(lambda e: e.scalar_tensor_tensor(
                lo[:, dc, 0:512], wst[:, s, dc, 0:512], g2c[:, dc:dc + 1], hi[:, dc, 0:512].bitcast(F32),
                ALU.mult, ALU.subtract), t1, free))

        def last():
            t1 = A(lambda e: e.activation(hi[:, :, 512:768], wst[:, s, :, 512:768], ACT.Copy), t_raw[ex], free)
            t_wsp[ex].append(V(lambda e: e.tensor_tensor(lo[:, :, 512:768], wst[:, s, :, 512:768],
                                                         hi[:, :, 512:768].bitcast(F32), ALU.subtract), t1, free))
            f_wst[s] = list(t_wsp[ex])
            nxt = order.index(ex) + 2
            if nxt < len(order):
                load_w(order[nxt])
        return [lambda: rows(0), lambda: rows(1), last]

    def shared_jobs():
        return split_w(NE, wsh, wsl, t_b0)

    nx0, k0, v0, q0, m0 = nx_jobs(0), k_jobs(0), v_jobs(0), q_jobs(0, 0), max_jobs(0, 0)
    silu()
    stats(1, 0, lambda: t_x[0])
    root(1, 0)
    norm1(0)
    stats(1, 1, lambda: t_x[1])
    mod_cols()
    root(1, 1)
    norm1(1)
    turn(0)
    stats(1, 2, lambda: t_x[2])
    root(1, 2)
    norm1(2)
    turn(1)
    stats(1, 3, lambda: t_x[3])
    project(0)
    t_wg1.extend(f() for f in fold_g1)
    root(1, 3)
    mod_rows(0, 0)
    norm1(3)
    turn(2)
    stats(1, 4, lambda: t_x[4])
    project(1)
    root(1, 4)
    mod_rows(1, 0)
    norm1(4)
    turn(3)
    stats(1, 5, lambda: t_x[5])
    project(2)
    root(1, 5)
    mod_rows(0, 1)
    norm1(5)
    turn(4)
    stats(1, 6, lambda: t_x[6])
    project(3)
    root(1, 6)
    mod_rows(1, 1)
    add_bias(0)
    add_bias(1)
    add_bias(2)
    add_bias(3)
    add_bias(4)
    add_bias(5)
    scales(0)
    norm1(6)
    turn(5)
    stats(1, 7, lambda: t_x[7])
    project(4)
    logits(0, 0)
    add_bias(6)
    root(1, 7)
    turn_logits(0, 0)
    softmax(0, 0)
    spread_pi(0, 0)
    norm1(7)
    turn(6)
    project(5)
    turn_pi(0, 0)
    dots(0, 0)
    logits(0, 1)
    add_bias(7)
    turn_logits(0, 1)
    softmax(0, 1)
    spread_pi(0, 1)
    turn(7)
    project(6)
    turn_pi(0, 1)
    dots(0, 1)
    logits(0, 2)
    turn_logits(0, 2)
    softmax(0, 2)
    spread_pi(0, 2)
    project(7)
    turn_pi(0, 2)
    dots(0, 2)
    logits(0, 3)
    turn_logits(0, 3)
    softmax(0, 3)
    spread_pi(0, 3)
    scales(1)
    turn_pi(0, 3)
    dots(0, 3)
    logits(1, 0)
    fold(0)
    turn_logits(1, 0)
    logits(1, 1)
    oproj(0, 0)
    softmax(1, 0)
    spread_pi(1, 0)
    oproj(0, 1)
    turn_pi(1, 0)
    turn_logits(1, 1)
    dots(1, 0)
    logits(1, 2)
    oproj(0, 2)
    softmax(1, 1)
    spread_pi(1, 1)
    oproj(0, 3)
    turn_pi(1, 1)
    turn_logits(1, 2)
    dots(1, 1)
    stats(2, 0, lambda: [t_x1[0], t_x1[1]])
    logits(1, 3)
    oproj(0, 4)
    softmax(1, 2)
    spread_pi(1, 2)
    oproj(0, 5)
    root(2, 0)
    norm2(0)
    turn_pi(1, 2)
    turn_logits(1, 3)
    stats(2, 1, lambda: [t_x1[2], t_x1[3]])
    dots(1, 2)
    oproj(0, 6)
    softmax(1, 3)
    spread_pi(1, 3)
    shift2(0)
    oproj(0, 7)
    root(2, 1)
    norm2(1)
    turn_pi(1, 3)
    stats(2, 2, lambda: [t_x1[4], t_x1[5]])
    dots(1, 3)
    squares(0)
    spill(0)
    rsqrt2(0)
    shift2(1)
    nx0[0]()
    nx0[1]()
    root(2, 2)
    norm2(2)
    nx0[2]()
    fold(1)
    nx0[3]()
    stats(2, 3, lambda: [t_x1[6], t_x1[7]])
    squares(1)
    nx0[4]()
    nx0[5]()
    oproj(1, 0)
    nx0[6]()
    rsqrt2(1)
    nx0[7]()
    shift2(2)
    nx0[8]()
    root(2, 3)
    norm2(3)
    oproj(1, 1)
    nx0[9]()
    stats(2, 4, lambda: [t_x1[8], t_x1[9]])
    minus_one(0)
    nx0[10]()
    k0[0]()
    squares(2)
    nx0[11]()
    v0[0]()
    oproj(1, 2)
    nx0[12]()
    root(2, 4)
    nx0[13]()
    nx0[14]()
    norm2(4)
    rsqrt2(2)
    shift2(3)
    oproj(1, 3)
    nx0[15]()
    stats(2, 5, lambda: [t_x1[10], t_x1[11]])
    nx0[16]()
    nx0[17]()
    oproj(1, 4)
    nx0[18]()
    k0[1]()
    root(2, 5)
    squares(3)
    nx0[19]()
    shift2(4)
    v0[1]()
    nx0[20]()
    norm2(5)
    oproj(1, 5)
    nx0[21]()
    stats(2, 6, lambda: [t_x1[12], t_x1[13]])
    rsqrt2(3)
    nx0[22]()
    nx0[23]()
    oproj(1, 6)
    nx0[24]()
    squares(4)
    root(2, 6)
    nx0[25]()
    shift2(5)
    nx0[26]()
    k0[2]()
    norm2(6)
    oproj(1, 7)
    nx0[27]()
    stats(2, 7, lambda: [t_x1[14], t_x1[15]])
    rsqrt2(4)
    v0[2]()
    nx0[28]()
    nx0[29]()
    spill(1)
    nx0[30]()
    squares(5)
    root(2, 7)
    nx0[31]()
    shift2(6)
    norm2(7)
    q0[0]()
    rsqrt2(5)
    k0[3]()
    q0[1]()
    q0[2]()
    v0[3]()
    squares(6)
    m0[0]()
    shift2(7)
    q0[3]()
    m0[1]()
    m0[2]()
    q0[4]()
    q0[5]()
    rsqrt2(6)
    m0[3]()
    m0[4]()
    m0[5]()
    squares(7)
    m0[6]()
    q0[6]()
    m0[7]()
    m0[8]()
    q0[7]()
    q0[8]()
    m0[9]()
    rsqrt2(7)
    m0[10]()
    m0[11]()
    q0[9]()
    m0[12]()
    m0[13]()
    q0[10]()
    q0[11]()
    m0[14]()
    m0[15]()
    m0[16]()
    m0[17]()
    m0[18]()
    m0[19]()
    m0[20]()
    m0[21]()
    m0[22]()
    m0[23]()
    m0[24]()
    m0[25]()
    m0[26]()
    m0[27]()
    m0[28]()
    m0[29]()
    m0[30]()
    m0[31]()
    m0[32]()
    m0[33]()
    m0[34]()
    m0[35]()
    t_p1 = t_sp + [t_h2[g] for g in range(8)] + [(pr.sem[k], pr.n[k]) for k in pr.sem]
    c1.close()

    QA2 = sb("QA2", [P, S], F32R, c=c3)
    QB2 = sb("QB2", [P, S], F32R, c=c3)
    KA1 = sb("KA1", [P, S], F32R, c=c3)
    KB1 = sb("KB1", [P, S], F32R, c=c3)
    PT = sb("PT", [P, 2, 1024], c=c3)
    PH = sb("PH", [P, 3, 1024], F32R, c=c3)
    PL = sb("PL", [P, 3, 1024], F32R, c=c3)
    O = sb("O", [65, S], c=c3)
    woa = sb("woa", [65, 4, 257], c=c3)
    QA.append(QA2[:, :])
    QB.append(QB2[:, :])
    KA.append(KA1[:, :])
    KB.append(KB1[:, :])
    qaf.append(QA[2].bitcast(F32))
    phf = PH[:, :, :].bitcast(F32)
    q_free[2] = t_p1
    t_woa = dma("sp", woa[:, :, :], I["woA"], t_p1)
    minus_one(1)
    zero_fill()

    ring = Ring([6, 7])
    qk(0)
    M1 = max_jobs(0, 1)
    for bh in range(8):
        jobs = spread(M1, 0, 41)
        if bh < 7:
            M1 = max_jobs(bh + 1, 1)
            jobs += spread(max_jobs(bh + 1, 0), 42, 88) + spread(M1[:5], 90, 95.9)
            M1 = M1[5:]
        if bh > 0:
            proj = proj_jobs(bh - 1)
            m, e = (30, 60) if bh == 4 else (49, 92)
            jobs += spread(proj[:8], 4, m) + spread(proj[8:], m + 1, e)
        if bh in (1, 3, 5):
            jobs += spread(q_jobs((bh + 1) // 4, (bh + 1) // 2 % 2), 0, 40)
        if bh == 1:
            NXJ = nx_jobs(1)
            jobs += spread(NXJ[:NT], 44, 92)
        if bh == 2:
            jobs += spread(NXJ[NT:], 2, 50) + spread(k_jobs(1), 54, 92)
        if bh == 3:
            jobs += spread(v_jobs(1), 20, 80)
        if bh == 4:
            jobs += spread(norm_jobs(0), 62, 92)
            RLJ = rlog_jobs(0)
        if bh == 5:
            jobs += spread(RLJ[:18], 30, 92)
        if bh == 6:
            jobs += [(30, lambda: load_w(NE)), (30, lambda: load_w(0))]
            jobs += spread(RLJ[18:42], 4, 92)
        if bh == 7:
            jobs += spread(RLJ[42:], 4, 16) + spread(route_jobs(0, 2), 16 + 2, 60) + spread(scatter_jobs(0), 60, 92)
            jobs += spread(shared_jobs(), 4, 40)
        main(bh, jobs)
        if bh == 3:
            t_b0 = (pr.sem["pe"], pr.n["pe"])
    av(8 * NSTEP - 1, 0)
    av(8 * NSTEP - 1, 1)
    t_q01 = [q_free[0], q_free[1]]
    t_p3 = []

    def attention_done():
        t_p3[:] = [(pr.sem[k], pr.n[k]) for k in pr.sem]
    c3.close()

    c4 = ExitStack()
    wh = sb("wh", [P, NE, 2, 768], F32R, c=c4)
    wl = sb("wl", [P, NE, 2, 768], F32R, c=c4)
    xhf = xh[:, :, :, :].bitcast(F32)
    hhf = hh[:, :, :, :].bitcast(F32)
    xo = nxT[:, 1, 1024:2048].rearrange("p (s d) -> p s d", d=D)

    def split_jobs(ex):
        return split_w(ex, wh[:, ex, :, :], wl[:, ex, :, :], t_p3)

    tiles = ([(None, i) for i in range(NT)] + [(0, i) for i in range(NTI)] + [(1, i) for i in range(NTI)]
             + [(None, NT + i) for i in range(NT)])
    NTL = len(tiles)
    tring, hring, yring = Ring([0, 1]), Ring([3, 4]), Ring([5, 6])
    ring = Ring([2, 7])
    c_x = [pr.counter() for _ in range(NX)]
    c_y = [pr.counter() for _ in range(3)]
    f_xg, f_x, f_sg, f_hg, f_h, f_yo = [t_q01] * NX, [t_q01] * 3, [t_q01] * 2, [t_q01] * 2, [t_q01] * 3, [t_q01] * 3
    d_xg, d_x, d_hg, d_h = {}, {}, {}, {}
    t_yo = {0: [], 1: []}
    regs = {}

    def expert(s, e):
        return None if tiles[s][0] is None else regs[s]

    def fetch(s):
        g, i = tiles[s]
        q = s % NX
        if g is None:
            d_xg[s] = A(lambda e: e.activation(xg[:, q, :], X2[:, i, :], ACT.Copy, scale=rs2[:, i:i + 1]),
                        t_rs[i // NT], f_xg[q])
        else:
            d_xg[s] = dma("sp", xg[:, q, :], xbuf[g][i * P:i * P + P, :], t_sc[g], t_zf, f_xg[q], on=c_x[q])

    def split_x(s):
        q, r = s % NX, s % 3
        k = tring.take()

        def tr(e):
            for dc in range(2):
                mm = e.transpose(PS[:, k, dc * P:dc * P + P], xg[:, q, dc * P:dc * P + P], ident[:, :])
            return mm
        t = T(tr, d_xg[s], rel[k])
        f_xg[q] = t
        pv = PS[:, k, 0:256].rearrange("p (c n) -> p c n", c=2)
        ta = A(lambda e: e.activation(xh[:, r, :, :], pv, ACT.Copy), t, f_x[r])
        tv = V(lambda e: e.tensor_tensor(xl[:, r, :, :], pv, xhf[:, r, :, :], ALU.subtract), ta, f_x[r])
        rel[k] = [tv]
        d_x[s] = tv

    def choose_expert(s):
        g, i = tiles[s]
        if g is not None:
            def ld(e):
                regs[s] = e.value_load(texp[0:1, g, i:i + 1], min_val=0, max_val=NE - 1)
            pr.do("pe", ld, t_texp[g])

    def up(s):
        r, q = s % 3, s % 2
        k = hring.take()
        g, i = tiles[s]
        def f(e):
            ex = expert(s, e)
            n = 0
            for dc in range(2):
                for w, a in ((0, xh), (0, xl), (1, xh)):
                    mm = e.matmul(PS[:, k, :], a[:, r, dc, :], wsel(w, ex, dc, 0, 512), start=(n == 0), stop=(n == 5))
                    n += 1
            return mm
        t = T(f, d_x[s], t_wsp[NE] if g is None else [t_wsp[ex] for ex in range(NE)], rel[k])
        f_x[r] = t
        if s + 1 < NTL:
            choose_expert(s + 1)
        ta = A(lambda e: e.activation(sg[:, q, :], PS[:, k, 0:256], ACT.Silu), t, f_sg[q])
        tv = V(lambda e: e.tensor_tensor(hg[:, q, :], PS[:, k, 256:512], sg[:, q, :], ALU.mult), ta, f_hg[q])
        f_sg[q] = tv
        rel[k] = [tv]
        d_hg[s] = tv

    def wsel(w, ex, dc, a, b):
        if ex is None:
            return (wsh, wsl)[w][:, dc, a:b]
        return (wh, wl)[w][:, bass.ds(ex, 1), dc, a:b].rearrange("p o n -> p (o n)")

    def split_h(s):
        q, r = s % 2, s % 3
        k = tring.take()

        def tr(e):
            for dc in range(2):
                mm = e.transpose(PS[:, k, dc * P:dc * P + P], hg[:, q, dc * P:dc * P + P], ident[:, :])
            return mm
        t = T(tr, d_hg[s], rel[k])
        f_hg[q] = t
        pv = PS[:, k, 0:256].rearrange("p (c n) -> p c n", c=2)
        ta = A(lambda e: e.activation(hh[:, r, :, :], pv, ACT.Copy), t, f_h[r])
        tv = V(lambda e: e.tensor_tensor(hl[:, r, :, :], pv, hhf[:, r, :, :], ALU.subtract), ta, f_h[r])
        rel[k] = [tv]
        d_h[s] = tv

    def down(s):
        g, i = tiles[s]
        r = s % 3
        k = yring.take()

        def f(e):
            ex = expert(s, e)
            n = 0
            for fc in range(2):
                for a, w in ((hh, 0), (hh, 1), (hl, 0)):
                    mm = e.matmul(PS[:, k, 0:256], a[:, r, fc, :], wsel(w, ex, fc, 512, 768), start=(n == 0), stop=(n == 5))
                    n += 1
            return mm
        t = T(f, d_h[s], rel[k])
        f_h[r] = t
        if g is None:
            t = V(lambda e: e.tensor_tensor(X2[:, i, :], PS[:, k, 0:256], X2[:, i, :], ALU.add), t, t_nxs[i], d_xg[s])
            t_X2[i] = t
        else:
            t = A(lambda e: e.activation(yo[:, r, :], PS[:, k, 0:256], ACT.Copy), t, f_yo[r])
            f_yo[r] = dma("act", ybuf[g][i * P:i * P + P, :], yo[:, r, :], t, on=c_y[r])
            t_yo[g] = [f_yo[x] for x in range(3)]
        rel[k] = [t]

    c_g = [pr.counter() for _ in range(NG)]
    c_xo = [pr.counter() for _ in range(NG)]
    f_g, f_xo = [t_q01] * NG, [t_q01] * NG
    d_xo = {}
    t_fin = []
    c_out = pr.counter()
    d_g = {}

    def gather(n):
        b, i, s = n // NT, n % NT, n % NG
        d_xo[n] = dma("sp", xo[:, s, :], tokens(x1d, b)[:, i, :], f_xo[s], t_sp, on=c_xo[s])
        for j in range(2):
            d_g[n] = pr.start("pool", lambda e, j=j: e.indirect_dma_start(
                out=y12[:, s, j, :], out_offset=None, in_=ybuf[b],
                in_offset=bass.IndirectOffsetOnAxis(ap=slot[:, b, j, i:i + 1], axis=0)),
                [t_yo[b], f_g[s], t_slot[b]], c_g[s])

    def finish(n):
        b, i, s = n // NT, n % NT, n % NG
        t = V(lambda e: e.scalar_tensor_tensor(X2[:, n, :], y12[:, s, 0, :], gate[:, b, 0, i:i + 1], X2[:, n, :],
                                               ALU.mult, ALU.add), d_g[n], t_gate[b], t_X2[n])
        t = V(lambda e: e.scalar_tensor_tensor(X2[:, n, :], y12[:, s, 1, :], gate[:, b, 1, i:i + 1], X2[:, n, :],
                                               ALU.mult, ALU.add), t)
        f_g[s] = t
        t = V(lambda e: e.tensor_tensor(X2[:, n, :], X2[:, n, :], gb[:, b, :], ALU.mult), t)
        add = G if b and i < 12 else V
        t = add(lambda e: e.tensor_tensor(X2[:, n, :], X2[:, n, :], xo[:, s, :], ALU.add), t, d_xo[n])
        f_xo[s] = t
        t_fin.append(dma("sp", tokens(out, b)[:, i, :], X2[:, n, :], t, on=c_out))

    def combine_jobs(b):
        def job(i):
            if i < NT:
                gather(b * NT + i)
            if i >= NG - 1:
                finish(b * NT + i - NG + 1)
        return [lambda i=i: job(i) for i in range(NT + NG - 1)]

    def last_jobs():
        norm = norm_jobs(1)
        return [f for j, proj in enumerate(proj_jobs(7)) for f in (proj, norm[j])] + [norm[NT], attention_done]

    side = [(-2, 9, last_jobs),
            (2, 2, lambda: [lambda j=j, ex=ex: split_jobs(ex)[j]() for ex in range(NE) for j in range(3)]),
            (2, 2.5, lambda: rlog_jobs(1)),
            (22, 1, lambda: route_jobs(1, 5) + scatter_jobs(1)),
            (NT + NTI + 3, 0.5, lambda: combine_jobs(0)),
            (NT + 2 * NTI + 1, 1, lambda: combine_jobs(1))]
    todo = []
    for s in range(-2, NTL + 2):
        for at, n, make in side:
            if s == at:
                todo.append((n, make()))
        if s == -2:
            for q in range(2):
                fetch(q)
        if 0 <= s + 4 < NTL and s + 4 >= 2:
            fetch(s + 4)
        if 0 <= s + 2 < NTL:
            split_x(s + 2)
        if 0 <= s + 1 < NTL:
            up(s + 1)
        if 0 <= s < NTL:
            split_h(s)
        for n, jobs in todo:
            for _ in range(min(int(n * (s + 1)) - int(n * s), len(jobs))):
                jobs.pop(0)()
        if 0 <= s - 1 < NTL:
            down(s - 1)
    for n, jobs in todo:
        while jobs:
            jobs.pop(0)()
    pr.wait("sp", t_fin[-1])
    c4.close()

    block = ctx.enter_context(nc.Block())

    @block.sync
    def _(eng):
        pr.play("sp", eng)

    @block.scalar
    def _(eng):
        pr.play("act", eng)

    @block.vector
    def _(eng):
        pr.play("dve", eng)

    @block.gpsimd
    def _(eng):
        pr.play("pool", eng)

    @block.tensor
    def _(eng):
        pr.play("pe", eng)


def kernel(**inputs):
    import numpy as np
    import concourse.bacc as bacc
    from concourse.bass_utils import run_bass_kernel_spmd

    a = {k: np.asarray(v) for k, v in inputs.items()}

    def tr(w):
        return np.ascontiguousarray(np.swapaxes(w, -1, -2))

    mask = np.zeros((D, 16), np.float32)
    mask[np.arange(D), np.arange(D) // 16] = 1.0
    woa = np.zeros((65, 4, 257), np.float32)
    woa[0:64, :, 0:256] = tr(a["L0_ffn_Wo"]).reshape(4, 64, D).transpose(1, 0, 2)
    woa[64, :, 256] = 1.0
    wexp = np.zeros((NE + 1, D, 768), np.float32)
    for i, (e, s) in enumerate((("eW1", "sW1"), ("eW3", "sW3"), ("eW2", "sW2"))):
        wexp[:NE, :, i * D:i * D + D] = tr(a["L0_ffn_" + e])
        wexp[NE, :, i * D:i * D + D] = tr(a["L0_ffn_" + s])
    wk = tr(a["L0_ffn_Wkc"])
    arrays = {
        "x": a["L0_attn_x"], "cT": tr(a["L0_c"]), "wmod": a["L0_wmod"],
        "wqkvT": tr(a["L0_attn_Wqkv"]), "woutT": tr(a["L0_attn_Wout"]), "bout": a["L0_attn_bout"],
        "temp": a["L0_attn_temp"], "g1": tr(a["L0_ffn_g1"].reshape(2, P)), "g2": tr(a["L0_ffn_g2"].reshape(2, P)),
        "wqT": tr(a["L0_ffn_Wq"]), "wkcT2": np.concatenate([wk, wk], axis=1), "wvcT": tr(a["L0_ffn_Wvc"]),
        "woA": woa, "wrT": tr(a["L0_ffn_Wr"]), "ebias": a["L0_ffn_expert_bias"], "wexp": wexp,
        "ident": np.eye(P, dtype=np.float32),
        "tri": np.stack([np.triu(np.ones((P, P), np.float32), 1), np.ones((P, P), np.float32)], axis=1),
        "thr": (np.arange(NTI) * P).astype(np.float32).reshape(1, NTI), "mask": mask,
        "pri": np.arange(NE, 0, -1).astype(np.float32),
    }
    nc = bacc.Bacc("TRN2", target_bir_lowering=False, num_devices=1)
    I, feeds = {}, {}
    for n, v in arrays.items():
        v = np.ascontiguousarray(v)
        feeds["in_" + n] = v
        I[n] = nc.dram_tensor("in_" + n, v.shape, mybir.dt.from_np(v.dtype), kind="ExternalInput").ap()
    out = nc.dram_tensor("out_0", (NB, S, D), F32, kind="ExternalOutput").ap()
    build(nc, I, out)
    r = run_bass_kernel_spmd(nc, [feeds], core_ids=[0])
    return r.results[0]["out_0"]
```
